# Optimizing a Trainium2 kernel written in Bass

```python
import numpy as np
import jax
import jax.numpy as jnp

def _softmax(x, axis=-1):
    return jax.nn.softmax(x, axis=axis)

def _gelu(x):
    return jax.nn.gelu(x, approximate=True)

def _silu(x):
    return jax.nn.silu(x)

def _sigmoid(x):
    return jax.nn.sigmoid(x)

def _layernorm(x, axis=-1, eps=1e-05):
    m = jnp.mean(x, axis=axis, keepdims=True)
    v = jnp.var(x, axis=axis, keepdims=True)
    return (x - m) / jnp.sqrt(v + eps)

def _scatter_add(tgt, idx, src, axis=0):
    return tgt.at[idx].add(src)

def _segment_sum(src, seg, n):
    return jax.ops.segment_sum(src, seg, n)
kernel_name = 'mk_macaron_d2_jaxref_r8_a1f1e8'

def setup_inputs(seed: int=0):
    np.random.seed(seed)
    _w = jnp.asarray

    def _L0_attn_setup():
        import jax, jax.numpy as jnp
        import numpy as np
        import math
        NUM_HEADS = 16
        D_MODEL = 128
        B, T = (1, 512)
        key = jax.random.key(seed)
        kx, kq, kk, kv, ko = jax.random.split(key, 5)
        s = 1.0 / math.sqrt(D_MODEL)
        return {'x': jax.random.normal(kx, (B, T, D_MODEL), dtype=jnp.float32), 'Wq': jax.random.normal(kq, (D_MODEL, D_MODEL), dtype=jnp.float32) * s, 'Wk': jax.random.normal(kk, (D_MODEL, D_MODEL), dtype=jnp.float32) * s, 'Wv': jax.random.normal(kv, (D_MODEL, D_MODEL), dtype=jnp.float32) * s, 'Wo': jax.random.normal(ko, (D_MODEL, D_MODEL), dtype=jnp.float32) * s}
    _L0_attn_in = _L0_attn_setup()

    def _L0_ffn_setup():
        import jax, jax.numpy as jnp
        import numpy as np
        NUM_EXPERTS = 4
        key = jax.random.key(seed)
        ks = jax.random.split(key, 8)
        B, L, H = (8, 256, 128)
        F = 4 * H
        s = 0.02
        x = jax.random.normal(ks[0], (B, L, H), dtype=jnp.float32)
        Wr = jax.random.normal(ks[1], (H, NUM_EXPERTS), dtype=jnp.float32) * s
        br = jnp.zeros((NUM_EXPERTS,), dtype=jnp.float32)
        We1 = jax.random.normal(ks[2], (NUM_EXPERTS, H, F), dtype=jnp.float32) * s
        be1 = jnp.zeros((NUM_EXPERTS, F), dtype=jnp.float32)
        We2 = jax.random.normal(ks[3], (NUM_EXPERTS, F, H), dtype=jnp.float32) * s
        be2 = jnp.zeros((NUM_EXPERTS, H), dtype=jnp.float32)
        return {'x': x, 'Wr': Wr, 'br': br, 'We1': We1, 'be1': be1, 'We2': We2, 'be2': be2}
    _L0_ffn_in = _L0_ffn_setup()

    def _L1_attn_setup():
        import jax, jax.numpy as jnp
        import numpy as np
        H = 16
        LN_EPS = 1e-05
        key = jax.random.key(seed)
        ks = jax.random.split(key, 10)
        B, N, D = (2, 256, 128)
        s = 1.0 / np.sqrt(D).astype(np.float32)
        x = jax.random.normal(ks[0], (B, N, D), jnp.float32)
        Wq = jax.random.normal(ks[1], (D, D), jnp.float32) * s
        Wk = jax.random.normal(ks[2], (D, D), jnp.float32) * s
        Wv = jax.random.normal(ks[3], (D, D), jnp.float32) * s
        Wo = jax.random.normal(ks[4], (D, D), jnp.float32) * s
        bq = jnp.zeros((D,), jnp.float32)
        bk = jnp.zeros((D,), jnp.float32)
        bv = jnp.zeros((D,), jnp.float32)
        bo = jnp.zeros((D,), jnp.float32)
        beta = jnp.ones((H,), jnp.float32)
        t = jnp.ones((H,), jnp.float32)
        ln_w = jnp.ones((D,), jnp.float32)
        ln_b = jnp.zeros((D,), jnp.float32)
        return {'x': x, 'Wq': Wq, 'bq': bq, 'Wk': Wk, 'bk': bk, 'Wv': Wv, 'bv': bv, 'Wo': Wo, 'bo': bo, 'beta': beta, 't': t, 'ln_w': ln_w, 'ln_b': ln_b}
    _L1_attn_in = _L1_attn_setup()

    def _L1_ffn_setup():
        import jax, jax.numpy as jnp
        import numpy as np
        B, S, D, M, E, K = (2, 256, 128, 176, 8, 2)
        key = jax.random.key(seed)
        k0, k1, k2, k3, k4 = jax.random.split(key, 5)
        scale = 0.02
        return {'x': jax.random.normal(k0, (B, S, D), dtype=jnp.float32), 'w_gate': jax.random.normal(k1, (D, E), dtype=jnp.float32) * scale, 'w_g': jax.random.normal(k2, (E, D, M), dtype=jnp.float32) * scale, 'w_u': jax.random.normal(k3, (E, D, M), dtype=jnp.float32) * scale, 'w_d': jax.random.normal(k4, (E, M, D), dtype=jnp.float32) * scale}
    _L1_ffn_in = _L1_ffn_setup()
    _d = {'L0_attn_x': _L0_attn_in['x'], 'L0_attn_Wq': _L0_attn_in['Wq'], 'L0_attn_Wk': _L0_attn_in['Wk'], 'L0_attn_Wv': _L0_attn_in['Wv'], 'L0_attn_Wo': _L0_attn_in['Wo'], 'L0_ffn_Wr': _L0_ffn_in['Wr'], 'L0_ffn_br': _L0_ffn_in['br'], 'L0_ffn_We1': _L0_ffn_in['We1'], 'L0_ffn_be1': _L0_ffn_in['be1'], 'L0_ffn_We2': _L0_ffn_in['We2'], 'L0_ffn_be2': _L0_ffn_in['be2'], 'L1_attn_Wq': _L1_attn_in['Wq'], 'L1_attn_bq': _L1_attn_in['bq'], 'L1_attn_Wk': _L1_attn_in['Wk'], 'L1_attn_bk': _L1_attn_in['bk'], 'L1_attn_Wv': _L1_attn_in['Wv'], 'L1_attn_bv': _L1_attn_in['bv'], 'L1_attn_Wo': _L1_attn_in['Wo'], 'L1_attn_bo': _L1_attn_in['bo'], 'L1_attn_beta': _L1_attn_in['beta'], 'L1_attn_t': _L1_attn_in['t'], 'L1_attn_ln_w': _L1_attn_in['ln_w'], 'L1_attn_ln_b': _L1_attn_in['ln_b'], 'L1_ffn_w_gate': _L1_ffn_in['w_gate'], 'L1_ffn_w_g': _L1_ffn_in['w_g'], 'L1_ffn_w_u': _L1_ffn_in['w_u'], 'L1_ffn_w_d': _L1_ffn_in['w_d']}
    _x0 = _d['L0_attn_x']
    _d['L0_attn_x'] = jax.random.normal(jax.random.fold_in(jax.random.key(seed), 1), (4, 1024, 128), dtype=_x0.dtype)
    del _x0
    return _d

def reference(L0_attn_x, L0_attn_Wq, L0_attn_Wk, L0_attn_Wv, L0_attn_Wo, L0_ffn_Wr, L0_ffn_br, L0_ffn_We1, L0_ffn_be1, L0_ffn_We2, L0_ffn_be2, L1_attn_Wq, L1_attn_bq, L1_attn_Wk, L1_attn_bk, L1_attn_Wv, L1_attn_bv, L1_attn_Wo, L1_attn_bo, L1_attn_beta, L1_attn_t, L1_attn_ln_w, L1_attn_ln_b, L1_ffn_w_gate, L1_ffn_w_g, L1_ffn_w_u, L1_ffn_w_d):

    def _L0_attn_ref(x, Wq, Wk, Wv, Wo):
        import jax, jax.numpy as jnp
        import numpy as np
        import math
        NUM_HEADS = 16
        D_MODEL = 128
        B, T = (1, 512)
        Bx, Tx, D = x.shape
        H = NUM_HEADS
        dk = D // H
        q = (x @ Wq.T).reshape(Bx, Tx, H, dk)
        k = (x @ Wk.T).reshape(Bx, Tx, H, dk)
        v = (x @ Wv.T).reshape(Bx, Tx, H, dk)
        scores = jnp.einsum('bthd,bshd->bhts', q, k) / math.sqrt(dk)
        causal_mask = jnp.triu(jnp.ones((Tx, Tx), dtype=bool), k=1)
        scores = jnp.where(causal_mask, jnp.float32(-jnp.inf), scores).astype(jnp.float32)
        attn = jax.nn.softmax(scores, axis=-1)
        out = jnp.einsum('bhts,bshd->bthd', attn, v).reshape(Bx, Tx, D)
        return out @ Wo.T

    def _L0_ffn_ref(x, Wr, br, We1, be1, We2, be2):
        import jax, jax.numpy as jnp
        import numpy as np
        NUM_EXPERTS = 4
        logits = jnp.einsum('blh,he->ble', x, Wr) + br
        top_expert = jnp.argmax(logits, axis=-1)
        mask = jax.nn.one_hot(top_expert, NUM_EXPERTS, dtype=x.dtype)
        out = jnp.zeros_like(x)
        for e in range(NUM_EXPERTS):
            h1 = jax.nn.relu(jnp.einsum('blh,hf->blf', x, We1[e]) + be1[e])
            oe = jnp.einsum('blf,fh->blh', h1, We2[e]) + be2[e]
            out = out + mask[..., e:e + 1] * oe
        return out

    def _L1_attn_ref(x, Wq, bq, Wk, bk, Wv, bv, Wo, bo, beta, t, ln_w, ln_b):
        import jax, jax.numpy as jnp
        import numpy as np
        H = 16
        LN_EPS = 1e-05
        B, N, D = x.shape
        dh = D // H

        def proj(W, b):
            return (x @ W.T + b).reshape(B, N, H, dh).transpose(0, 2, 1, 3)
        Q, K, V = (proj(Wq, bq), proj(Wk, bk), proj(Wv, bv))
        S = jnp.einsum('bhnd,bhmd->bhnm', Q, K) / dh ** 0.5
        W_tau = jax.nn.softmax(S, axis=-1)
        b_ = beta.reshape(1, H, 1, 1)
        t_ = t.reshape(1, H, 1, 1)
        W_sigma = 1.0 / ((1.0 + jnp.abs(S) / b_) ** 2 + t_ ** 2)
        W_sigma = W_sigma / W_sigma.sum(axis=-1, keepdims=True)
        tau = jnp.einsum('bhnm,bhmd->bhnd', W_tau, V).transpose(0, 2, 1, 3).reshape(B, N, D)
        sigma = jnp.einsum('bhnm,bhmd->bhnd', W_sigma, V).transpose(0, 2, 1, 3).reshape(B, N, D)
        f = 0.5 * tau + 0.5 * sigma
        y = f @ Wo.T + bo
        mu = y.mean(axis=-1, keepdims=True)
        var = jnp.mean((y - mu) ** 2, axis=-1, keepdims=True)
        out = x + ln_w * (y - mu) * jax.lax.rsqrt(var + LN_EPS) + ln_b
        return out

    def _L1_ffn_ref(x, w_gate, w_g, w_u, w_d):
        import jax, jax.numpy as jnp
        import numpy as np
        B, S, D, M, E, K = (2, 256, 128, 176, 8, 2)
        scores = x @ w_gate
        topk_scores, topk_idx = jax.lax.top_k(scores, K)
        topk_probs = jax.nn.softmax(topk_scores, axis=-1)
        gating = jnp.sum(jax.nn.one_hot(topk_idx, E, dtype=topk_probs.dtype) * topk_probs[..., None], axis=-2)
        hidden = jax.nn.silu(jnp.einsum('bsd,edm->ebsm', x, w_g)) * jnp.einsum('bsd,edm->ebsm', x, w_u)
        expert_out = jnp.einsum('ebsm,emd->ebsd', hidden, w_d)
        y = jnp.einsum('bse,ebsd->bsd', gating, expert_out)
        return y
    x = L0_attn_x
    x = x + 0.5 * _L0_ffn_ref(_layernorm(x, axis=-1), L0_ffn_Wr, L0_ffn_br, L0_ffn_We1, L0_ffn_be1, L0_ffn_We2, L0_ffn_be2)
    x = x + _L0_attn_ref(_layernorm(x, axis=-1), L0_attn_Wq, L0_attn_Wk, L0_attn_Wv, L0_attn_Wo)
    x = x + 0.5 * _L0_ffn_ref(_layernorm(x, axis=-1), L0_ffn_Wr, L0_ffn_br, L0_ffn_We1, L0_ffn_be1, L0_ffn_We2, L0_ffn_be2)
    x = x + 0.5 * _L1_ffn_ref(_layernorm(x, axis=-1), L1_ffn_w_gate, L1_ffn_w_g, L1_ffn_w_u, L1_ffn_w_d)
    x = x + _L1_attn_ref(_layernorm(x, axis=-1), L1_attn_Wq, L1_attn_bq, L1_attn_Wk, L1_attn_bk, L1_attn_Wv, L1_attn_bv, L1_attn_Wo, L1_attn_bo, L1_attn_beta, L1_attn_t, L1_attn_ln_w, L1_attn_ln_b)
    x = x + 0.5 * _L1_ffn_ref(_layernorm(x, axis=-1), L1_ffn_w_gate, L1_ffn_w_g, L1_ffn_w_u, L1_ffn_w_d)
    return x

_drawn_inputs = setup_inputs


def setup_inputs(seed=0):
    import zlib

    import numpy as np

    out = dict(_drawn_inputs(seed))
    spreads = {'L0_ffn_br': (0.0, 0.1),
     'L0_ffn_be1': (0.0, 0.1),
     'L0_ffn_be2': (0.0, 0.1),
     'L1_attn_bq': (0.0, 0.606),
     'L1_attn_bk': (0.0, 0.8),
     'L1_attn_bv': (0.0, 0.1),
     'L1_attn_bo': (0.0, 0.1),
     'L1_attn_beta': (1.0, 0.6),
     'L1_attn_t': (1.0, 0.6),
     'L1_attn_ln_w': (1.0, 0.2),
     'L1_attn_ln_b': (0.0, 0.1)}
    factors = {'L1_ffn_w_gate': 8.0, 'L1_ffn_w_g': 8.0, 'L1_ffn_w_u': 8.0, 'L1_ffn_w_d': 8.0}
    for name, (base, spread) in spreads.items():
        noise = np.random.default_rng([zlib.crc32(name.encode()), seed]).standard_normal(out[name].shape)
        drawn = base * np.exp(spread * noise) if base else spread * noise
        out[name] = jnp.asarray(drawn.astype(out[name].dtype))
    for name, factor in factors.items():
        out[name] = (out[name] * factor).astype(out[name].dtype)
    return out
```

```python
from contextlib import ExitStack

import numpy as np

import concourse.bass as bass
from concourse import mybir

F32 = mybir.dt.float32
BF16 = mybir.dt.bfloat16
I32 = mybir.dt.int32
ALU = mybir.AluOpType
ACT = mybir.ActivationFunctionType
AX = mybir.AxisListType

P = 128
B, T, D = 4, 1024, 128
H, DH = 16, 8
TOK = B * T
NT = TOK // P
TT = T // P
HEADS = B * H
CH = 512
NCH = TOK // CH
LN_EPS = 1e-5
E0, F0 = 4, 512
FT0 = F0 // P
E1, M1 = 8, 176
KT1 = E1 * M1 // P
SPLIT = 3
PROD = SPLIT * SPLIT * DH
ONES_ROW = 96
RING = 4
SIGN_OFF = 0x7FFFFFFF


class Chain:

    def __init__(self, eng, sem, base=0):
        self.eng, self.sem, self.n = eng, sem, base

    def __call__(self, ins):
        ins.then_inc(self.sem, 1)
        self.n = self.n + 1
        self.eng.wait_ge(self.sem, self.n)


class Mem:
    def __init__(self, nc, ctx, tag):
        self.nc, self.ctx, self.tag, self.sems = nc, ctx, tag, []

    def sb(self, name, shape, dt=F32):
        return self.ctx.enter_context(self.nc.sbuf_tensor(f"{self.tag}_{name}", shape, dt))

    def ps(self, name, shape, dt=F32):
        return self.ctx.enter_context(self.nc.psum_tensor(f"{self.tag}_{name}", shape, dt))

    def sem(self, name):
        self.sems.append(self.ctx.enter_context(self.nc.semaphore(f"{self.tag}_{name}")))
        return self.sems[-1]

    def clear_sems(self):
        nums = sorted(s.num for s in self.sems)
        starts = [n for n in nums if n - 1 not in nums]
        ends = [n + 1 for n in nums if n + 1 not in nums]
        with self.nc.Block() as block:

            @block.gpsimd
            def _(pool):
                for a, b in zip(starts, ends):
                    self.nc.gpsimd.sem_clear(range(a, b))


def ln_transposed(nc, tag, X, XNT, ident, add_to_x=False):
    G = 4
    GT = NT // G
    with ExitStack() as ctx:
        m = Mem(nc, ctx, tag)
        stats = m.sb("stats", [P, NT, 6])
        mv = m.sb("mv", [P, NT, 2])
        rs = m.sb("rs", [P, NT])
        t1 = m.sb("t1", [P, NT])
        rstd = m.sb("rstd", [P, NT])
        ve = m.sb("ve", [P, NT])
        xn = m.sb("xn", [P, NT, P])
        pt = m.ps("pt", [P, 4, CH])
        stats_done, mv_done, ve_ready, ln_var, rs_ready = (m.sem(x) for x in ("stats", "mvs", "ve", "lnv", "rsr"))
        dve_chain, xn_ready, turned, evacuated = (m.sem(x) for x in ("chain", "xnr", "turned", "evac"))
        x_added = m.sem("xadd")
        with nc.Block() as block:

            @block.vector
            def _(dve):

                def statistics(g):
                    for k in range(g * GT, (g + 1) * GT):
                        nc.vector.bn_stats(stats[:, k, :], X[:, k, :]).then_inc(stats_done, 1)
                    for k in range(g * GT, (g + 1) * GT):
                        dve.wait_ge(stats_done, k + 1)
                        nc.vector.bn_aggr(mv[:, k, :], stats[:, k, :]).then_inc(mv_done, 1)
                    tiles = slice(g * GT, (g + 1) * GT)
                    dve.wait_ge(mv_done, (g + 1) * GT)
                    nc.vector.tensor_scalar(ve[:, tiles], mv[:, tiles, 1], LN_EPS, None, ALU.add).then_inc(ve_ready, 1)

                def normalise(g):
                    tiles = slice(g * GT, (g + 1) * GT)
                    dve.wait_ge(ve_ready, g + 1)
                    dve.wait_ge(rs_ready, g + 1)
                    link = Chain(dve, dve_chain, 4 * g)
                    link(nc.vector.tensor_tensor(t1[:, tiles], rs[:, tiles], rs[:, tiles], ALU.mult))
                    link(nc.vector.tensor_tensor(t1[:, tiles], t1[:, tiles], ve[:, tiles], ALU.mult))
                    link(nc.vector.tensor_scalar(t1[:, tiles], t1[:, tiles], -0.5, 1.5, ALU.mult, ALU.add))
                    link(nc.vector.tensor_tensor(rstd[:, tiles], rs[:, tiles], t1[:, tiles], ALU.mult))
                    for k in range(g * GT, (g + 1) * GT):
                        nc.vector.tensor_scalar(xn[:, k, :], X[:, k, :], mv[:, k, 0:1], rstd[:, k:k + 1],
                                                ALU.subtract, ALU.mult).then_inc(xn_ready, 1)

                statistics(0)
                for g in range(1, G):
                    statistics(g)
                    normalise(g - 1)
                normalise(G - 1)

            if add_to_x:

                @block.gpsimd
                def _(pool):
                    for k in range(NT):
                        pool.wait_ge(xn_ready, k + 1)
                        nc.gpsimd.tensor_tensor(X[:, k, :], X[:, k, :], xn[:, k, :], ALU.add).then_inc(x_added, 1)

            @block.scalar
            def _(act):
                nc.scalar.preload_act_table_set("natural_log_exp_and_others")

                def evacuate(c):
                    act.wait_ge(turned, c + 1)
                    nc.scalar.activation(XNT[:, c * CH:(c + 1) * CH], pt[:, c % 4, :], ACT.Copy).then_inc(evacuated, 1)

                for g in range(G):
                    tiles = slice(g * GT, (g + 1) * GT)
                    act.wait_ge(ve_ready, g + 1)
                    nc.scalar.activation(rs[:, tiles], ve[:, tiles], ACT.Ln).then_inc(ln_var, 1)
                    act.wait_ge(ln_var, g + 1)
                    nc.scalar.activation(rs[:, tiles], rs[:, tiles], ACT.Exp, scale=-0.5).then_inc(rs_ready, 1)
                    if g >= 2:
                        for c in range((g - 2) * NCH // G, (g - 1) * NCH // G):
                            evacuate(c)
                for c in range((G - 2) * NCH // G, NCH):
                    evacuate(c)

            @block.tensor
            def _(pe):
                for c in range(NCH):
                    if c >= 4:
                        pe.wait_ge(evacuated, c - 3)
                    for q in range(4):
                        k = 4 * c + q
                        pe.wait_ge(xn_ready, k + 1)
                        last = nc.tensor.transpose(pt[:, c % 4, q * P:(q + 1) * P], xn[:, k, :], ident[:])
                    last.then_inc(turned, 1)
        m.clear_sems()


def first_argmax(link, nc, onehot, score, top, pref, eq, rank, n):
    link(nc.vector.tensor_reduce(top[:], score[:], AX.X, ALU.max))
    link(nc.vector.tensor_tensor(eq[:], score[:], top[:].unsqueeze(2).broadcast_to([P, NT, n]), ALU.is_equal))
    link(nc.vector.tensor_tensor(pref[:], eq[:], rank[:].unsqueeze(1).broadcast_to([P, NT, n]), ALU.mult))
    link(nc.vector.tensor_reduce(eq[:, :, 0], pref[:], AX.X, ALU.max))
    link(nc.vector.tensor_tensor(onehot[:], pref[:], eq[:, :, 0:1].broadcast_to([P, NT, n]), ALU.is_equal))


def load_ffn0(nc, m, w, sem):
    w1 = m.sb("w1", [P, E0, F0])
    w2 = m.sb("w2", [P, E0 * FT0, D])
    b1 = m.sb("b1", [P, E0 * FT0])
    b2 = m.sb("b2", [P, E0, D])
    wr = m.sb("wr", [P, E0])
    br = m.sb("br", [P, E0])

    def load(eng):
        eng.dma_start(wr[:], w["Wr"]).then_inc(sem, 16)
        eng.dma_start(br[:], w["br"].unsqueeze(0).broadcast_to([P, E0])).then_inc(sem, 16)
        eng.dma_start(w1[:], w["We1"].rearrange("e h f -> h e f")).then_inc(sem, 16)
        eng.dma_start(b1[:], w["be1T"]).then_inc(sem, 16)
        eng.dma_start(b2[:], w["be2"].unsqueeze(0).broadcast_to([P, E0, D])).then_inc(sem, 16)
        eng.dma_start(w2[:], w["We2"].rearrange("e (j p) d -> p (e j) d", p=P)).then_inc(sem, 16)

    return (w1, w2, b1, b2, wr, br), load


FFN0_LOADS = 16 * 6


def ffn0(nc, tag, X, XNT, rank, w, weights_in):
    with ExitStack() as ctx:
        m = Mem(nc, ctx, tag)
        score = m.sb("score", [P, NT, E0])
        top = m.sb("top", [P, NT])
        eq = m.sb("eq", [P, NT, E0])
        pref = m.sb("pref", [P, NT, E0])
        mask = m.sb("mask", [P, NT, E0])
        hid = m.sb("hid", [P, 2, FT0, CH])
        psr = m.ps("psr", [P, NT, E0])
        psh = m.ps("psh", [P, 4, CH])
        psy = m.ps("psy", [P, 2, 4, D])
        routed, chain, biased = (m.sem(x) for x in ("routed", "chain", "biased"))
        w1, w2, b1, b2, wr, br = w
        h_done, relu_done, y_done, added = (m.sem(x) for x in ("h", "relu", "y", "added"))
        with nc.Block() as block:

            @block.tensor
            def _(pe):
                pe.wait_ge(weights_in, FFN0_LOADS)
                for k in range(NT):
                    last = nc.tensor.matmul(psr[:, k, :], XNT[:, k * P:(k + 1) * P], wr[:], start=True, stop=True)
                last.then_inc(routed, 1)

                def hidden(c, e):
                    for j in range(FT0):
                        if e or not isinstance(c, int):
                            pe.wait_ge(relu_done, FT0 * (E0 * c + e - 1) + j + 1)
                        nc.tensor.matmul(psh[:, j, :], w1[:, e, j * P:(j + 1) * P], XNT[:, bass.ds(c * CH, CH)],
                                         start=True, stop=True).then_inc(h_done, 1)

                def output(c, e):
                    s = E0 * c + e
                    pe.wait_ge(relu_done, FT0 * s + FT0)
                    if e >= 2:
                        pe.wait_ge(added, 4 * (s - 1))
                    elif not isinstance(c, int):
                        pe.wait_ge(added, 4 * (s - 1))
                    for q in range(4):
                        for j in range(FT0):
                            last = nc.tensor.matmul(psy[:, e % 2, q, :], hid[:, e % 2, j, q * P:(q + 1) * P],
                                                    w2[:, e * FT0 + j, :], start=(j == 0), stop=(j == FT0 - 1))
                    last.then_inc(y_done, 1)

                def chunk(c):
                    hidden(c, 0)
                    for e in range(1, E0):
                        hidden(c, e)
                        output(c, e - 1)
                    output(c, E0 - 1)

                chunk(0)
                with pe.Fori(1, NCH) as c:
                    chunk(c)

            @block.scalar
            def _(act):
                act.wait_ge(weights_in, FFN0_LOADS)

                def relu(c, e, j):
                    s = E0 * c + e
                    act.wait_ge(h_done, FT0 * s + j + 1)
                    if e >= 2 or not isinstance(c, int):
                        act.wait_ge(y_done, s - 1)
                    nc.scalar.activation(hid[:, e % 2, j, :], psh[:, j, :], ACT.Relu,
                                         bias=b1[:, e * FT0 + j:e * FT0 + j + 1]).then_inc(relu_done, 1)

                for e in range(E0):
                    for j in range(FT0):
                        relu(0, e, j)
                with act.Fori(1, NCH) as c:
                    for e in range(E0):
                        for j in range(FT0):
                            relu(c, e, j)

            @block.vector
            def _(dve):
                dve.wait_ge(weights_in, FFN0_LOADS)
                dve.wait_ge(routed, 1)
                link = Chain(dve, chain)
                link(nc.vector.tensor_tensor(score[:], psr[:], br[:].unsqueeze(1).broadcast_to([P, NT, E0]), ALU.add))
                first_argmax(link, nc, mask, score, top, pref, eq, rank, E0)
                link(nc.vector.tensor_scalar(mask[:], mask[:], 0.5, None, ALU.mult))

                def bias(c):
                    for e in range(E0):
                        for q in range(4):
                            if e:
                                dve.wait_ge(biased, 4 * (E0 * c + e - 1) + q + 1)
                            nc.vector.scalar_tensor_tensor(X[:, 4 * c + q, :], b2[:, e, :], mask[:, 4 * c + q, e:e + 1],
                                                           X[:, 4 * c + q, :], ALU.mult, ALU.add).then_inc(biased, 1)

                def add(c, e):
                    dve.wait_ge(y_done, E0 * c + e + 1)
                    for q in range(4):
                        if e:
                            dve.wait_ge(added, 4 * (E0 * c + e - 1) + q + 1)
                        else:
                            dve.wait_ge(biased, 4 * (E0 * c + E0 - 1) + q + 1)
                        nc.vector.scalar_tensor_tensor(X[:, 4 * c + q, :], psy[:, e % 2, q, :],
                                                       mask[:, 4 * c + q, e:e + 1], X[:, 4 * c + q, :],
                                                       ALU.mult, ALU.add).then_inc(added, 1)

                with dve.Fori(0, NCH) as c:
                    bias(c)
                    for e in range(E0):
                        add(c, e)
        m.clear_sems()


def load_ffn1(nc, m, w, sem):
    wgate = m.sb("wgate", [P, E1])
    wg = m.sb("wg", [P, E1 * M1])
    wu = m.sb("wu", [P, E1 * M1])
    wd = m.sb("wd", [P, KT1, D])
    sel = m.sb("sel", [96, KT1, P], BF16)

    def load(eng):
        eng.dma_start(wgate[:], w["w_gate"]).then_inc(sem, 16)
        eng.dma_start(wg[:], w["w_gP"]).then_inc(sem, 16)
        eng.dma_start(wu[:], w["w_uP"]).then_inc(sem, 16)
        eng.dma_start(wd[:], w["w_dP"].rearrange("(k p) d -> p k d", p=P)).then_inc(sem, 16)
        eng.dma_start(sel[:], w["sel"].rearrange("r (k p) -> r k p", p=P)).then_inc(sem, 16)

    return (wgate, wg, wu, wd, sel), load


FFN1_LOADS = 16 * 5


def ffn1(nc, tag, X, XNT, ident, rank, w, weights_in):
    with ExitStack() as ctx:
        m = Mem(nc, ctx, tag)
        wgate, wg, wu, wd, sel = w
        score = m.sb("score", [P, NT, E1])
        rest = m.sb("rest", [P, NT, E1])
        top = m.sb("top", [P, NT])
        top2 = m.sb("top2", [P, NT])
        eq = m.sb("eq", [P, NT, E1])
        pref = m.sb("pref", [P, NT, E1])
        one1 = m.sb("one1", [P, NT, E1])
        one2 = m.sb("one2", [P, NT, E1])
        pr = m.sb("pr", [P, 4, NT])
        gate = m.sb("gate", [P, NT, E1])
        gate3 = m.sb("gate3", [P, NT, 96], BF16)
        gateT = m.sb("gateT", [96, TOK], BF16)
        identb = m.sb("identb", [P, P], BF16)
        sg = m.sb("sg", [P, 2, CH])
        su = m.sb("su", [P, 2, CH])
        hid = m.sb("hid", [P, KT1, CH])
        psg = m.ps("psg", [P, 2, CH])
        psu = m.ps("psu", [P, 2, CH])
        psm = m.ps("psm", [P, 2, CH])
        psy = m.ps("psy", [P, 2, 4, D])
        ident_ready, routed, chain, e2 = (m.sem(x) for x in ("identb", "routed", "chain", "e2"))
        cleared, gate_ready, turned, gate_out = (m.sem(x) for x in ("cleared", "gate", "turned", "gateout"))
        g_done, u_done, m_done, silu_done, su_done, hid_done, y_done, added = (
            m.sem(x) for x in ("gd", "ud", "md", "silu", "sud", "hidd", "yd", "added"))
        with nc.Block() as block:

            @block.gpsimd
            def _(pool):
                nc.gpsimd.memset(gate3[:], 0.0).then_inc(cleared, 1)

            @block.tensor
            def _(pe):
                pe.wait_ge(weights_in, FFN1_LOADS)
                pr_out = psg[:, 0, 0:NT * E1].rearrange("p (k e) -> p k e", e=E1)
                for k in range(NT):
                    last = nc.tensor.matmul(pr_out[:, k, :], XNT[:, k * P:(k + 1) * P], wgate[:],
                                            start=True, stop=True)
                last.then_inc(routed, 1)
                pe.wait_ge(gate_ready, 1)
                pe.wait_ge(ident_ready, 1)
                for c in range(NCH):
                    if c >= 2:
                        pe.wait_ge(gate_out, c - 1)
                    out = psm[:, c % 2, :].bitcast(BF16)
                    for q in range(4):
                        last = nc.tensor.transpose(out[0:96, q * P:(q + 1) * P], gate3[:, 4 * c + q, :], identb[:])
                    last.then_inc(turned, 1)
                pe.wait_ge(gate_out, NCH)

                def chunk(c, first):
                    for k in range(KT1):
                        s = KT1 * c + k
                        if k >= 2 or not first:
                            pe.wait_ge(silu_done, s - 1)
                            pe.wait_ge(su_done, s - 1)
                            pe.wait_ge(hid_done, s - 1)
                        b = (k % 2)
                        x = XNT[:, bass.ds(c * CH, CH)]
                        nc.tensor.matmul(psg[:, b, :], wg[:, k * P:(k + 1) * P], x, start=True, stop=True)\
                            .then_inc(g_done, 1)
                        nc.tensor.matmul(psu[:, b, :], wu[:, k * P:(k + 1) * P], x, start=True, stop=True)\
                            .then_inc(u_done, 1)
                        nc.tensor.matmul(psm[:, b, :], sel[:, k, :], gateT[:, bass.ds(c * CH, CH)],
                                         start=True, stop=True).then_inc(m_done, 1)

                def output(c, first):
                    pe.wait_ge(hid_done, KT1 * c + KT1)
                    if not first:
                        pe.wait_ge(added, 4 * c)
                    for q in range(4):
                        for k in range(KT1):
                            last = nc.tensor.matmul(psy[:, 0, q, :], hid[:, k, q * P:(q + 1) * P], wd[:, k, :],
                                                    start=(k == 0), stop=(k == KT1 - 1))
                    last.then_inc(y_done, 1)

                chunk(0, True)
                output(0, True)
                with pe.Fori(1, NCH) as c:
                    chunk(c, False)
                    output(c, False)

            @block.scalar
            def _(act):
                act.wait_ge(e2, 1)
                nc.scalar.activation(pr[:, 1, :], pr[:, 0, :], ACT.Exp).then_inc(e2, 1)
                for c in range(NCH):
                    act.wait_ge(turned, c + 1)
                    nc.scalar.activation(gateT[:, c * CH:(c + 1) * CH], psm[:, c % 2, :].bitcast(BF16)[0:96, 0:CH],
                                         ACT.Copy).then_inc(gate_out, 1)

                def silu(c, k, first):
                    s = KT1 * c + k
                    act.wait_ge(g_done, s + 1)
                    if k >= 2 or not first:
                        act.wait_ge(su_done, s - 1)
                    nc.scalar.activation(sg[:, k % 2, :], psg[:, k % 2, :], ACT.Silu).then_inc(silu_done, 1)

                for k in range(KT1):
                    silu(0, k, True)
                with act.Fori(1, NCH) as c:
                    for k in range(KT1):
                        silu(c, k, False)

            @block.vector
            def _(dve):
                nc.vector.tensor_copy(identb[:], ident[:]).then_inc(ident_ready, 1)
                dve.wait_ge(routed, 1)
                link = Chain(dve, chain)
                link(nc.vector.tensor_copy(score[:], psg[:, 0, 0:NT * E1].rearrange("p (k e) -> p k e", e=E1)))
                first_argmax(link, nc, one1, score, top, pref, eq, rank, E1)
                link(nc.vector.scalar_tensor_tensor(rest[:], one1[:], -3.0e38, score[:], ALU.mult, ALU.add))
                first_argmax(link, nc, one2, rest, top2, pref, eq, rank, E1)
                nc.vector.tensor_tensor(pr[:, 0, :], top2[:], top[:], ALU.subtract).then_inc(e2, 1)
                dve.wait_ge(e2, 2)
                link(nc.vector.tensor_scalar(pr[:, 0, :], pr[:, 1, :], 2.0, 2.0, ALU.mult, ALU.add))
                link(nc.vector.reciprocal(pr[:, 2, :], pr[:, 0, :]))
                link(nc.vector.tensor_tensor(pr[:, 3, :], pr[:, 2, :], pr[:, 1, :], ALU.mult))
                link(nc.vector.tensor_tensor(gate[:], one1[:], pr[:, 2, :].unsqueeze(2).broadcast_to([P, NT, E1]),
                                             ALU.mult))
                link(nc.vector.tensor_tensor(eq[:], one2[:], pr[:, 3, :].unsqueeze(2).broadcast_to([P, NT, E1]),
                                             ALU.mult))
                link(nc.vector.tensor_tensor(gate[:], gate[:], eq[:], ALU.add))
                dve.wait_ge(cleared, 1)
                link(nc.vector.tensor_copy(gate3[:, :, 0:E1], gate[:]))
                link(nc.vector.tensor_tensor(gate[:], gate[:], gate3[:, :, 0:E1], ALU.subtract))
                link(nc.vector.tensor_copy(gate3[:, :, 32:32 + E1], gate[:]))
                link(nc.vector.tensor_tensor(gate[:], gate[:], gate3[:, :, 32:32 + E1], ALU.subtract))
                nc.vector.tensor_copy(gate3[:, :, 64:64 + E1], gate[:]).then_inc(gate_ready, 1)

                def products(c, k, first):
                    s = KT1 * c + k
                    dve.wait_ge(silu_done, s + 1)
                    dve.wait_ge(u_done, s + 1)
                    if k >= 2 or not first:
                        dve.wait_ge(hid_done, s - 1)
                    nc.vector.tensor_tensor(su[:, k % 2, :], psu[:, k % 2, :], sg[:, k % 2, :], ALU.mult)\
                        .then_inc(su_done, 1)
                    dve.wait_ge(m_done, s + 1)
                    dve.wait_ge(su_done, s + 1)
                    if not first:
                        dve.wait_ge(y_done, c)
                    nc.vector.tensor_tensor(hid[:, k, :], psm[:, k % 2, :], su[:, k % 2, :], ALU.mult)\
                        .then_inc(hid_done, 1)

                def add(c):
                    dve.wait_ge(y_done, c + 1)
                    for q in range(4):
                        nc.vector.tensor_tensor(X[:, 4 * c + q, :], psy[:, 0, q, :], X[:, 4 * c + q, :], ALU.add)\
                            .then_inc(added, 1)

                for k in range(KT1):
                    products(0, k, True)
                add(0)
                with dve.Fori(1, NCH) as c:
                    for k in range(KT1):
                        products(c, k, False)
                    add(c)
        m.clear_sems()


def load_attention(nc, m, w, sem, biased):
    wqT, wkT, wvT, woT = (m.sb(f"w{n}T{int(biased)}", [P, D]) for n in "qkvo")
    bq, bv, bo, lw, lb = (m.sb(n, [P, 2 if n == "bq" else D]) if biased else None
                          for n in ("bq", "bv", "bo", "lw", "lb"))

    def load(eng):
        for dst, name in ((wqT, "WqT"), (wkT, "WkT"), (wvT, "WvT"), (woT, "WoT")):
            eng.dma_start(dst[:], w[name]).then_inc(sem, 16)
        if biased:
            eng.dma_start(bq[:, 0:1], w["bq"].unsqueeze(1)).then_inc(sem, 16)
            eng.dma_start(bq[:, 1:2], w["bk"].unsqueeze(1)).then_inc(sem, 16)
            for dst, name in ((bv, "bv"), (bo, "bo"), (lw, "ln_w"), (lb, "ln_b")):
                eng.dma_start(dst[:], w[name].unsqueeze(0).broadcast_to([P, D])).then_inc(sem, 16)

    return (wqT, wkT, wvT, bq, bv, woT, bo, lw, lb), load


ATTENTION_LOADS = (16 * 4, 16 * 10)


def project(nc, tag, XNT, V, qd, kd, w, weights_in, biased, ones):
    with ExitStack() as ctx:
        m = Mem(nc, ctx, tag)
        wqT, wkT, wvT, bq, bv = w[:5]
        parts = m.sb("parts", [P, 2, SPLIT, CH], BF16)
        r1 = m.sb("r1", [P, 2, CH])
        psq = m.ps("psq", [P, 2, CH])
        psv = m.ps("psv", [P, 4, D])
        q_done, hi_done, r1_done, mid_done, lo_done = (
            m.sem(x) for x in ("qd", "hi", "r1", "mid", "lo"))
        stored = [m.sem("stored_q"), m.sem("stored_k")]
        v_done, v_out, ones_set = m.sem("vd"), m.sem("vo"), m.sem("ones")
        loads = ATTENTION_LOADS[biased]
        with nc.Block() as block:

            @block.sync
            def _(sp):
                with sp.Fori(0, B) as b:
                    for half in range(2):
                        for n, dst in enumerate((qd, kd)):
                            sp.wait_ge(lo_done, 4 * b + 2 * half + n + 1)
                            for s in range(SPLIT):
                                sp.dma_start(dst[s, bass.ds(b * H, H), :, half * CH:(half + 1) * CH],
                                             parts[:, n, s, :])\
                                    .then_inc(stored[n], 16)
                for n in range(2):
                    sp.wait_ge(stored[n], 16 * SPLIT * NCH)

            @block.tensor
            def _(pe):
                pe.wait_ge(weights_in, loads)

                def chunk(c, first):
                    for n, wT in enumerate((wqT, wkT)):
                        if not first:
                            pe.wait_ge(r1_done, 2 * c - 1 + n)
                        nc.tensor.matmul(psq[:, n, :], wT[:], XNT[:, bass.ds(c * CH, CH)], start=True, stop=True)\
                            .then_inc(q_done, 1)

                chunk(0, True)
                with pe.Fori(1, NCH) as c:
                    chunk(c, False)
                for c in range(NCH):
                    if c:
                        pe.wait_ge(v_out, 4 * c)
                    for q in range(4):
                        last = nc.tensor.matmul(psv[:, q, :], XNT[:, (4 * c + q) * P:(4 * c + q + 1) * P], wvT[:],
                                                start=True, stop=True)
                    last.then_inc(v_done, 1)

            @block.scalar
            def _(act):
                act.wait_ge(weights_in, loads)

                def chunk(c, first):
                    for n in range(2):
                        act.wait_ge(q_done, 2 * c + n + 1)
                        if not first:
                            act.wait_ge(stored[n], 16 * SPLIT * c)
                        nc.scalar.activation(parts[:, n, 0, :], psq[:, n, :], ACT.Identity,
                                             bias=bq[:, n:n + 1] if biased else 0.0).then_inc(hi_done, 1)
                        act.wait_ge(r1_done, 2 * c + n + 1)
                        nc.scalar.activation(parts[:, n, 1, :], r1[:, n, :], ACT.Copy).then_inc(mid_done, 1)

                chunk(0, True)
                with act.Fori(1, NCH) as c:
                    chunk(c, False)

            @block.vector
            def _(dve):
                dve.wait_ge(weights_in, loads)
                nc.vector.memset(V[:, :, :, DH:DH + 1], ones).then_inc(ones_set, 1)

                def chunk(c, first):
                    for n in range(2):
                        dve.wait_ge(hi_done, 2 * c + n + 1)
                        if not first:
                            dve.wait_ge(lo_done, 2 * c - 1 + n)
                        nc.vector.scalar_tensor_tensor(r1[:, n, :], psq[:, n, :], bq[:, n:n + 1] if biased else 0.0,
                                                       parts[:, n, 0, :], ALU.add, ALU.subtract).then_inc(r1_done, 1)
                        dve.wait_ge(mid_done, 2 * c + n + 1)
                        nc.vector.tensor_tensor(parts[:, n, 2, :], r1[:, n, :], parts[:, n, 1, :], ALU.subtract)\
                            .then_inc(lo_done, 1)

                chunk(0, True)
                with dve.Fori(1, NCH) as c:
                    chunk(c, False)
                for c in range(NCH):
                    dve.wait_ge(v_done, c + 1)
                    for q in range(4):
                        b, t = c // 2, (4 * c + q) % TT
                        out = V[:, b * H:(b + 1) * H, t, 0:DH]
                        src = psv[:, q, :].rearrange("p (h d) -> p h d", d=DH)
                        if biased:
                            nc.vector.tensor_tensor(out, src, bv[:].rearrange("p (h d) -> p h d", d=DH), ALU.add)\
                                .then_inc(v_out, 1)
                        else:
                            nc.vector.tensor_copy(out, src).then_inc(v_out, 1)
        m.clear_sems()


def project_out(nc, tag, X, F, ident, w, weights_in, normed):
    with ExitStack() as ctx:
        m = Mem(nc, ctx, tag)
        woT, bo, lw, lb = w[5:]
        fT = m.sb("fT", [P, 2, P])
        y = m.sb("y", [P, NT, D])
        stats = m.sb("stats", [P, NT, 6])
        mv = m.sb("mv", [P, NT, 2])
        ve = m.sb("ve", [P, NT])
        rs = m.sb("rs", [P, NT])
        t1 = m.sb("t1", [P, NT])
        t2 = m.sb("t2", [P, NT])
        ptr = m.ps("ptr", [P, 2, CH])
        psy = m.ps("psy", [P, 2, CH])
        turned, copied, y_done, added, chain, ve_ready, lnv, st, ag, p1, p2 = (
            m.sem(x) for x in ("turned", "copied", "yd", "added", "chain", "ve", "lnv", "st", "ag", "p1", "p2"))
        loads = ATTENTION_LOADS[normed]
        with nc.Block() as block:

            @block.tensor
            def _(pe):
                pe.wait_ge(weights_in, loads)

                def turn(k):
                    if k >= 2:
                        pe.wait_ge(copied, k - 1)
                    nc.tensor.transpose(ptr[:, k % 2, 0:P], F[k], ident[:]).then_inc(turned, 1)

                turn(0)
                for k in range(NT):
                    if k + 1 < NT:
                        turn(k + 1)
                    pe.wait_ge(copied, k + 1)
                    if k >= 2:
                        pe.wait_ge(added, k - 1)
                    nc.tensor.matmul(psy[:, k % 2, 0:D], fT[:, k % 2, :], woT[:], start=True, stop=True)\
                        .then_inc(y_done, 1)

            @block.scalar
            def _(act):
                for k in range(NT):
                    act.wait_ge(turned, k + 1)
                    if k >= 2:
                        act.wait_ge(y_done, k - 1)
                    nc.scalar.activation(fT[:, k % 2, :], ptr[:, k % 2, 0:P], ACT.Copy).then_inc(copied, 1)
                if normed:
                    act.wait_ge(ve_ready, 1)
                    nc.scalar.activation(rs[:], ve[:], ACT.Ln).then_inc(lnv, 1)
                    act.wait_ge(lnv, 1)
                    nc.scalar.activation(rs[:], rs[:], ACT.Exp, scale=-0.5).then_inc(lnv, 1)

            @block.vector
            def _(dve):
                dve.wait_ge(weights_in, loads)
                for k in range(NT):
                    dve.wait_ge(y_done, k + 1)
                    if normed:
                        nc.vector.tensor_tensor(y[:, k, :], psy[:, k % 2, 0:D], bo[:], ALU.add).then_inc(added, 1)
                    else:
                        nc.vector.tensor_tensor(X[:, k, :], psy[:, k % 2, 0:D], X[:, k, :], ALU.add).then_inc(added, 1)
                if not normed:
                    return
                dve.wait_ge(added, NT)
                with dve.Fori(0, NT) as i:
                    nc.vector.bn_stats(stats[:, i, :], y[:, i, :]).then_inc(st, 1)
                dve.wait_ge(st, NT)
                for i in range(NT):
                    nc.vector.bn_aggr(mv[:, i, :], stats[:, i, :]).then_inc(ag, 1)
                dve.wait_ge(ag, NT)
                nc.vector.tensor_scalar(ve[:], mv[:, :, 1], LN_EPS, None, ALU.add).then_inc(ve_ready, 1)
                dve.wait_ge(ve_ready, 1)
                dve.wait_ge(lnv, 2)
                link = Chain(dve, chain)
                link(nc.vector.tensor_tensor(t1[:], rs[:], rs[:], ALU.mult))
                link(nc.vector.tensor_tensor(t2[:], t1[:], ve[:], ALU.mult))
                link(nc.vector.tensor_scalar(t1[:], t2[:], -0.5, 1.5, ALU.mult, ALU.add))
                link(nc.vector.tensor_tensor(t2[:], rs[:], t1[:], ALU.mult))
                with dve.Fori(0, NT) as k:
                    nc.vector.tensor_scalar(y[:, k, :], y[:, k, :], mv[:, k, 0:1], t2[:, bass.ds(k, 1)],
                                            ALU.subtract, ALU.mult).then_inc(p1, 1)
                dve.wait_ge(p1, NT)
                lwb = lw[:].unsqueeze(1).broadcast_to([P, NT, D])
                lbb = lb[:].unsqueeze(1).broadcast_to([P, NT, D])
                link(nc.vector.tensor_tensor(y[:], y[:], lwb, ALU.mult))
                link(nc.vector.tensor_tensor(X[:], X[:], lbb, ALU.add))
                link(nc.vector.tensor_tensor(X[:], X[:], y[:], ALU.add))
        m.clear_sems()


def load_stacks(eng, Q, K, qd, kd, g, sem):
    for i in range(SPLIT):
        rows = slice(i * SPLIT * DH, (i + 1) * SPLIT * DH)
        eng.dma_start(Q[rows, :], qd[:, g]).then_inc(sem, 16)
        eng.dma_start(K[rows, :], kd[i, g].unsqueeze(0).broadcast_to([SPLIT, DH, T])).then_inc(sem, 16)


STACK_DMAS = 2 * SPLIT


def clear_stacks(eng, Qs, Ks, sem):
    eng.memset(Qs[64:P], 0.0).then_inc(sem, 1)
    eng.memset(Ks[64:ONES_ROW], 0.0).then_inc(sem, 1)
    eng.memset(Ks[ONES_ROW:P], 1.0).then_inc(sem, 1)


CLEARS = 3


def attend_causal(nc, tag, V, F, qd, kd, ident, masks):
    SLOTS = HEADS // 2
    UNROLL = RING
    LT = 2
    SC = DH ** -0.5
    MAXIMA = [(u, t, half) for u in range(2) for t in range(TT) for half in range(2) if half * CH < (t + 1) * P]
    WEIGHTS = [(u, t, half) for t in range(TT) for u in range(2) for half in range(2) if t * P < (half + 1) * CH]
    NP = len(MAXIMA)
    done = [1 + max(y for y, (_, t, _) in enumerate(WEIGHTS) if t == k) for k in range(TT)]
    with ExitStack() as ctx:
        m = Mem(nc, ctx, tag)
        Qs = m.sb("Q", [P, 2 * RING, T], BF16)
        Ks = m.sb("K", [P, 2 * RING, T], BF16)
        Q, K = ([stack[:, r, :] for r in range(2 * RING)] for stack in (Qs, Ks))
        mask_nm = m.sb("mask_nm", [P, P], BF16)
        mask_mn = m.sb("mask_mn", [P, P], BF16)
        identb = m.sb("identb", [P, P], BF16)
        Vh = m.sb("Vh", [P, 2, 2, TT, 32])
        mx = m.sb("mx", [P, 2, 2, 2, TT])
        rem = m.sb("rem", [P, 2, TT])
        neg = m.sb("neg", [P, P], BF16)
        neg3 = neg[:, 0:2 * SPLIT * TT].rearrange("p (u s t) -> p u s t", u=2, s=SPLIT)
        rows = m.sb("rows", [2 * SPLIT * TT, P], BF16)
        pt = m.sb("pt", [P, 2, 2, T])
        osb = m.sb("osb", [P, CH])
        rz = m.sb("rz", [P, 4, 4])
        pm = m.ps("pm", [P, 3, CH])
        pb = m.ps("pb", [P, 3, CH])
        po = m.ps("po", [P, CH])
        ptr = m.ps("ptr", [P, CH])
        loaded, identb_ready, cleared, vh_cleared, neg_cleared = (
            m.sem(x) for x in ("loaded", "identb", "cleared", "vhc", "negc"))
        stack_in = [m.sem(f"stack{r}") for r in range(RING)]
        rows_in = [m.sem(f"rowsin{r}") for r in range(RING)]
        max_mm, max_red, parts_ready, rows_turned, rows_sb, chain = (
            m.sem(x) for x in ("maxmm", "maxred", "parts", "rturned", "rsb", "chain"))
        tau_exp = [m.sem(f"tauexp{r}") for r in range(3)]
        tau_mm, vh_ready, pv_done, o_sb, o_turned, f_done, rz_done = (
            m.sem(x) for x in ("taumm", "vh", "pv", "osb", "oturned", "fd", "rz"))
        PAIR_LOADS = 16 * 2 * STACK_DMAS

        def at(it, j, lag):
            s = UNROLL * it + (j - lag)
            return None if isinstance(s, int) and not 0 <= s < SLOTS else s

        def wait_from(eng, sem, value):
            if not (isinstance(value, int) and value <= 0):
                eng.wait_ge(sem, value)

        def slots(eng, body):
            for j in range(UNROLL):
                body(0, j)
            with eng.Fori(1, SLOTS // UNROLL) as it:
                for j in range(UNROLL):
                    body(it, j)
            for j in range(LT + 1):
                body(SLOTS // UNROLL, j)

        with nc.Block() as block:

            @block.gpsimd
            def _(pool):
                nc.gpsimd.memset(Vh[:], 0.0).then_inc(vh_cleared, 1)
                pool.wait_ge(vh_cleared, 1)

                def body(it, j):
                    s = at(it, j, LT)
                    if s is None:
                        return
                    if not (isinstance(s, int) and s < 2):
                        pool.wait_ge(pv_done, TT * (s - 1))
                    for u in range(2):
                        nc.gpsimd.tensor_copy(Vh[:, (j - LT) % 2, u, :, 0:DH + 1], V[:, 2 * s + u, :, :])\
                            .then_inc(vh_ready, 1)

                slots(pool, body)

            @block.sync
            def _(sp):
                sp.dma_start(mask_nm[:], masks[0]).then_inc(loaded, 16)
                sp.dma_start(mask_mn[:], masks[1]).then_inc(loaded, 16)
                sp.wait_ge(cleared, CLEARS)

                def load(s, r, wait):
                    if wait:
                        sp.wait_ge(tau_mm, NP * (s - RING) + NP)
                    for u in range(2):
                        load_stacks(sp, Q[2 * r + u], K[2 * r + u], qd, kd, 2 * s + u, stack_in[r])

                def send_rows(s, r):
                    sp.wait_ge(rows_sb, s + 1)
                    for u in range(2):
                        n = SPLIT * TT
                        sp.dma_start(Q[2 * r + u][ONES_ROW:ONES_ROW + SPLIT, :].rearrange("s (t n) -> s t n", n=P),
                                     rows[u * n:(u + 1) * n, :])\
                            .then_inc(rows_in[r], 16)

                load(0, 0, False)
                load(1, 1, False)
                for j in range(UNROLL):
                    load(j + 2, (j + 2) % RING, j + 2 >= RING)
                    send_rows(j, j)
                with sp.Fori(1, SLOTS // UNROLL - 1) as it:
                    for j in range(UNROLL):
                        load(UNROLL * it + j + 2, (j + 2) % RING, True)
                        send_rows(UNROLL * it + j, j)
                for j in range(UNROLL):
                    s = SLOTS - UNROLL + j
                    if s + 2 < SLOTS:
                        load(s + 2, (j + 2) % RING, True)
                    send_rows(s, j)

            @block.tensor
            def _(pe):
                pe.wait_ge(loaded, 32)
                pe.wait_ge(identb_ready, 1)

                def scores_max(s, j, y):
                    u, t, half = MAXIMA[y]
                    r, lo, hi = 2 * (j % RING) + u, half * CH, min((half + 1) * CH, (t + 1) * P)
                    diagonal = hi == (t + 1) * P
                    wait_from(pe, max_red, NP * s + y - 2)
                    out = pm[:, y % 3, :]
                    last = nc.tensor.matmul(out[:, 0:hi - lo], Q[r][0:96, t * P:(t + 1) * P], K[r][0:96, lo:hi],
                                            start=True, stop=not diagonal)
                    if diagonal:
                        last = nc.tensor.matmul(out[:, hi - lo - P:hi - lo], identb[:], mask_nm[:],
                                                start=False, stop=True)
                    last.then_inc(max_mm, 1)

                def scores_tau(s, j, y):
                    u, t, half = WEIGHTS[y]
                    r, lo, hi = 2 * (j % RING) + u, max(half * CH, t * P), (half + 1) * CH
                    diagonal = lo == t * P
                    wait_from(pe, tau_exp[y % 3], NP // 3 * s + y // 3)
                    out = pb[:, y % 3, :]
                    last = nc.tensor.matmul(out[:, lo % CH:CH], K[r][:, t * P:(t + 1) * P], Q[r][:, lo:hi],
                                            start=True, stop=not diagonal)
                    if diagonal:
                        last = nc.tensor.matmul(out[:, lo % CH:lo % CH + P], identb[:], mask_mn[:],
                                                start=False, stop=True)
                    last.then_inc(tau_mm, 1)

                def weigh(s, j, t):
                    final = done[t] - 1
                    pe.wait_ge(tau_exp[final % 3], NP // 3 * s + final // 3 + 1)
                    if t == 0:
                        pe.wait_ge(vh_ready, 2 * s + 2)
                        if not (isinstance(s, int) and s < 1):
                            pe.wait_ge(o_sb, s)
                    for u in range(2):
                        for half in range(2):
                            lo, hi = max(half * CH, t * P), (half + 1) * CH
                            if lo >= hi:
                                continue
                            q = 2 * u + half
                            last = nc.tensor.matmul(po[32 * q:32 * q + 32, lo - half * CH:CH],
                                                    Vh[:, j % 2, u, t, :], pt[:, u, t % 2, lo:hi],
                                                    start=(t == 0), stop=(lo + P == hi))
                    last.then_inc(pv_done, 1)

                def turn_rows(s):
                    pe.wait_ge(parts_ready, s + 1)
                    if not (isinstance(s, int) and s < LT + 1):
                        pe.wait_ge(f_done, 2 * (s - LT))
                    nc.tensor.transpose(ptr[:].bitcast(BF16)[:, 0:P], neg[:], identb[:]).then_inc(rows_turned, 1)

                def turn_out(s, rows_before):
                    pe.wait_ge(o_sb, s + 1)
                    if rows_before is not None:
                        pe.wait_ge(rows_sb, rows_before + 1)
                    else:
                        pe.wait_ge(rows_sb, SLOTS)
                        pe.wait_ge(f_done, 2 * s)
                    for c in range(4):
                        last = nc.tensor.transpose(ptr[:, c * P:(c + 1) * P], osb[:, c * P:(c + 1) * P], ident[:])
                    last.then_inc(o_turned, 1)

                def body(it, j):
                    sm, sr, st, so = at(it, j, 0), at(it, j, 1), at(it, j, LT), at(it, j, LT + 1)
                    if sm is not None:
                        pe.wait_ge(stack_in[j % RING], PAIR_LOADS * (it + 1))
                    if st is not None:
                        jt = j - LT
                        pe.wait_ge(rows_in[jt % RING], 32 * (it + jt // RING + 1))
                    for y in range(NP):
                        if sm is not None:
                            scores_max(sm, j, y)
                        if y == 9 and sr is not None:
                            turn_rows(sr)
                        if st is not None:
                            scores_tau(st, j - LT, y)
                            if y - 2 in done:
                                weigh(st, j - LT, done.index(y - 2))
                        if y == 15 and so is not None:
                            turn_out(so, sr)
                    if st is not None:
                        for t in range(TT):
                            if done[t] >= NP - 2:
                                weigh(st, j - LT, t)

                slots(pe, body)

            @block.scalar
            def _(act):

                def exp_tau(s, y):
                    u, t, half = WEIGHTS[y]
                    lo, hi = max(half * CH, t * P), (half + 1) * CH
                    act.wait_ge(tau_mm, NP * s + y + 1)
                    wait_from(act, pv_done, TT * s + t - 1)
                    nc.scalar.activation(pt[:, u, t % 2, lo:hi], pb[:, y % 3, lo % CH:CH], ACT.Exp, scale=SC)\
                        .then_inc(tau_exp[y % 3], 1)

                def copy_out(s):
                    act.wait_ge(pv_done, TT * s + TT)
                    if not (isinstance(s, int) and s < 1):
                        act.wait_ge(o_turned, s)
                    nc.scalar.activation(osb[:], po[:], ACT.Copy).then_inc(o_sb, 1)

                def body(it, j):
                    st, so = at(it, j, LT), at(it, j, LT + 1)
                    for y in range(NP):
                        if st is not None:
                            exp_tau(st, y)
                        if y == 0 and so is not None:
                            copy_out(so)

                slots(act, body)

            @block.vector
            def _(dve):
                clear_stacks(nc.vector, Qs, Ks, cleared)
                nc.vector.tensor_copy(identb[:], ident[:]).then_inc(identb_ready, 1)
                nc.vector.memset(neg[:], 0.0).then_inc(neg_cleared, 1)
                dve.wait_ge(neg_cleared, 1)

                def part(s, j, n):
                    far, top = mx[:, (j - 1) % 2, 1], mx[:, (j - 1) % 2, 0]
                    if n == 0:
                        dve.wait_ge(max_red, NP * s + NP)
                        nc.vector.tensor_tensor(top[:, :, TT // 2:], top[:, :, TT // 2:], far[:, :, TT // 2:], ALU.max)\
                            .then_inc(chain, 1)
                    else:
                        dve.wait_ge(chain, 5 * s + n)
                    if n == 1:
                        wait_from(dve, rows_turned, s)
                        nc.vector.tensor_scalar(neg3[:, :, 0, :], top, -1.0, None, ALU.mult).then_inc(chain, 1)
                    if n == 2:
                        nc.vector.scalar_tensor_tensor(rem[:], top, -1.0, neg3[:, :, 0, :], ALU.mult, ALU.subtract)\
                            .then_inc(chain, 1)
                    if n == 3:
                        nc.vector.tensor_copy(neg3[:, :, 1, :], rem[:]).then_inc(chain, 1)
                    if n == 4:
                        nc.vector.tensor_tensor(rem[:], rem[:], neg3[:, :, 1, :], ALU.subtract).then_inc(chain, 1)
                    if n == 5:
                        nc.vector.tensor_copy(neg3[:, :, 2, :], rem[:]).then_inc(parts_ready, 1)

                def output(s, n):
                    o = ptr[:].rearrange("p (c q k) -> p c q k", c=4, q=4)
                    if n == 0:
                        dve.wait_ge(o_turned, s + 1)
                        if not (isinstance(s, int) and s < 1):
                            dve.wait_ge(f_done, 2 * s)
                        nc.vector.reciprocal(rz[:], o[:, :, :, DH]).then_inc(rz_done, 1)
                    else:
                        u = n - 1
                        dve.wait_ge(rz_done, s + 1)
                        nc.vector.tensor_tensor(
                            F[:, :, 2 * s + u, :].rearrange("p (h c) d -> p c h d", h=2),
                            o[:, :, 2 * u:2 * u + 2, 0:DH],
                            rz[:, :, 2 * u:2 * u + 2].unsqueeze(3).broadcast_to([P, 4, 2, DH]), ALU.mult)\
                            .then_inc(f_done, 1)

                def body(it, j):
                    sm, sr, so = at(it, j, 0), at(it, j, 1), at(it, j, LT + 1)
                    for y in range(NP):
                        if y < 6 and sr is not None:
                            part(sr, j, y)
                        if sm is not None:
                            u, t, half = MAXIMA[y]
                            dve.wait_ge(max_mm, NP * sm + y + 1)
                            nc.vector.tensor_reduce(mx[:, j % 2, half, u, t:t + 1],
                                                    pm[:, y % 3, 0:min(CH, (t + 1) * P - half * CH)],
                                                    AX.X, ALU.max).then_inc(max_red, 1)
                        if y == 11 and sr is not None:
                            dve.wait_ge(rows_turned, sr + 1)
                            if not (isinstance(sr, int) and sr < 1):
                                jr = j - 2
                                dve.wait_ge(rows_in[jr % RING], 32 * (it + jr // RING + 1))
                            nc.vector.tensor_copy(rows[:], ptr[:].bitcast(BF16)[0:2 * SPLIT * TT, 0:P])\
                                .then_inc(rows_sb, 1)
                        if 17 <= y < 20 and so is not None:
                            output(so, y - 17)

                slots(dve, body)
        m.clear_sems()


def attend_both(nc, tag, V, F, par, qd, kd, ident):
    SLOTS = HEADS * TT // 2
    PER = TT // 2
    UNROLL = PER * RING
    LS, LT, LE, LP = 4, 6, 6, 7
    SC = DH ** -0.5
    EDGE = 8
    CUT = 25 * T // 32
    with ExitStack() as ctx:
        m = Mem(nc, ctx, tag)
        Qs = m.sb("Q", [P, RING, T], BF16)
        Ks = m.sb("K", [P, RING, T], BF16)
        Q, K = ([stack[:, r, :] for r in range(RING)] for stack in (Qs, Ks))
        identb = m.sb("identb", [P, P], BF16)
        Vh = m.sb("Vh", [P, 2, TT, 32])
        parh = m.sb("parh", [P, RING, 2])
        mx = m.sb("mx", [P, 2, TT])
        rem = m.sb("rem", [P, TT])
        neg3 = m.sb("neg3", [P, SPLIT, TT], BF16)
        rows = m.sb("rows", [SPLIT * TT, P], BF16)
        pt = [m.sb(f"pt{r}", [P, 2, T]) for r in range(4)]
        sg = [m.sb(f"sg{r}", [P, 2, T]) for r in range(4)]
        shifted = m.sb("shifted", [P, 2, CUT])
        osb = m.sb("osb", [P, CH])
        rz = m.sb("rz", [P, 4, 4])
        fw = m.sb("fw", [P, 4, 4, DH])
        pm = m.ps("pm", [P, T])
        pa = m.ps("pa", [P, T])
        pb = m.ps("pb", [P, T])
        po = m.ps("po", [P, CH])
        ptr = m.ps("ptr", [P, CH])
        identb_ready, cleared, vh_cleared = (m.sem(x) for x in ("identb", "cleared", "vhc"))
        stack_in = [m.sem(f"stack{r}") for r in range(RING)]
        rows_in = [m.sem(f"rowsin{r}") for r in range(RING)]
        max_mm, max_red, parts_ready, rows_turned, rows_sb, chain = (
            m.sem(x) for x in ("maxmm", "maxred", "parts", "rturned", "rsb", "chain"))
        abs_mm, abs_done, shift_done, sq_pool, sq_dve, ln_done, sig_done = (
            m.sem(x) for x in ("absmm", "abs", "shift", "sqp", "sqd", "ln", "sig"))
        tau_mm, tau_exp, vh_ready, par_ready, pv_done, o_sb, o_turned, f_done, rz_done, weighed = (
            m.sem(x) for x in ("taumm", "tauexp", "vh", "par", "pv", "osb", "oturned", "fd", "rz", "weighed"))
        HEAD_LOADS = 16 * STACK_DMAS

        def at(it, j, lag):
            s = UNROLL * it + (j - lag)
            return None if isinstance(s, int) and not 0 <= s < SLOTS else s

        def head(it, j, lag):
            return RING * it + (j - lag) // PER

        def slots(eng, body):
            for j in range(UNROLL):
                body(0, j)
            with eng.Fori(1, SLOTS // UNROLL) as it:
                for j in range(UNROLL):
                    body(it, j)
            for j in range(LP + 2):
                body(SLOTS // UNROLL, j)

        def some(x, least=1):
            return not (isinstance(x, int) and x < least)

        with nc.Block() as block:

            @block.gpsimd
            def _(pool):
                nc.gpsimd.memset(Vh[:], 0.0).then_inc(vh_cleared, 1)
                pool.wait_ge(vh_cleared, 1)

                def body(it, j):
                    s = at(it, j, LS)
                    if s is None:
                        return
                    h = head(it, j, LS)
                    if (j - LS) % PER == 0:
                        if some(h, 2):
                            pool.wait_ge(pv_done, PER * (h - 1))
                        nc.gpsimd.tensor_copy(parh[:, ((j - LS) // PER) % RING, :], par[:, h, :])\
                            .then_inc(par_ready, 1)
                        nc.gpsimd.tensor_copy(Vh[:, ((j - LS) // PER) % 2, :, 0:DH + 1], V[:, h, :, :])\
                            .then_inc(vh_ready, 1)
                    buf = sg[(j - LS) % 4]
                    if some(s):
                        pool.wait_ge(sq_pool, s)
                    pool.wait_ge(abs_done, 2 * s + 2)
                    pool.wait_ge(par_ready, h + 1)
                    b2 = parh[:, ((j - LS) // PER) % RING, 0:1]
                    nc.gpsimd.tensor_tensor(shifted[:, :, 0:EDGE], buf[:, :, 0:EDGE],
                                            b2.unsqueeze(2).broadcast_to([P, 2, EDGE]), ALU.add).then_inc(shift_done, 1)
                    nc.gpsimd.tensor_scalar(shifted[:, :, EDGE:CUT], buf[:, :, EDGE:CUT], b2, 1.0, ALU.add, ALU.mult)\
                        .then_inc(shift_done, 1)
                    pool.wait_ge(shift_done, 2 * s + 2)
                    nc.gpsimd.tensor_tensor(buf[:, :, 0:CUT], buf[:, :, 0:CUT], shifted[:], ALU.mult)\
                        .then_inc(sq_pool, 1)

                slots(pool, body)

            @block.sync
            def _(sp):
                sp.wait_ge(cleared, CLEARS)

                def load(h, r, wait):
                    if wait:
                        sp.wait_ge(tau_mm, TT * (h - RING) + TT)
                    load_stacks(sp, Q[r], K[r], qd, kd, h, stack_in[r])

                def send_rows(h, r):
                    sp.wait_ge(rows_sb, h + 1)
                    sp.dma_start(Q[r][ONES_ROW:ONES_ROW + SPLIT, :].rearrange("s (t n) -> s t n", n=P),
                                 rows[:]).then_inc(rows_in[r], 16)

                load(0, 0, False)
                load(1, 1, False)
                for j in range(RING):
                    load(j + 2, (j + 2) % RING, j + 2 >= RING)
                    send_rows(j, j)
                with sp.Fori(1, HEADS // RING - 1) as it:
                    for j in range(RING):
                        load(RING * it + j + 2, (j + 2) % RING, True)
                        send_rows(RING * it + j, j)
                for j in range(RING):
                    h = HEADS - RING + j
                    if h + 2 < HEADS:
                        load(h + 2, (j + 2) % RING, True)
                    send_rows(h, j)

            @block.tensor
            def _(pe):
                pe.wait_ge(identb_ready, 1)

                def scores(out, lhsT, rhs, t, rows_, sem):
                    for lo in range(0, T, CH):
                        last = nc.tensor.matmul(out[:, lo:lo + CH], lhsT[0:rows_, t * P:(t + 1) * P],
                                                rhs[0:rows_, lo:lo + CH], start=True, stop=True)
                    last.then_inc(sem, 1)

                def weigh(it, j, s, i):
                    h, k, r = head(it, j, LP), (j - LP) % PER, (j - LP) % 4
                    t = 2 * k + i
                    if i == 0:
                        pe.wait_ge(tau_exp, 2 * s + 2)
                        pe.wait_ge(sig_done, s + 1)
                    if t == 0:
                        pe.wait_ge(vh_ready, h + 1)
                        if some(h):
                            pe.wait_ge(o_sb, h)
                    for q, (wts, half) in enumerate(((pt[r], 0), (pt[r], 1), (sg[r], 0), (sg[r], 1))):
                        last = nc.tensor.matmul(po[32 * q:32 * q + 32, :], Vh[:, ((j - LP) // PER) % 2, t, :],
                                                wts[:, i, half * CH:(half + 1) * CH],
                                                start=(t == 0), stop=(t == TT - 1))
                    if i:
                        last.then_inc(pv_done, 1)

                def body(it, j):
                    sm, ss, st, sp_ = at(it, j, 0), at(it, j, LS), at(it, j, LT), at(it, j, LP)
                    rm, rs, rt = (((j - lag) // PER) % RING for lag in (0, LS, LT))
                    if sm is not None and j % PER == 0:
                        pe.wait_ge(stack_in[rm], HEAD_LOADS * (it + 1))
                    if st is not None and (j - LT) % PER == 0:
                        pe.wait_ge(rows_in[rt], 16 * (it + (j - LT) // PER // RING + 1))
                    for i in range(2):
                        if sm is not None:
                            if some(2 * sm + i):
                                pe.wait_ge(max_red, 2 * sm + i)
                            scores(pm, Q[rm], K[rm], 2 * (j % PER) + i, 96, max_mm)
                        if ss is not None:
                            if some(2 * ss + i):
                                pe.wait_ge(abs_done, 2 * ss + i)
                            scores(pa, K[rs], Q[rs], 2 * ((j - LS) % PER) + i, 96, abs_mm)
                        if i and sp_ is not None:
                            weigh(it, j, sp_, 0)
                        if st is not None:
                            if some(2 * st + i):
                                pe.wait_ge(tau_exp, 2 * st + i)
                            scores(pb, K[rt], Q[rt], 2 * ((j - LT) % PER) + i, P, tau_mm)
                        if i and sp_ is not None:
                            weigh(it, j, sp_, 1)
                    if j % PER == 0 and at(it, j, 1) is not None:
                        h = head(it, j, 1)
                        pe.wait_ge(parts_ready, h + 1)
                        if some(h, 2):
                            pe.wait_ge(f_done, h - 1)
                        nc.tensor.transpose(ptr[:].bitcast(BF16)[0:SPLIT * TT, 0:P],
                                            neg3[:].rearrange("p s t -> p (s t)"), identb[:])\
                            .then_inc(rows_turned, 1)
                    if (j - LP - 1) % PER == PER - 1 and at(it, j, LP + 1) is not None:
                        h = head(it, j, LP + 1)
                        pe.wait_ge(o_sb, h + 1)
                        if isinstance(h, int) and h + 3 > HEADS:
                            pe.wait_ge(rows_sb, HEADS)
                            pe.wait_ge(f_done, h)
                        else:
                            pe.wait_ge(rows_sb, h + 2)
                        for c in range(4):
                            last = nc.tensor.transpose(ptr[:, c * P:(c + 1) * P], osb[:, c * P:(c + 1) * P],
                                                       ident[:])
                        last.then_inc(o_turned, 1)

                slots(pe, body)

            @block.scalar
            def _(act):
                nc.scalar.preload_act_table_set("natural_log_exp_and_others")

                def body(it, j):
                    st, se, so = at(it, j, LT), at(it, j, LE), at(it, j, LP + 1)
                    for i in range(2):
                        if st is not None:
                            act.wait_ge(tau_mm, 2 * st + i + 1)
                            if i == 0 and some(st, 4):
                                act.wait_ge(pv_done, st - 3)
                            nc.scalar.activation(pt[(j - LT) % 4][:, i, :], pb[:], ACT.Exp, scale=SC)\
                                .then_inc(tau_exp, 1)
                        if i == 0 and so is not None and (j - LP - 1) % PER == PER - 1:
                            h = head(it, j, LP + 1)
                            act.wait_ge(pv_done, PER * h + PER)
                            if some(h):
                                act.wait_ge(o_turned, h)
                            nc.scalar.activation(osb[:], po[:], ACT.Copy).then_inc(o_sb, 1)
                        if se is not None:
                            buf = sg[(j - LE) % 4]
                            if i == 0:
                                h = head(it, j, LE)
                                act.wait_ge(sq_pool, se + 1)
                                act.wait_ge(sq_dve, se + 1)
                                act.wait_ge(par_ready, h + 1)
                                nc.scalar.activation(buf[:], buf[:], ACT.Ln,
                                                     bias=parh[:, ((j - LE) // PER) % RING, 1:2]).then_inc(ln_done, 1)
                            else:
                                act.wait_ge(ln_done, se + 1)
                                nc.scalar.activation(buf[:], buf[:], ACT.Exp, scale=-1.0).then_inc(sig_done, 1)

                slots(act, body)

            @block.vector
            def _(dve):
                clear_stacks(nc.vector, Qs, Ks, cleared)
                nc.vector.tensor_copy(identb[:], ident[:]).then_inc(identb_ready, 1)

                def part(it, j, n):
                    if j % PER or at(it, j, 1) is None:
                        return
                    h, top = head(it, j, 1), mx[:, ((j - 1) // PER) % 2, :]
                    if n == 0:
                        dve.wait_ge(max_red, TT * h + TT)
                        if some(h):
                            dve.wait_ge(rows_turned, h)
                        nc.vector.tensor_scalar(neg3[:, 0, :], top, -1.0, None, ALU.mult).then_inc(chain, 1)
                    else:
                        dve.wait_ge(chain, 4 * h + n)
                    if n == 1:
                        nc.vector.scalar_tensor_tensor(rem[:], top, -1.0, neg3[:, 0, :], ALU.mult, ALU.subtract)\
                            .then_inc(chain, 1)
                    if n == 2:
                        nc.vector.tensor_copy(neg3[:, 1, :], rem[:]).then_inc(chain, 1)
                    if n == 3:
                        nc.vector.tensor_tensor(rem[:], rem[:], neg3[:, 1, :], ALU.subtract).then_inc(chain, 1)
                    if n == 4:
                        nc.vector.tensor_copy(neg3[:, 2, :], rem[:]).then_inc(parts_ready, 1)

                def output(it, j, n):
                    if (j - LP - 2) % PER != PER - 1 or at(it, j, LP + 2) is None:
                        return
                    h = head(it, j, LP + 2)
                    o = ptr[:].rearrange("p (c q k) -> p c q k", c=4, q=4)
                    if n == 0:
                        dve.wait_ge(o_turned, h + 1)
                        if some(h):
                            dve.wait_ge(weighed, h)
                        nc.vector.reciprocal(rz[:], o[:, :, :, DH]).then_inc(rz_done, 1)
                    if n == 1:
                        dve.wait_ge(rz_done, h + 1)
                        if some(h):
                            dve.wait_ge(f_done, h)
                        nc.vector.tensor_tensor(fw[:], o[:, :, :, 0:DH], rz[:].unsqueeze(3).broadcast_to([P, 4, 4, DH]),
                                                ALU.mult).then_inc(weighed, 1)
                    if n == 2:
                        dve.wait_ge(weighed, h + 1)
                        nc.vector.tensor_tensor(F[:, :, h, :].rearrange("p (s c) d -> p s c d", s=2),
                                                fw[:, :, 0:2, :].rearrange("p c s d -> p s c d"),
                                                fw[:, :, 2:4, :].rearrange("p c s d -> p s c d"), ALU.add)\
                            .then_inc(f_done, 1)

                def body(it, j):
                    sm, ss = at(it, j, 0), at(it, j, LS)
                    part(it, j, 0)
                    for i in range(2):
                        if sm is not None:
                            t = 2 * (j % PER) + i
                            dve.wait_ge(max_mm, 2 * sm + i + 1)
                            nc.vector.tensor_reduce(mx[:, (j // PER) % 2, t:t + 1], pm[:], AX.X, ALU.max)\
                                .then_inc(max_red, 1)
                        part(it, j, 2 * i + 1)
                        output(it, j, 2 * i)
                        if ss is not None:
                            dve.wait_ge(abs_mm, 2 * ss + i + 1)
                            if i == 0 and some(ss, 4):
                                dve.wait_ge(pv_done, ss - 3)
                            nc.vector.tensor_scalar(sg[(j - LS) % 4][:, i, :].bitcast(I32), pa[:].bitcast(I32),
                                                    SIGN_OFF, None, ALU.bitwise_and).then_inc(abs_done, 1)
                        part(it, j, 2 * i + 2)
                        output(it, j, 2 * i + 1)
                        if i == 0 and j % PER == 1 and at(it, j, 2) is not None:
                            h, r = head(it, j, 2), ((j - 2) // PER - 1) % RING
                            dve.wait_ge(rows_turned, h + 1)
                            if some(h):
                                dve.wait_ge(rows_in[r], 16 * (it + ((j - 2) // PER - 1) // RING + 1))
                            nc.vector.tensor_copy(rows[:], ptr[:].bitcast(BF16)[0:SPLIT * TT, 0:P])\
                                .then_inc(rows_sb, 1)
                    if ss is not None:
                        h, buf = head(it, j, LS), sg[(j - LS) % 4]
                        dve.wait_ge(abs_done, 2 * ss + 2)
                        dve.wait_ge(par_ready, h + 1)
                        nc.vector.scalar_tensor_tensor(buf[:, :, CUT:T], buf[:, :, CUT:T],
                                                       parh[:, ((j - LS) // PER) % RING, 0:1], buf[:, :, CUT:T],
                                                       ALU.add, ALU.mult).then_inc(sq_dve, 1)

                slots(dve, body)
        m.clear_sems()


def load_sharpness(nc, tag, par, beta, t):
    with ExitStack() as ctx:
        m = Mem(nc, ctx, tag)
        bt = m.sb("bt", [P, 2, H])
        one = m.sb("one", [P, 2, H])
        loaded, chain = m.sem("loaded"), m.sem("chain")
        with nc.Block() as block:

            @block.sync
            def _(sp):
                sp.dma_start(bt[:, 0, :], beta.unsqueeze(0).broadcast_to([P, H])).then_inc(loaded, 16)
                sp.dma_start(bt[:, 1, :], t.unsqueeze(0).broadcast_to([P, H])).then_inc(loaded, 16)

            @block.vector
            def _(dve):
                dve.wait_ge(loaded, 32)
                link = Chain(dve, chain)
                link(nc.vector.tensor_scalar(bt[:, 0, :], bt[:, 0, :], DH ** 0.5, None, ALU.mult))
                link(nc.vector.tensor_tensor(bt[:, 1, :], bt[:, 0, :], bt[:, 1, :], ALU.mult))
                link(nc.vector.tensor_tensor(one[:], bt[:], bt[:], ALU.mult))
                for b in range(B):
                    link(nc.vector.tensor_scalar(par[:, b * H:(b + 1) * H, 0], bt[:, 0, :], 2.0, None, ALU.mult))
                    link(nc.vector.tensor_tensor(par[:, b * H:(b + 1) * H, 1], one[:, 0, :], one[:, 1, :], ALU.add))
        m.clear_sems()


def program(nc, x, out, w, stop=99):
    x_v = x.rearrange("b (t p) d -> p (b t) d", p=P)
    out_v = out.rearrange("b (t p) d -> p (b t) d", p=P)
    qd = nc.dram_tensor("q_parts", (SPLIT, HEADS, DH, T), BF16, kind="Internal").ap()
    kd = nc.dram_tensor("k_parts", (SPLIT, HEADS, DH, T), BF16, kind="Internal").ap()
    with ExitStack() as ctx:
        m = Mem(nc, ctx, "all")
        X = m.sb("X", [P, NT, D])
        XNT = m.sb("XNT", [P, TOK])
        V = m.sb("V", [P, HEADS, TT, DH + 1])
        ident = m.sb("ident", [P, P])
        rank0 = m.sb("rank0", [P, E0])
        rank1 = m.sb("rank1", [P, E1])
        par = m.sb("par", [P, HEADS, 2])
        loaded, saved = m.sem("loaded"), m.sem("saved")
        layer = {n: {k[3:]: v for k, v in w.items() if k.startswith(n)} for n in ("f0_", "a0_", "a1_", "f1_")}
        f0_in, a0_in, f1_in, a1_in = (m.sem(n) for n in ("f0_in", "a0_in", "f1_in", "a1_in"))
        f0, load_f0 = load_ffn0(nc, m, layer["f0_"], f0_in)
        a0, load_a0 = load_attention(nc, m, layer["a0_"], a0_in, False)
        f1, load_f1 = load_ffn1(nc, m, layer["f1_"], f1_in)
        a1, load_a1 = load_attention(nc, m, layer["a1_"], a1_in, True)
        with nc.Block() as block:

            @block.sync
            def _(sp):
                sp.dma_start(X[:], x_v).then_inc(loaded, 16)
                sp.dma_start(ident[:], w["ident"]).then_inc(loaded, 16)
                sp.dma_start(rank0[:], w["rank"][:, E1 - E0:]).then_inc(loaded, 16)
                sp.dma_start(rank1[:], w["rank"]).then_inc(loaded, 16)
                for load in (load_f0, load_a0, load_f1, load_a1):
                    load(sp)
                sp.wait_ge(loaded, 64)

        F = XNT[:].rearrange("p (t h d) -> p t h d", h=HEADS, t=TT)
        tiles = [XNT[:, (k % TT) * HEADS * DH + (k // TT) * D:][:, 0:D] for k in range(NT)]

        steps = [
            lambda: ln_transposed(nc, "n1", X, XNT, ident),
            lambda: ffn0(nc, "f1", X, XNT, rank0, f0, f0_in),
            lambda: ln_transposed(nc, "n2", X, XNT, ident),
            lambda: project(nc, "p2", XNT, V, qd, kd, a0, a0_in, False, 1.0),
            lambda: attend_causal(nc, "a2", V, F, qd, kd, ident, (w["mask_nm"], w["mask_mn"])),
            lambda: project_out(nc, "o2", X, tiles, ident, a0, a0_in, False),
            lambda: ln_transposed(nc, "n3", X, XNT, ident),
            lambda: ffn0(nc, "f3", X, XNT, rank0, f0, f0_in),
            lambda: ln_transposed(nc, "n4", X, XNT, ident),
            lambda: ffn1(nc, "f4", X, XNT, ident, rank1, f1, f1_in),
            lambda: ln_transposed(nc, "n5", X, XNT, ident, add_to_x=True),
            lambda: load_sharpness(nc, "s5", par, layer["a1_"]["beta"], layer["a1_"]["t"]),
            lambda: project(nc, "p5", XNT, V, qd, kd, a1, a1_in, True, 2.0),
            lambda: attend_both(nc, "a5", V, F, par, qd, kd, ident),
            lambda: project_out(nc, "o5", X, tiles, ident, a1, a1_in, True),
            lambda: ln_transposed(nc, "n6", X, XNT, ident),
            lambda: ffn1(nc, "f6", X, XNT, ident, rank1, f1, f1_in),
        ]
        for step in (steps[:stop] if isinstance(stop, int) else [steps[i] for i in stop]):
            step()
        with nc.Block() as block:

            @block.sync
            def _(sp):
                sp.dma_start(out_v, X[:]).then_inc(saved, 16)
                sp.wait_ge(saved, 16)


def kernel(**inputs):
    import numpy as _np
    import ml_dtypes as _ml
    import concourse.bacc as _bacc
    from concourse import mybir as _mybir
    from concourse.bass_utils import run_bass_kernel_spmd as _run

    i = {k: _np.asarray(v) for k, v in inputs.items()}
    c = _np.ascontiguousarray
    arrays = {"x": c(i["L0_attn_x"])}
    for n in ("Wr", "br", "We1", "We2", "be2"):
        arrays["f0_" + n] = c(i["L0_ffn_" + n])
    arrays["f0_be1T"] = c(i["L0_ffn_be1"].reshape(E0 * FT0, P).T)
    for n in ("Wq", "Wk", "Wv", "Wo"):
        arrays[f"a0_{n}T"] = c(i["L0_attn_" + n].T)
        arrays[f"a1_{n}T"] = c(i["L1_attn_" + n].T)
    for n in ("bq", "bk", "bv", "bo", "beta", "t", "ln_w", "ln_b"):
        arrays["a1_" + n] = c(i["L1_attn_" + n])
    arrays["f1_w_gate"] = c(i["L1_ffn_w_gate"])
    arrays["f1_w_gP"] = c(i["L1_ffn_w_g"].transpose(1, 0, 2).reshape(D, E1 * M1))
    arrays["f1_w_uP"] = c(i["L1_ffn_w_u"].transpose(1, 0, 2).reshape(D, E1 * M1))
    arrays["f1_w_dP"] = c(i["L1_ffn_w_d"].reshape(E1 * M1, D))
    sel = _np.zeros((96, E1 * M1), _np.float32)
    for part in range(SPLIT):
        sel[32 * part + _np.arange(E1 * M1) // M1, _np.arange(E1 * M1)] = 1.0
    arrays["f1_sel"] = sel.astype(_ml.bfloat16)
    arrays["ident"] = _np.eye(P, dtype=_np.float32)
    arrays["rank"] = _np.tile(_np.arange(E1, 0, -1, dtype=_np.float32), (P, 1))
    above = _np.triu(_np.full((P, P), -1e30, _np.float32), 1)
    arrays["mask_nm"] = above.astype(_ml.bfloat16)
    arrays["mask_mn"] = c(above.T).astype(_ml.bfloat16)

    nc = _bacc.Bacc("TRN2", target_bir_lowering=False, num_devices=1)
    named, aps = {}, {}
    for n, a in arrays.items():
        named[f"in_{n}_dram"] = a
        aps[n] = nc.dram_tensor(f"in_{n}_dram", a.shape, _mybir.dt.from_np(a.dtype), kind="ExternalInput").ap()
    out = nc.dram_tensor("out_0_dram", (B, T, D), _mybir.dt.float32, kind="ExternalOutput").ap()
    program(nc, aps.pop("x"), out, aps)
    r = _run(nc, [named], core_ids=[0])
    return r.results[0]["out_0_dram"]
```

```python
from contextlib import ExitStack

import numpy as np

import concourse.bass as bass
from concourse import mybir

F32 = mybir.dt.float32
BF16 = mybir.dt.bfloat16
I32 = mybir.dt.int32
ALU = mybir.AluOpType
ACT = mybir.ActivationFunctionType
AX = mybir.AxisListType

P = 128
B, T, D = 4, 1024, 128
H, DH = 16, 8
TOK = B * T
NT = TOK // P
TT = T // P
HEADS = B * H
CH = 512
NCH = TOK // CH
LN_EPS = 1e-5
E0, F0 = 4, 512
FT0 = F0 // P
E1, M1 = 8, 176
KT1 = E1 * M1 // P
SPLIT = 3
PROD = SPLIT * SPLIT * DH
ONES_ROW = 96
RING = 4
SIGN_OFF = 0x7FFFFFFF


class Chain:

    def __init__(self, eng, sem, base=0):
        self.eng, self.sem, self.n = eng, sem, base

    def __call__(self, ins):
        ins.then_inc(self.sem, 1)
        self.n = self.n + 1
        self.eng.wait_ge(self.sem, self.n)


class Mem:
    def __init__(self, nc, ctx, tag):
        self.nc, self.ctx, self.tag, self.sems = nc, ctx, tag, []

    def sb(self, name, shape, dt=F32):
        return self.ctx.enter_context(self.nc.sbuf_tensor(f"{self.tag}_{name}", shape, dt))

    def ps(self, name, shape, dt=F32):
        return self.ctx.enter_context(self.nc.psum_tensor(f"{self.tag}_{name}", shape, dt))

    def sem(self, name):
        self.sems.append(self.ctx.enter_context(self.nc.semaphore(f"{self.tag}_{name}")))
        return self.sems[-1]

    def clear_sems(self):
        nums = sorted(s.num for s in self.sems)
        starts = [n for n in nums if n - 1 not in nums]
        ends = [n + 1 for n in nums if n + 1 not in nums]
        with self.nc.Block() as block:

            @block.gpsimd
            def _(pool):
                for a, b in zip(starts, ends):
                    self.nc.gpsimd.sem_clear(range(a, b))


def ln_transposed(nc, tag, X, XNT, ident, add_to_x=False):
    G = 4
    GT = NT // G
    with ExitStack() as ctx:
        m = Mem(nc, ctx, tag)
        stats = m.sb("stats", [P, NT, 6])
        mv = m.sb("mv", [P, NT, 2])
        rs = m.sb("rs", [P, NT])
        t1 = m.sb("t1", [P, NT])
        rstd = m.sb("rstd", [P, NT])
        ve = m.sb("ve", [P, NT])
        xn = m.sb("xn", [P, NT, P])
        pt = m.ps("pt", [P, 4, CH])
        stats_done, mv_done, ve_ready, ln_var, rs_ready = (m.sem(x) for x in ("stats", "mvs", "ve", "lnv", "rsr"))
        dve_chain, xn_ready, turned, evacuated = (m.sem(x) for x in ("chain", "xnr", "turned", "evac"))
        x_added = m.sem("xadd")
        with nc.Block() as block:

            @block.vector
            def _(dve):

                def statistics(g):
                    for k in range(g * GT, (g + 1) * GT):
                        nc.vector.bn_stats(stats[:, k, :], X[:, k, :]).then_inc(stats_done, 1)
                    for k in range(g * GT, (g + 1) * GT):
                        dve.wait_ge(stats_done, k + 1)
                        nc.vector.bn_aggr(mv[:, k, :], stats[:, k, :]).then_inc(mv_done, 1)
                    tiles = slice(g * GT, (g + 1) * GT)
                    dve.wait_ge(mv_done, (g + 1) * GT)
                    nc.vector.tensor_scalar(ve[:, tiles], mv[:, tiles, 1], LN_EPS, None, ALU.add).then_inc(ve_ready, 1)

                def normalise(g):
                    tiles = slice(g * GT, (g + 1) * GT)
                    dve.wait_ge(ve_ready, g + 1)
                    dve.wait_ge(rs_ready, g + 1)
                    link = Chain(dve, dve_chain, 4 * g)
                    link(nc.vector.tensor_tensor(t1[:, tiles], rs[:, tiles], rs[:, tiles], ALU.mult))
                    link(nc.vector.tensor_tensor(t1[:, tiles], t1[:, tiles], ve[:, tiles], ALU.mult))
                    link(nc.vector.tensor_scalar(t1[:, tiles], t1[:, tiles], -0.5, 1.5, ALU.mult, ALU.add))
                    link(nc.vector.tensor_tensor(rstd[:, tiles], rs[:, tiles], t1[:, tiles], ALU.mult))
                    for k in range(g * GT, (g + 1) * GT):
                        nc.vector.tensor_scalar(xn[:, k, :], X[:, k, :], mv[:, k, 0:1], rstd[:, k:k + 1],
                                                ALU.subtract, ALU.mult).then_inc(xn_ready, 1)

                statistics(0)
                for g in range(1, G):
                    statistics(g)
                    normalise(g - 1)
                normalise(G - 1)

            if add_to_x:

                @block.gpsimd
                def _(pool):
                    for k in range(NT):
                        pool.wait_ge(xn_ready, k + 1)
                        nc.gpsimd.tensor_tensor(X[:, k, :], X[:, k, :], xn[:, k, :], ALU.add).then_inc(x_added, 1)

            @block.scalar
            def _(act):
                nc.scalar.preload_act_table_set("natural_log_exp_and_others")

                def evacuate(c):
                    act.wait_ge(turned, c + 1)
                    nc.scalar.activation(XNT[:, c * CH:(c + 1) * CH], pt[:, c % 4, :], ACT.Copy).then_inc(evacuated, 1)

                for g in range(G):
                    tiles = slice(g * GT, (g + 1) * GT)
                    act.wait_ge(ve_ready, g + 1)
                    nc.scalar.activation(rs[:, tiles], ve[:, tiles], ACT.Ln).then_inc(ln_var, 1)
                    act.wait_ge(ln_var, g + 1)
                    nc.scalar.activation(rs[:, tiles], rs[:, tiles], ACT.Exp, scale=-0.5).then_inc(rs_ready, 1)
                    if g >= 2:
                        for c in range((g - 2) * NCH // G, (g - 1) * NCH // G):
                            evacuate(c)
                for c in range((G - 2) * NCH // G, NCH):
                    evacuate(c)

            @block.tensor
            def _(pe):
                for c in range(NCH):
                    if c >= 4:
                        pe.wait_ge(evacuated, c - 3)
                    for q in range(4):
                        k = 4 * c + q
                        pe.wait_ge(xn_ready, k + 1)
                        last = nc.tensor.transpose(pt[:, c % 4, q * P:(q + 1) * P], xn[:, k, :], ident[:])
                    last.then_inc(turned, 1)
        m.clear_sems()


def first_argmax(link, nc, onehot, score, top, pref, eq, rank, n):
    link(nc.vector.tensor_reduce(top[:], score[:], AX.X, ALU.max))
    link(nc.vector.tensor_tensor(eq[:], score[:], top[:].unsqueeze(2).broadcast_to([P, NT, n]), ALU.is_equal))
    link(nc.vector.tensor_tensor(pref[:], eq[:], rank[:].unsqueeze(1).broadcast_to([P, NT, n]), ALU.mult))
    link(nc.vector.tensor_reduce(eq[:, :, 0], pref[:], AX.X, ALU.max))
    link(nc.vector.tensor_tensor(onehot[:], pref[:], eq[:, :, 0:1].broadcast_to([P, NT, n]), ALU.is_equal))


def load_ffn0(nc, m, w, sem):
    w1 = m.sb("w1", [P, E0, F0])
    w2 = m.sb("w2", [P, E0 * FT0, D])
    b1 = m.sb("b1", [P, E0 * FT0])
    b2 = m.sb("b2", [P, E0, D])
    wr = m.sb("wr", [P, E0])
    br = m.sb("br", [P, E0])

    def load(eng):
        eng.dma_start(wr[:], w["Wr"]).then_inc(sem, 16)
        eng.dma_start(br[:], w["br"].unsqueeze(0).broadcast_to([P, E0])).then_inc(sem, 16)
        eng.dma_start(w1[:], w["We1"].rearrange("e h f -> h e f")).then_inc(sem, 16)
        eng.dma_start(b1[:], w["be1T"]).then_inc(sem, 16)
        eng.dma_start(b2[:], w["be2"].unsqueeze(0).broadcast_to([P, E0, D])).then_inc(sem, 16)
        eng.dma_start(w2[:], w["We2"].rearrange("e (j p) d -> p (e j) d", p=P)).then_inc(sem, 16)

    return (w1, w2, b1, b2, wr, br), load


FFN0_LOADS = 16 * 6


def ffn0(nc, tag, X, XNT, rank, w, weights_in, beside=None):
    with ExitStack() as ctx:
        m = Mem(nc, ctx, tag)
        score = m.sb("score", [P, NT, E0])
        top = m.sb("top", [P, NT])
        eq = m.sb("eq", [P, NT, E0])
        pref = m.sb("pref", [P, NT, E0])
        mask = m.sb("mask", [P, NT, E0])
        hid = m.sb("hid", [P, 2, FT0, CH])
        psr = m.ps("psr", [P, NT, E0])
        psh = m.ps("psh", [P, 4, CH])
        psy = m.ps("psy", [P, 2, 4, D])
        routed, chain, biased = (m.sem(x) for x in ("routed", "chain", "biased"))
        w1, w2, b1, b2, wr, br = w
        h_done, relu_done, y_done, added = (m.sem(x) for x in ("h", "relu", "y", "added"))
        with nc.Block() as block:

            @block.gpsimd
            def _(pool):
                if beside:
                    beside(pool)

            @block.tensor
            def _(pe):
                pe.wait_ge(weights_in, FFN0_LOADS)
                for k in range(NT):
                    last = nc.tensor.matmul(psr[:, k, :], XNT[:, k * P:(k + 1) * P], wr[:], start=True, stop=True)
                last.then_inc(routed, 1)

                def hidden(c, e):
                    for j in range(FT0):
                        if e or not isinstance(c, int):
                            pe.wait_ge(relu_done, FT0 * (E0 * c + e - 1) + j + 1)
                        nc.tensor.matmul(psh[:, j, :], w1[:, e, j * P:(j + 1) * P], XNT[:, bass.ds(c * CH, CH)],
                                         start=True, stop=True).then_inc(h_done, 1)

                def output(c, e):
                    s = E0 * c + e
                    pe.wait_ge(relu_done, FT0 * s + FT0)
                    if e >= 2:
                        pe.wait_ge(added, 4 * (s - 1))
                    elif not isinstance(c, int):
                        pe.wait_ge(added, 4 * (s - 1))
                    for q in range(4):
                        for j in range(FT0):
                            last = nc.tensor.matmul(psy[:, e % 2, q, :], hid[:, e % 2, j, q * P:(q + 1) * P],
                                                    w2[:, e * FT0 + j, :], start=(j == 0), stop=(j == FT0 - 1))
                    last.then_inc(y_done, 1)

                def chunk(c):
                    hidden(c, 0)
                    for e in range(1, E0):
                        hidden(c, e)
                        output(c, e - 1)
                    output(c, E0 - 1)

                chunk(0)
                with pe.Fori(1, NCH) as c:
                    chunk(c)

            @block.scalar
            def _(act):
                act.wait_ge(weights_in, FFN0_LOADS)

                def relu(c, e, j):
                    s = E0 * c + e
                    act.wait_ge(h_done, FT0 * s + j + 1)
                    if e >= 2 or not isinstance(c, int):
                        act.wait_ge(y_done, s - 1)
                    nc.scalar.activation(hid[:, e % 2, j, :], psh[:, j, :], ACT.Relu,
                                         bias=b1[:, e * FT0 + j:e * FT0 + j + 1]).then_inc(relu_done, 1)

                for e in range(E0):
                    for j in range(FT0):
                        relu(0, e, j)
                with act.Fori(1, NCH) as c:
                    for e in range(E0):
                        for j in range(FT0):
                            relu(c, e, j)

            @block.vector
            def _(dve):
                dve.wait_ge(weights_in, FFN0_LOADS)
                dve.wait_ge(routed, 1)
                link = Chain(dve, chain)
                link(nc.vector.tensor_tensor(score[:], psr[:], br[:].unsqueeze(1).broadcast_to([P, NT, E0]), ALU.add))
                first_argmax(link, nc, mask, score, top, pref, eq, rank, E0)
                link(nc.vector.tensor_scalar(mask[:], mask[:], 0.5, None, ALU.mult))

                def bias(c):
                    for e in range(E0):
                        for q in range(4):
                            if e:
                                dve.wait_ge(biased, 4 * (E0 * c + e - 1) + q + 1)
                            nc.vector.scalar_tensor_tensor(X[:, 4 * c + q, :], b2[:, e, :], mask[:, 4 * c + q, e:e + 1],
                                                           X[:, 4 * c + q, :], ALU.mult, ALU.add).then_inc(biased, 1)

                def add(c, e):
                    dve.wait_ge(y_done, E0 * c + e + 1)
                    for q in range(4):
                        if e:
                            dve.wait_ge(added, 4 * (E0 * c + e - 1) + q + 1)
                        else:
                            dve.wait_ge(biased, 4 * (E0 * c + E0 - 1) + q + 1)
                        nc.vector.scalar_tensor_tensor(X[:, 4 * c + q, :], psy[:, e % 2, q, :],
                                                       mask[:, 4 * c + q, e:e + 1], X[:, 4 * c + q, :],
                                                       ALU.mult, ALU.add).then_inc(added, 1)

                with dve.Fori(0, NCH) as c:
                    bias(c)
                    for e in range(E0):
                        add(c, e)
        m.clear_sems()


def load_ffn1(nc, m, w, sem):
    wgate = m.sb("wgate", [P, E1])
    wg = m.sb("wg", [P, E1 * M1])
    wu = m.sb("wu", [P, E1 * M1])
    wd = m.sb("wd", [P, KT1, D])
    sel = m.sb("sel", [96, KT1, P], BF16)

    def load(eng):
        eng.dma_start(wgate[:], w["w_gate"]).then_inc(sem, 16)
        eng.dma_start(wg[:], w["w_gP"]).then_inc(sem, 16)
        eng.dma_start(wu[:], w["w_uP"]).then_inc(sem, 16)
        eng.dma_start(wd[:], w["w_dP"].rearrange("(k p) d -> p k d", p=P)).then_inc(sem, 16)
        eng.dma_start(sel[:], w["sel"].rearrange("r (k p) -> r k p", p=P)).then_inc(sem, 16)

    return (wgate, wg, wu, wd, sel), load


FFN1_LOADS = 16 * 5


def ffn1(nc, tag, X, XNT, ident, rank, w, weights_in):
    with ExitStack() as ctx:
        m = Mem(nc, ctx, tag)
        wgate, wg, wu, wd, sel = w
        score = m.sb("score", [P, NT, E1])
        rest = m.sb("rest", [P, NT, E1])
        top = m.sb("top", [P, NT])
        top2 = m.sb("top2", [P, NT])
        eq = m.sb("eq", [P, NT, E1])
        pref = m.sb("pref", [P, NT, E1])
        one1 = m.sb("one1", [P, NT, E1])
        one2 = m.sb("one2", [P, NT, E1])
        pr = m.sb("pr", [P, 4, NT])
        gate = m.sb("gate", [P, NT, E1])
        gate3 = m.sb("gate3", [P, NT, 96], BF16)
        gateT = m.sb("gateT", [96, TOK], BF16)
        identb = m.sb("identb", [P, P], BF16)
        sg = m.sb("sg", [P, 2, CH])
        su = m.sb("su", [P, 2, CH])
        hid = m.sb("hid", [P, KT1, CH])
        psg = m.ps("psg", [P, 2, CH])
        psu = m.ps("psu", [P, 2, CH])
        psm = m.ps("psm", [P, 2, CH])
        psy = m.ps("psy", [P, 2, 4, D])
        ident_ready, routed, chain, e2 = (m.sem(x) for x in ("identb", "routed", "chain", "e2"))
        cleared, gate_ready, turned, gate_out = (m.sem(x) for x in ("cleared", "gate", "turned", "gateout"))
        g_done, u_done, m_done, silu_done, su_done, hid_done, y_done, added = (
            m.sem(x) for x in ("gd", "ud", "md", "silu", "sud", "hidd", "yd", "added"))
        with nc.Block() as block:

            @block.gpsimd
            def _(pool):
                nc.gpsimd.memset(gate3[:], 0.0).then_inc(cleared, 1)

            @block.tensor
            def _(pe):
                pe.wait_ge(weights_in, FFN1_LOADS)
                pr_out = psg[:, 0, 0:NT * E1].rearrange("p (k e) -> p k e", e=E1)
                for k in range(NT):
                    last = nc.tensor.matmul(pr_out[:, k, :], XNT[:, k * P:(k + 1) * P], wgate[:],
                                            start=True, stop=True)
                last.then_inc(routed, 1)
                pe.wait_ge(gate_ready, 1)
                pe.wait_ge(ident_ready, 1)
                for c in range(NCH):
                    if c >= 2:
                        pe.wait_ge(gate_out, c - 1)
                    out = psm[:, c % 2, :].bitcast(BF16)
                    for q in range(4):
                        last = nc.tensor.transpose(out[0:96, q * P:(q + 1) * P], gate3[:, 4 * c + q, :], identb[:])
                    last.then_inc(turned, 1)
                pe.wait_ge(gate_out, NCH)

                def chunk(c, first):
                    for k in range(KT1):
                        s = KT1 * c + k
                        if k >= 2 or not first:
                            pe.wait_ge(silu_done, s - 1)
                            pe.wait_ge(su_done, s - 1)
                            pe.wait_ge(hid_done, s - 1)
                        b = (k % 2)
                        x = XNT[:, bass.ds(c * CH, CH)]
                        nc.tensor.matmul(psg[:, b, :], wg[:, k * P:(k + 1) * P], x, start=True, stop=True)\
                            .then_inc(g_done, 1)
                        nc.tensor.matmul(psu[:, b, :], wu[:, k * P:(k + 1) * P], x, start=True, stop=True)\
                            .then_inc(u_done, 1)
                        nc.tensor.matmul(psm[:, b, :], sel[:, k, :], gateT[:, bass.ds(c * CH, CH)],
                                         start=True, stop=True).then_inc(m_done, 1)

                def output(c, first):
                    pe.wait_ge(hid_done, KT1 * c + KT1)
                    if not first:
                        pe.wait_ge(added, 4 * c)
                    for q in range(4):
                        for k in range(KT1):
                            last = nc.tensor.matmul(psy[:, 0, q, :], hid[:, k, q * P:(q + 1) * P], wd[:, k, :],
                                                    start=(k == 0), stop=(k == KT1 - 1))
                    last.then_inc(y_done, 1)

                chunk(0, True)
                output(0, True)
                with pe.Fori(1, NCH) as c:
                    chunk(c, False)
                    output(c, False)

            @block.scalar
            def _(act):
                act.wait_ge(e2, 1)
                nc.scalar.activation(pr[:, 1, :], pr[:, 0, :], ACT.Exp).then_inc(e2, 1)
                for c in range(NCH):
                    act.wait_ge(turned, c + 1)
                    nc.scalar.activation(gateT[:, c * CH:(c + 1) * CH], psm[:, c % 2, :].bitcast(BF16)[0:96, 0:CH],
                                         ACT.Copy).then_inc(gate_out, 1)

                def silu(c, k, first):
                    s = KT1 * c + k
                    act.wait_ge(g_done, s + 1)
                    if k >= 2 or not first:
                        act.wait_ge(su_done, s - 1)
                    nc.scalar.activation(sg[:, k % 2, :], psg[:, k % 2, :], ACT.Silu).then_inc(silu_done, 1)

                for k in range(KT1):
                    silu(0, k, True)
                with act.Fori(1, NCH) as c:
                    for k in range(KT1):
                        silu(c, k, False)

            @block.vector
            def _(dve):
                nc.vector.tensor_copy(identb[:], ident[:]).then_inc(ident_ready, 1)
                dve.wait_ge(routed, 1)
                link = Chain(dve, chain)
                link(nc.vector.tensor_copy(score[:], psg[:, 0, 0:NT * E1].rearrange("p (k e) -> p k e", e=E1)))
                first_argmax(link, nc, one1, score, top, pref, eq, rank, E1)
                link(nc.vector.scalar_tensor_tensor(rest[:], one1[:], -3.0e38, score[:], ALU.mult, ALU.add))
                first_argmax(link, nc, one2, rest, top2, pref, eq, rank, E1)
                nc.vector.tensor_tensor(pr[:, 0, :], top2[:], top[:], ALU.subtract).then_inc(e2, 1)
                dve.wait_ge(e2, 2)
                link(nc.vector.tensor_scalar(pr[:, 0, :], pr[:, 1, :], 2.0, 2.0, ALU.mult, ALU.add))
                link(nc.vector.reciprocal(pr[:, 2, :], pr[:, 0, :]))
                link(nc.vector.tensor_tensor(pr[:, 3, :], pr[:, 2, :], pr[:, 1, :], ALU.mult))
                link(nc.vector.tensor_tensor(gate[:], one1[:], pr[:, 2, :].unsqueeze(2).broadcast_to([P, NT, E1]),
                                             ALU.mult))
                link(nc.vector.tensor_tensor(eq[:], one2[:], pr[:, 3, :].unsqueeze(2).broadcast_to([P, NT, E1]),
                                             ALU.mult))
                link(nc.vector.tensor_tensor(gate[:], gate[:], eq[:], ALU.add))
                dve.wait_ge(cleared, 1)
                link(nc.vector.tensor_copy(gate3[:, :, 0:E1], gate[:]))
                link(nc.vector.tensor_tensor(gate[:], gate[:], gate3[:, :, 0:E1], ALU.subtract))
                link(nc.vector.tensor_copy(gate3[:, :, 32:32 + E1], gate[:]))
                link(nc.vector.tensor_tensor(gate[:], gate[:], gate3[:, :, 32:32 + E1], ALU.subtract))
                nc.vector.tensor_copy(gate3[:, :, 64:64 + E1], gate[:]).then_inc(gate_ready, 1)

                def products(c, k, first):
                    s = KT1 * c + k
                    dve.wait_ge(silu_done, s + 1)
                    dve.wait_ge(u_done, s + 1)
                    if k >= 2 or not first:
                        dve.wait_ge(hid_done, s - 1)
                    nc.vector.tensor_tensor(su[:, k % 2, :], psu[:, k % 2, :], sg[:, k % 2, :], ALU.mult)\
                        .then_inc(su_done, 1)
                    dve.wait_ge(m_done, s + 1)
                    dve.wait_ge(su_done, s + 1)
                    if not first:
                        dve.wait_ge(y_done, c)
                    nc.vector.tensor_tensor(hid[:, k, :], psm[:, k % 2, :], su[:, k % 2, :], ALU.mult)\
                        .then_inc(hid_done, 1)

                def add(c):
                    dve.wait_ge(y_done, c + 1)
                    for q in range(4):
                        nc.vector.tensor_tensor(X[:, 4 * c + q, :], psy[:, 0, q, :], X[:, 4 * c + q, :], ALU.add)\
                            .then_inc(added, 1)

                for k in range(KT1):
                    products(0, k, True)
                add(0)
                with dve.Fori(1, NCH) as c:
                    for k in range(KT1):
                        products(c, k, False)
                    add(c)
        m.clear_sems()


def load_attention(nc, m, w, sem, biased):
    wqT, wkT, wvT, woT = (m.sb(f"w{n}T{int(biased)}", [P, D]) for n in "qkvo")
    bq, bv, bo, lw, lb = (m.sb(n, [P, 2 if n == "bq" else D]) if biased else None
                          for n in ("bq", "bv", "bo", "lw", "lb"))

    def load(eng):
        for dst, name in ((wqT, "WqT"), (wkT, "WkT"), (wvT, "WvT"), (woT, "WoT")):
            eng.dma_start(dst[:], w[name]).then_inc(sem, 16)
        if biased:
            eng.dma_start(bq[:, 0:1], w["bq"].unsqueeze(1)).then_inc(sem, 16)
            eng.dma_start(bq[:, 1:2], w["bk"].unsqueeze(1)).then_inc(sem, 16)
            for dst, name in ((bv, "bv"), (bo, "bo"), (lw, "ln_w"), (lb, "ln_b")):
                eng.dma_start(dst[:], w[name].unsqueeze(0).broadcast_to([P, D])).then_inc(sem, 16)

    return (wqT, wkT, wvT, bq, bv, woT, bo, lw, lb), load


ATTENTION_LOADS = (16 * 4, 16 * 10)


def project(nc, tag, XNT, V, qd, kd, w, weights_in, biased, ones):
    wqT, wkT, wvT, bq, bv = w[:5]
    with ExitStack() as ctx:
        m = Mem(nc, ctx, tag)
        parts = m.sb("parts", [P, 4, SPLIT, CH], BF16)
        rest = m.sb("rest", [P, 4, CH])
        psq = m.ps("psq", [P, 4, CH])
        psv = m.ps("psv", [P, 2, 4, D])
        q_done, hi_done, rest_done, mid_done, lo_done = (m.sem(x) for x in ("qd", "hi", "rest", "mid", "lo"))
        stored = [m.sem(f"stored{r}") for r in range(4)]
        v_done, v_out, ones_set = m.sem("vd"), m.sem("vo"), m.sem("ones")
        loads = ATTENTION_LOADS[biased]
        pieces = range(2 * NCH)
        with nc.Block() as block:

            @block.sync
            def _(sp):
                for i in pieces:
                    c, n = divmod(i, 2)
                    b, half = divmod(c, 2)
                    sp.wait_ge(lo_done, i + 1)
                    sp.dma_start((qd, kd)[n][:, b * H:(b + 1) * H, :, half * CH:(half + 1) * CH]
                                 .rearrange("s h d t -> (h d) s t"), parts[:, i % 4]).then_inc(stored[i % 4], 16)
                for r in range(4):
                    sp.wait_ge(stored[r], 16 * 2 * NCH // 4)

            @block.tensor
            def _(pe):
                pe.wait_ge(weights_in, loads)
                for c in range(NCH):
                    for n, wT in enumerate((wqT, wkT)):
                        i = 2 * c + n
                        if i >= 4:
                            pe.wait_ge(rest_done, i - 3)
                        nc.tensor.matmul(psq[:, i % 4, :], wT[:], XNT[:, c * CH:(c + 1) * CH], start=True, stop=True)\
                            .then_inc(q_done, 1)
                    if c >= 2:
                        pe.wait_ge(v_out, 4 * (c - 1))
                    for q in range(4):
                        last = nc.tensor.matmul(psv[:, c % 2, q, :], XNT[:, (4 * c + q) * P:(4 * c + q + 1) * P],
                                                wvT[:], start=True, stop=True)
                    last.then_inc(v_done, 1)

            @block.scalar
            def _(act):
                act.wait_ge(weights_in, loads)

                def high(i):
                    act.wait_ge(q_done, i + 1)
                    if i >= 4:
                        act.wait_ge(stored[i % 4], 16 * (i // 4))
                    nc.scalar.activation(parts[:, i % 4, 0, :], psq[:, i % 4, :], ACT.Identity,
                                         bias=bq[:, i % 2:i % 2 + 1] if biased else 0.0).then_inc(hi_done, 1)

                def middle(i):
                    act.wait_ge(rest_done, i + 1)
                    nc.scalar.activation(parts[:, i % 4, 1, :], rest[:, i % 4, :], ACT.Copy).then_inc(mid_done, 1)

                high(0)
                for i in pieces[1:]:
                    high(i)
                    middle(i - 1)
                middle(pieces[-1])

            @block.vector
            def _(dve):
                dve.wait_ge(weights_in, loads)
                nc.vector.memset(V[:, :, :, DH:DH + 1], ones).then_inc(ones_set, 1)

                def rest_of(i):
                    dve.wait_ge(hi_done, i + 1)
                    if i >= 4:
                        dve.wait_ge(lo_done, i - 3)
                    nc.vector.scalar_tensor_tensor(rest[:, i % 4, :], psq[:, i % 4, :],
                                                   bq[:, i % 2:i % 2 + 1] if biased else 0.0,
                                                   parts[:, i % 4, 0, :], ALU.add, ALU.subtract).then_inc(rest_done, 1)

                def low(i):
                    dve.wait_ge(mid_done, i + 1)
                    nc.vector.tensor_tensor(parts[:, i % 4, 2, :], rest[:, i % 4, :], parts[:, i % 4, 1, :],
                                            ALU.subtract).then_inc(lo_done, 1)

                def values(c):
                    dve.wait_ge(v_done, c + 1)
                    for q in range(4):
                        b, t = c // 2, (4 * c + q) % TT
                        out = V[:, b * H:(b + 1) * H, t, 0:DH]
                        src = psv[:, c % 2, q, :].rearrange("p (h d) -> p h d", d=DH)
                        if biased:
                            nc.vector.tensor_tensor(out, src, bv[:].rearrange("p (h d) -> p h d", d=DH), ALU.add)\
                                .then_inc(v_out, 1)
                        else:
                            nc.vector.tensor_copy(out, src).then_inc(v_out, 1)

                for c in range(NCH):
                    rest_of(2 * c)
                    if c:
                        low(2 * c - 1)
                    rest_of(2 * c + 1)
                    if c:
                        values(c - 1)
                    low(2 * c)
                low(2 * NCH - 1)
                values(NCH - 1)
        m.clear_sems()


def project_out(nc, tag, X, F, ident, w, weights_in, normed):
    G = 4
    GT = NT // G
    woT, bo, lw, lb = w[5:]
    with ExitStack() as ctx:
        m = Mem(nc, ctx, tag)
        fT = m.sb("fT", [P, 2, CH])
        y = m.sb("y", [P, NT, D])
        stats = m.sb("stats", [P, NT, 6])
        mv = m.sb("mv", [P, NT, 2])
        ve = m.sb("ve", [P, NT])
        rs = m.sb("rs", [P, NT])
        t1 = m.sb("t1", [P, NT])
        rstd = m.sb("rstd", [P, NT])
        ptr = m.ps("ptr", [P, 2, CH])
        psy = m.ps("psy", [P, 2, 4, D])
        turned, copied, y_done, added, chain, ve_ready, ln_var, rs_ready = (
            m.sem(x) for x in ("turned", "copied", "yd", "added", "chain", "ve", "lnv", "rsr"))
        stats_done, mv_done, centred, weighted, lb_added, x_added = (
            m.sem(x) for x in ("st", "ag", "centred", "weighted", "lbadded", "xadded"))
        loads = ATTENTION_LOADS[normed]
        with nc.Block() as block:

            @block.tensor
            def _(pe):
                pe.wait_ge(weights_in, loads)

                def turn(c):
                    if c >= 2:
                        pe.wait_ge(copied, c - 1)
                    for q in range(4):
                        last = nc.tensor.transpose(ptr[:, c % 2, q * P:(q + 1) * P], F[4 * c + q], ident[:])
                    last.then_inc(turned, 1)

                turn(0)
                for c in range(NCH):
                    if c + 1 < NCH:
                        turn(c + 1)
                    pe.wait_ge(copied, c + 1)
                    if c >= 2:
                        pe.wait_ge(added, c - 1)
                    for q in range(4):
                        last = nc.tensor.matmul(psy[:, c % 2, q, :], fT[:, c % 2, q * P:(q + 1) * P], woT[:],
                                                start=True, stop=True)
                    last.then_inc(y_done, 1)

            @block.scalar
            def _(act):

                def copy(c):
                    act.wait_ge(turned, c + 1)
                    if c >= 2:
                        act.wait_ge(y_done, c - 1)
                    nc.scalar.activation(fT[:, c % 2, :], ptr[:, c % 2, :], ACT.Copy).then_inc(copied, 1)

                for c in range(NCH):
                    copy(c)
                for g in range(G if normed else 0):
                    tiles = slice(g * GT, (g + 1) * GT)
                    act.wait_ge(ve_ready, g + 1)
                    nc.scalar.activation(rs[:, tiles], ve[:, tiles], ACT.Ln).then_inc(ln_var, 1)
                    act.wait_ge(ln_var, g + 1)
                    nc.scalar.activation(rs[:, tiles], rs[:, tiles], ACT.Exp, scale=-0.5).then_inc(rs_ready, 1)

            if normed:

                @block.gpsimd
                def _(pool):
                    pool.wait_ge(weights_in, loads)
                    for g in range(G):
                        tiles = slice(g * GT, (g + 1) * GT)
                        nc.gpsimd.tensor_tensor(X[:, tiles, :], X[:, tiles, :],
                                                lb[:].unsqueeze(1).broadcast_to([P, GT, D]), ALU.add)\
                            .then_inc(lb_added, 1)
                        pool.wait_ge(centred, (g + 1) * GT)
                        nc.gpsimd.tensor_tensor(y[:, tiles, :], y[:, tiles, :],
                                                lw[:].unsqueeze(1).broadcast_to([P, GT, D]), ALU.mult)\
                            .then_inc(weighted, 1)

            @block.vector
            def _(dve):
                dve.wait_ge(weights_in, loads)

                def add(c):
                    dve.wait_ge(y_done, c + 1)
                    tiles = slice(4 * c, 4 * c + 4)
                    if normed:
                        nc.vector.tensor_tensor(y[:, tiles, :], psy[:, c % 2], bo[:].unsqueeze(1).broadcast_to([P, 4, D]),
                                                ALU.add).then_inc(added, 1)
                    else:
                        nc.vector.tensor_tensor(X[:, tiles, :], psy[:, c % 2], X[:, tiles, :], ALU.add)\
                            .then_inc(added, 1)

                def statistics(g):
                    for k in range(g * GT, (g + 1) * GT):
                        dve.wait_ge(added, k // 4 + 1)
                        nc.vector.bn_stats(stats[:, k, :], y[:, k, :]).then_inc(stats_done, 1)
                    for k in range(g * GT, (g + 1) * GT):
                        dve.wait_ge(stats_done, k + 1)
                        nc.vector.bn_aggr(mv[:, k, :], stats[:, k, :]).then_inc(mv_done, 1)
                    tiles = slice(g * GT, (g + 1) * GT)
                    dve.wait_ge(mv_done, (g + 1) * GT)
                    nc.vector.tensor_scalar(ve[:, tiles], mv[:, tiles, 1], LN_EPS, None, ALU.add).then_inc(ve_ready, 1)

                def centre(g):
                    tiles = slice(g * GT, (g + 1) * GT)
                    dve.wait_ge(ve_ready, g + 1)
                    dve.wait_ge(rs_ready, g + 1)
                    link = Chain(dve, chain, 4 * g)
                    link(nc.vector.tensor_tensor(t1[:, tiles], rs[:, tiles], rs[:, tiles], ALU.mult))
                    link(nc.vector.tensor_tensor(t1[:, tiles], t1[:, tiles], ve[:, tiles], ALU.mult))
                    link(nc.vector.tensor_scalar(t1[:, tiles], t1[:, tiles], -0.5, 1.5, ALU.mult, ALU.add))
                    link(nc.vector.tensor_tensor(rstd[:, tiles], rs[:, tiles], t1[:, tiles], ALU.mult))
                    for k in range(g * GT, (g + 1) * GT):
                        nc.vector.tensor_scalar(y[:, k, :], y[:, k, :], mv[:, k, 0:1], rstd[:, k:k + 1],
                                                ALU.subtract, ALU.mult).then_inc(centred, 1)

                def add_normed(g):
                    tiles = slice(g * GT, (g + 1) * GT)
                    dve.wait_ge(lb_added, g + 1)
                    dve.wait_ge(weighted, g + 1)
                    nc.vector.tensor_tensor(X[:, tiles, :], X[:, tiles, :], y[:, tiles, :], ALU.add)\
                        .then_inc(x_added, 1)

                if not normed:
                    for c in range(NCH):
                        add(c)
                    return
                for g in range(G):
                    for c in range(g * GT // 4, (g + 1) * GT // 4):
                        add(c)
                    statistics(g)
                    if g:
                        centre(g - 1)
                    if g > 1:
                        add_normed(g - 2)
                centre(G - 1)
                add_normed(G - 2)
                add_normed(G - 1)
        m.clear_sems()


def load_stacks(eng, Q, K, qd, kd, g, sem):
    for i in range(SPLIT):
        rows = slice(i * SPLIT * DH, (i + 1) * SPLIT * DH)
        eng.dma_start(Q[rows, :], qd[:, g]).then_inc(sem, 16)
        eng.dma_start(K[rows, :], kd[i, g].unsqueeze(0).broadcast_to([SPLIT, DH, T])).then_inc(sem, 16)


STACK_DMAS = 2 * SPLIT


def clear_stacks(eng, Qs, Ks, sem):
    eng.memset(Qs[64:P], 0.0).then_inc(sem, 1)
    eng.memset(Ks[64:P], 0.0).then_inc(sem, 1)
    eng.wait_ge(sem, 2)
    eng.memset(Ks[ONES_ROW:P], 1.0).then_inc(sem, 1)


CLEARS = 3


def attend_causal(nc, tag, V, F, qd, kd, ident, stacks, cleared, masks):
    SLOTS = HEADS // 2
    UNROLL = RING
    LT = 2
    SC = DH ** -0.5
    MAXIMA = [(u, t, half) for u in range(2) for t in range(TT) for half in range(2) if half * CH < (t + 1) * P]
    WEIGHTS = [(u, t, half) for t in range(TT) for u in range(2) for half in range(2) if t * P < (half + 1) * CH]
    NP = len(MAXIMA)
    done = [1 + max(y for y, (_, t, _) in enumerate(WEIGHTS) if t == k) for k in range(TT)]
    with ExitStack() as ctx:
        m = Mem(nc, ctx, tag)
        Q, K = ([stack[:, r, :] for r in range(2 * RING)] for stack in stacks)
        mask_nm = m.sb("mask_nm", [P, P], BF16)
        mask_mn = m.sb("mask_mn", [P, P], BF16)
        identb = m.sb("identb", [P, P], BF16)
        Vh = m.sb("Vh", [P, 2, 2, TT, 32])
        mx = m.sb("mx", [P, 2, 2, 2, TT])
        rem = m.sb("rem", [P, 2, TT])
        neg = m.sb("neg", [P, P], BF16)
        neg3 = neg[:, 0:2 * SPLIT * TT].rearrange("p (u s t) -> p u s t", u=2, s=SPLIT)
        rows = m.sb("rows", [2 * SPLIT * TT, P], BF16)
        pt = m.sb("pt", [P, 2, 2, T])
        osb = m.sb("osb", [P, CH])
        rz = m.sb("rz", [P, 4, 4])
        pm = m.ps("pm", [P, 3, CH])
        pb = m.ps("pb", [P, 3, CH])
        po = m.ps("po", [P, CH])
        ptr = m.ps("ptr", [P, CH])
        loaded, identb_ready, vh_cleared, neg_cleared = (
            m.sem(x) for x in ("loaded", "identb", "vhc", "negc"))
        stack_in = [m.sem(f"stack{r}") for r in range(RING)]
        rows_in = [m.sem(f"rowsin{r}") for r in range(RING)]
        max_mm, max_red, parts_ready, rows_turned, rows_sb, chain = (
            m.sem(x) for x in ("maxmm", "maxred", "parts", "rturned", "rsb", "chain"))
        tau_exp = [m.sem(f"tauexp{r}") for r in range(3)]
        tau_mm, vh_ready, pv_done, o_sb, o_turned, f_done, rz_done = (
            m.sem(x) for x in ("taumm", "vh", "pv", "osb", "oturned", "fd", "rz"))
        PAIR_LOADS = 16 * 2 * STACK_DMAS

        def at(it, j, lag):
            s = UNROLL * it + (j - lag)
            return None if isinstance(s, int) and not 0 <= s < SLOTS else s

        def wait_from(eng, sem, value):
            if not (isinstance(value, int) and value <= 0):
                eng.wait_ge(sem, value)

        def slots(eng, body):
            for j in range(UNROLL):
                body(0, j)
            with eng.Fori(1, SLOTS // UNROLL) as it:
                for j in range(UNROLL):
                    body(it, j)
            for j in range(LT + 1):
                body(SLOTS // UNROLL, j)

        with nc.Block() as block:

            @block.gpsimd
            def _(pool):
                pool.wait_ge(cleared, CLEARS)
                nc.gpsimd.memset(Vh[:], 0.0).then_inc(vh_cleared, 1)
                pool.wait_ge(vh_cleared, 1)

                def body(it, j):
                    s = at(it, j, LT)
                    if s is None:
                        return
                    if not (isinstance(s, int) and s < 2):
                        pool.wait_ge(pv_done, TT * (s - 1))
                    for u in range(2):
                        nc.gpsimd.tensor_copy(Vh[:, (j - LT) % 2, u, :, 0:DH + 1], V[:, 2 * s + u, :, :])\
                            .then_inc(vh_ready, 1)

                slots(pool, body)

            @block.sync
            def _(sp):
                sp.dma_start(mask_nm[:], masks[0]).then_inc(loaded, 16)
                sp.dma_start(mask_mn[:], masks[1]).then_inc(loaded, 16)
                sp.wait_ge(cleared, CLEARS)

                def load(s, r, wait):
                    if wait:
                        sp.wait_ge(tau_mm, NP * (s - RING) + NP)
                    for u in range(2):
                        load_stacks(sp, Q[2 * r + u], K[2 * r + u], qd, kd, 2 * s + u, stack_in[r])

                def send_rows(s, r):
                    sp.wait_ge(rows_sb, s + 1)
                    for u in range(2):
                        n = SPLIT * TT
                        sp.dma_start(Q[2 * r + u][ONES_ROW:ONES_ROW + SPLIT, :].rearrange("s (t n) -> s t n", n=P),
                                     rows[u * n:(u + 1) * n, :])\
                            .then_inc(rows_in[r], 16)

                load(0, 0, False)
                load(1, 1, False)
                for j in range(UNROLL):
                    load(j + 2, (j + 2) % RING, j + 2 >= RING)
                    send_rows(j, j)
                with sp.Fori(1, SLOTS // UNROLL - 1) as it:
                    for j in range(UNROLL):
                        load(UNROLL * it + j + 2, (j + 2) % RING, True)
                        send_rows(UNROLL * it + j, j)
                for j in range(UNROLL):
                    s = SLOTS - UNROLL + j
                    if s + 2 < SLOTS:
                        load(s + 2, (j + 2) % RING, True)
                    send_rows(s, j)

            @block.tensor
            def _(pe):
                pe.wait_ge(loaded, 32)
                pe.wait_ge(identb_ready, 1)

                def scores_max(s, j, y):
                    u, t, half = MAXIMA[y]
                    r, lo, hi = 2 * (j % RING) + u, half * CH, min((half + 1) * CH, (t + 1) * P)
                    diagonal = hi == (t + 1) * P
                    wait_from(pe, max_red, NP * s + y - 2)
                    out = pm[:, y % 3, :]
                    last = nc.tensor.matmul(out[:, 0:hi - lo], Q[r][0:96, t * P:(t + 1) * P], K[r][0:96, lo:hi],
                                            start=True, stop=not diagonal)
                    if diagonal:
                        last = nc.tensor.matmul(out[:, hi - lo - P:hi - lo], identb[:], mask_nm[:],
                                                start=False, stop=True)
                    last.then_inc(max_mm, 1)

                def scores_tau(s, j, y):
                    u, t, half = WEIGHTS[y]
                    r, lo, hi = 2 * (j % RING) + u, max(half * CH, t * P), (half + 1) * CH
                    diagonal = lo == t * P
                    wait_from(pe, tau_exp[y % 3], NP // 3 * s + y // 3)
                    out = pb[:, y % 3, :]
                    last = nc.tensor.matmul(out[:, lo % CH:CH], K[r][:, t * P:(t + 1) * P], Q[r][:, lo:hi],
                                            start=True, stop=not diagonal)
                    if diagonal:
                        last = nc.tensor.matmul(out[:, lo % CH:lo % CH + P], identb[:], mask_mn[:],
                                                start=False, stop=True)
                    last.then_inc(tau_mm, 1)

                def weigh(s, j, t):
                    final = done[t] - 1
                    pe.wait_ge(tau_exp[final % 3], NP // 3 * s + final // 3 + 1)
                    if t == 0:
                        pe.wait_ge(vh_ready, 2 * s + 2)
                        if not (isinstance(s, int) and s < 1):
                            pe.wait_ge(o_sb, s)
                    for u in range(2):
                        for half in range(2):
                            lo, hi = max(half * CH, t * P), (half + 1) * CH
                            if lo >= hi:
                                continue
                            q = 2 * u + half
                            last = nc.tensor.matmul(po[32 * q:32 * q + 32, lo - half * CH:CH],
                                                    Vh[:, j % 2, u, t, :], pt[:, u, t % 2, lo:hi],
                                                    start=(t == 0), stop=(lo + P == hi))
                    last.then_inc(pv_done, 1)

                def turn_rows(s):
                    pe.wait_ge(parts_ready, s + 1)
                    if not (isinstance(s, int) and s < LT + 1):
                        pe.wait_ge(f_done, 2 * (s - LT))
                    nc.tensor.transpose(ptr[:].bitcast(BF16)[:, 0:P], neg[:], identb[:]).then_inc(rows_turned, 1)

                def turn_out(s, rows_before):
                    pe.wait_ge(o_sb, s + 1)
                    if rows_before is not None:
                        pe.wait_ge(rows_sb, rows_before + 1)
                    else:
                        pe.wait_ge(rows_sb, SLOTS)
                        pe.wait_ge(f_done, 2 * s)
                    for c in range(4):
                        last = nc.tensor.transpose(ptr[:, c * P:(c + 1) * P], osb[:, c * P:(c + 1) * P], ident[:])
                    last.then_inc(o_turned, 1)

                def body(it, j):
                    sm, sr, st, so = at(it, j, 0), at(it, j, 1), at(it, j, LT), at(it, j, LT + 1)
                    if sm is not None:
                        pe.wait_ge(stack_in[j % RING], PAIR_LOADS * (it + 1))
                    if st is not None:
                        jt = j - LT
                        pe.wait_ge(rows_in[jt % RING], 32 * (it + jt // RING + 1))
                    for y in range(NP):
                        if sm is not None:
                            scores_max(sm, j, y)
                        if y == 9 and sr is not None:
                            turn_rows(sr)
                        if st is not None:
                            scores_tau(st, j - LT, y)
                            if y - 2 in done:
                                weigh(st, j - LT, done.index(y - 2))
                        if y == 15 and so is not None:
                            turn_out(so, sr)
                    if st is not None:
                        for t in range(TT):
                            if done[t] >= NP - 2:
                                weigh(st, j - LT, t)

                slots(pe, body)

            @block.scalar
            def _(act):

                def exp_tau(s, y):
                    u, t, half = WEIGHTS[y]
                    lo, hi = max(half * CH, t * P), (half + 1) * CH
                    act.wait_ge(tau_mm, NP * s + y + 1)
                    wait_from(act, pv_done, TT * s + t - 1)
                    nc.scalar.activation(pt[:, u, t % 2, lo:hi], pb[:, y % 3, lo % CH:CH], ACT.Exp, scale=SC)\
                        .then_inc(tau_exp[y % 3], 1)

                def copy_out(s):
                    act.wait_ge(pv_done, TT * s + TT)
                    if not (isinstance(s, int) and s < 1):
                        act.wait_ge(o_turned, s)
                    nc.scalar.activation(osb[:], po[:], ACT.Copy).then_inc(o_sb, 1)

                def body(it, j):
                    st, so = at(it, j, LT), at(it, j, LT + 1)
                    for y in range(NP):
                        if st is not None:
                            exp_tau(st, y)
                        if y == 0 and so is not None:
                            copy_out(so)

                slots(act, body)

            @block.vector
            def _(dve):
                nc.vector.tensor_copy(identb[:], ident[:]).then_inc(identb_ready, 1)
                nc.vector.memset(neg[:], 0.0).then_inc(neg_cleared, 1)
                dve.wait_ge(neg_cleared, 1)

                def part(s, j, n):
                    far, top = mx[:, (j - 1) % 2, 1], mx[:, (j - 1) % 2, 0]
                    if n == 0:
                        dve.wait_ge(max_red, NP * s + NP)
                        nc.vector.tensor_tensor(top[:, :, TT // 2:], top[:, :, TT // 2:], far[:, :, TT // 2:], ALU.max)\
                            .then_inc(chain, 1)
                    else:
                        dve.wait_ge(chain, 5 * s + n)
                    if n == 1:
                        wait_from(dve, rows_turned, s)
                        nc.vector.tensor_scalar(neg3[:, :, 0, :], top, -1.0, None, ALU.mult).then_inc(chain, 1)
                    if n == 2:
                        nc.vector.scalar_tensor_tensor(rem[:], top, -1.0, neg3[:, :, 0, :], ALU.mult, ALU.subtract)\
                            .then_inc(chain, 1)
                    if n == 3:
                        nc.vector.tensor_copy(neg3[:, :, 1, :], rem[:]).then_inc(chain, 1)
                    if n == 4:
                        nc.vector.tensor_tensor(rem[:], rem[:], neg3[:, :, 1, :], ALU.subtract).then_inc(chain, 1)
                    if n == 5:
                        nc.vector.tensor_copy(neg3[:, :, 2, :], rem[:]).then_inc(parts_ready, 1)

                def output(s, n):
                    o = ptr[:].rearrange("p (c q k) -> p c q k", c=4, q=4)
                    if n == 0:
                        dve.wait_ge(o_turned, s + 1)
                        if not (isinstance(s, int) and s < 1):
                            dve.wait_ge(f_done, 2 * s)
                        nc.vector.reciprocal(rz[:], o[:, :, :, DH]).then_inc(rz_done, 1)
                    else:
                        u = n - 1
                        dve.wait_ge(rz_done, s + 1)
                        nc.vector.tensor_tensor(
                            F[:, :, 2 * s + u, :].rearrange("p (h c) d -> p c h d", h=2),
                            o[:, :, 2 * u:2 * u + 2, 0:DH],
                            rz[:, :, 2 * u:2 * u + 2].unsqueeze(3).broadcast_to([P, 4, 2, DH]), ALU.mult)\
                            .then_inc(f_done, 1)

                def body(it, j):
                    sm, sr, so = at(it, j, 0), at(it, j, 1), at(it, j, LT + 1)
                    for y in range(NP):
                        if y < 6 and sr is not None:
                            part(sr, j, y)
                        if sm is not None:
                            u, t, half = MAXIMA[y]
                            dve.wait_ge(max_mm, NP * sm + y + 1)
                            nc.vector.tensor_reduce(mx[:, j % 2, half, u, t:t + 1],
                                                    pm[:, y % 3, 0:min(CH, (t + 1) * P - half * CH)],
                                                    AX.X, ALU.max).then_inc(max_red, 1)
                        if y == 11 and sr is not None:
                            dve.wait_ge(rows_turned, sr + 1)
                            if not (isinstance(sr, int) and sr < 1):
                                jr = j - 2
                                dve.wait_ge(rows_in[jr % RING], 32 * (it + jr // RING + 1))
                            nc.vector.tensor_copy(rows[:], ptr[:].bitcast(BF16)[0:2 * SPLIT * TT, 0:P])\
                                .then_inc(rows_sb, 1)
                        if 17 <= y < 20 and so is not None:
                            output(so, y - 17)

                slots(dve, body)
        m.clear_sems()


def attend_both(nc, tag, V, F, par, qd, kd, ident, stacks, cleared):
    SLOTS = HEADS * TT // 2
    PER = TT // 2
    UNROLL = PER * RING
    LS, LT, LE, LP = 4, 6, 6, 7
    SC = DH ** -0.5
    EDGE = 8
    CUT = 25 * T // 32
    with ExitStack() as ctx:
        m = Mem(nc, ctx, tag)
        Q, K = ([stack[:, r, :] for r in range(RING)] for stack in stacks)
        identb = m.sb("identb", [P, P], BF16)
        Vh = m.sb("Vh", [P, 2, TT, 32])
        parh = m.sb("parh", [P, RING, 2])
        mx = m.sb("mx", [P, 2, TT])
        rem = m.sb("rem", [P, TT])
        neg3 = m.sb("neg3", [P, SPLIT, TT], BF16)
        rows = m.sb("rows", [SPLIT * TT, P], BF16)
        pt = [m.sb(f"pt{r}", [P, 2, T]) for r in range(4)]
        sg = [m.sb(f"sg{r}", [P, 2, T]) for r in range(4)]
        shifted = m.sb("shifted", [P, 2, CUT])
        osb = m.sb("osb", [P, CH])
        rz = m.sb("rz", [P, 4, 4])
        fw = m.sb("fw", [P, 4, 4, DH])
        pm = m.ps("pm", [P, T])
        pa = m.ps("pa", [P, T])
        pb = m.ps("pb", [P, T])
        po = m.ps("po", [P, CH])
        ptr = m.ps("ptr", [P, CH])
        identb_ready, vh_cleared = (m.sem(x) for x in ("identb", "vhc"))
        stack_in = [m.sem(f"stack{r}") for r in range(RING)]
        rows_in = [m.sem(f"rowsin{r}") for r in range(RING)]
        max_mm, max_red, parts_ready, rows_turned, rows_sb, chain = (
            m.sem(x) for x in ("maxmm", "maxred", "parts", "rturned", "rsb", "chain"))
        abs_mm, abs_done, shift_done, sq_pool, sq_dve, ln_done, sig_done = (
            m.sem(x) for x in ("absmm", "abs", "shift", "sqp", "sqd", "ln", "sig"))
        tau_mm, tau_exp, vh_ready, par_ready, pv_done, o_sb, o_turned, f_done, rz_done, weighed = (
            m.sem(x) for x in ("taumm", "tauexp", "vh", "par", "pv", "osb", "oturned", "fd", "rz", "weighed"))
        HEAD_LOADS = 16 * STACK_DMAS

        def at(it, j, lag):
            s = UNROLL * it + (j - lag)
            return None if isinstance(s, int) and not 0 <= s < SLOTS else s

        def head(it, j, lag):
            return RING * it + (j - lag) // PER

        def slots(eng, body):
            for j in range(UNROLL):
                body(0, j)
            with eng.Fori(1, SLOTS // UNROLL) as it:
                for j in range(UNROLL):
                    body(it, j)
            for j in range(LP + 2):
                body(SLOTS // UNROLL, j)

        def some(x, least=1):
            return not (isinstance(x, int) and x < least)

        with nc.Block() as block:

            @block.gpsimd
            def _(pool):
                pool.wait_ge(cleared, CLEARS)
                nc.gpsimd.memset(Vh[:], 0.0).then_inc(vh_cleared, 1)
                pool.wait_ge(vh_cleared, 1)

                def body(it, j):
                    s = at(it, j, LS)
                    if s is None:
                        return
                    h = head(it, j, LS)
                    if (j - LS) % PER == 0:
                        if some(h, 2):
                            pool.wait_ge(pv_done, PER * (h - 1))
                        nc.gpsimd.tensor_copy(parh[:, ((j - LS) // PER) % RING, :], par[:, h, :])\
                            .then_inc(par_ready, 1)
                        nc.gpsimd.tensor_copy(Vh[:, ((j - LS) // PER) % 2, :, 0:DH + 1], V[:, h, :, :])\
                            .then_inc(vh_ready, 1)
                    buf = sg[(j - LS) % 4]
                    if some(s):
                        pool.wait_ge(sq_pool, s)
                    pool.wait_ge(abs_done, 2 * s + 2)
                    pool.wait_ge(par_ready, h + 1)
                    b2 = parh[:, ((j - LS) // PER) % RING, 0:1]
                    nc.gpsimd.tensor_tensor(shifted[:, :, 0:EDGE], buf[:, :, 0:EDGE],
                                            b2.unsqueeze(2).broadcast_to([P, 2, EDGE]), ALU.add).then_inc(shift_done, 1)
                    nc.gpsimd.tensor_scalar(shifted[:, :, EDGE:CUT], buf[:, :, EDGE:CUT], b2, 1.0, ALU.add, ALU.mult)\
                        .then_inc(shift_done, 1)
                    pool.wait_ge(shift_done, 2 * s + 2)
                    nc.gpsimd.tensor_tensor(buf[:, :, 0:CUT], buf[:, :, 0:CUT], shifted[:], ALU.mult)\
                        .then_inc(sq_pool, 1)

                slots(pool, body)

            @block.sync
            def _(sp):
                sp.wait_ge(cleared, CLEARS)

                def load(h, r, wait):
                    if wait:
                        sp.wait_ge(tau_mm, TT * (h - RING) + TT)
                    load_stacks(sp, Q[r], K[r], qd, kd, h, stack_in[r])

                def send_rows(h, r):
                    sp.wait_ge(rows_sb, h + 1)
                    sp.dma_start(Q[r][ONES_ROW:ONES_ROW + SPLIT, :].rearrange("s (t n) -> s t n", n=P),
                                 rows[:]).then_inc(rows_in[r], 16)

                load(0, 0, False)
                load(1, 1, False)
                for j in range(RING):
                    load(j + 2, (j + 2) % RING, j + 2 >= RING)
                    send_rows(j, j)
                with sp.Fori(1, HEADS // RING - 1) as it:
                    for j in range(RING):
                        load(RING * it + j + 2, (j + 2) % RING, True)
                        send_rows(RING * it + j, j)
                for j in range(RING):
                    h = HEADS - RING + j
                    if h + 2 < HEADS:
                        load(h + 2, (j + 2) % RING, True)
                    send_rows(h, j)

            @block.tensor
            def _(pe):
                pe.wait_ge(identb_ready, 1)

                def scores(out, lhsT, rhs, t, rows_, sem):
                    for lo in range(0, T, CH):
                        last = nc.tensor.matmul(out[:, lo:lo + CH], lhsT[0:rows_, t * P:(t + 1) * P],
                                                rhs[0:rows_, lo:lo + CH], start=True, stop=True)
                    last.then_inc(sem, 1)

                def weigh(it, j, s, i):
                    h, k, r = head(it, j, LP), (j - LP) % PER, (j - LP) % 4
                    t = 2 * k + i
                    if i == 0:
                        pe.wait_ge(tau_exp, 2 * s + 2)
                        pe.wait_ge(sig_done, s + 1)
                    if t == 0:
                        pe.wait_ge(vh_ready, h + 1)
                        if some(h):
                            pe.wait_ge(o_sb, h)
                    for q, (wts, half) in enumerate(((pt[r], 0), (pt[r], 1), (sg[r], 0), (sg[r], 1))):
                        last = nc.tensor.matmul(po[32 * q:32 * q + 32, :], Vh[:, ((j - LP) // PER) % 2, t, :],
                                                wts[:, i, half * CH:(half + 1) * CH],
                                                start=(t == 0), stop=(t == TT - 1))
                    if i:
                        last.then_inc(pv_done, 1)

                def body(it, j):
                    sm, ss, st, sp_ = at(it, j, 0), at(it, j, LS), at(it, j, LT), at(it, j, LP)
                    rm, rs, rt = (((j - lag) // PER) % RING for lag in (0, LS, LT))
                    if sm is not None and j % PER == 0:
                        pe.wait_ge(stack_in[rm], HEAD_LOADS * (it + 1))
                    if st is not None and (j - LT) % PER == 0:
                        pe.wait_ge(rows_in[rt], 16 * (it + (j - LT) // PER // RING + 1))
                    for i in range(2):
                        if sm is not None:
                            if some(2 * sm + i):
                                pe.wait_ge(max_red, 2 * sm + i)
                            scores(pm, Q[rm], K[rm], 2 * (j % PER) + i, 96, max_mm)
                        if ss is not None:
                            if some(2 * ss + i):
                                pe.wait_ge(abs_done, 2 * ss + i)
                            scores(pa, K[rs], Q[rs], 2 * ((j - LS) % PER) + i, 96, abs_mm)
                        if i and sp_ is not None:
                            weigh(it, j, sp_, 0)
                        if st is not None:
                            if some(2 * st + i):
                                pe.wait_ge(tau_exp, 2 * st + i)
                            scores(pb, K[rt], Q[rt], 2 * ((j - LT) % PER) + i, P, tau_mm)
                        if i and sp_ is not None:
                            weigh(it, j, sp_, 1)
                    if j % PER == 0 and at(it, j, 1) is not None:
                        h = head(it, j, 1)
                        pe.wait_ge(parts_ready, h + 1)
                        if some(h, 2):
                            pe.wait_ge(f_done, h - 1)
                        nc.tensor.transpose(ptr[:].bitcast(BF16)[0:SPLIT * TT, 0:P],
                                            neg3[:].rearrange("p s t -> p (s t)"), identb[:])\
                            .then_inc(rows_turned, 1)
                    if (j - LP - 1) % PER == PER - 1 and at(it, j, LP + 1) is not None:
                        h = head(it, j, LP + 1)
                        pe.wait_ge(o_sb, h + 1)
                        if isinstance(h, int) and h + 3 > HEADS:
                            pe.wait_ge(rows_sb, HEADS)
                            pe.wait_ge(f_done, h)
                        else:
                            pe.wait_ge(rows_sb, h + 2)
                        for c in range(4):
                            last = nc.tensor.transpose(ptr[:, c * P:(c + 1) * P], osb[:, c * P:(c + 1) * P],
                                                       ident[:])
                        last.then_inc(o_turned, 1)

                slots(pe, body)

            @block.scalar
            def _(act):
                nc.scalar.preload_act_table_set("natural_log_exp_and_others")

                def body(it, j):
                    st, se, so = at(it, j, LT), at(it, j, LE), at(it, j, LP + 1)
                    for i in range(2):
                        if st is not None:
                            act.wait_ge(tau_mm, 2 * st + i + 1)
                            if i == 0 and some(st, 4):
                                act.wait_ge(pv_done, st - 3)
                            nc.scalar.activation(pt[(j - LT) % 4][:, i, :], pb[:], ACT.Exp, scale=SC)\
                                .then_inc(tau_exp, 1)
                        if i == 0 and so is not None and (j - LP - 1) % PER == PER - 1:
                            h = head(it, j, LP + 1)
                            act.wait_ge(pv_done, PER * h + PER)
                            if some(h):
                                act.wait_ge(o_turned, h)
                            nc.scalar.activation(osb[:], po[:], ACT.Copy).then_inc(o_sb, 1)
                        if se is not None:
                            buf = sg[(j - LE) % 4]
                            if i == 0:
                                h = head(it, j, LE)
                                act.wait_ge(sq_pool, se + 1)
                                act.wait_ge(sq_dve, se + 1)
                                act.wait_ge(par_ready, h + 1)
                                nc.scalar.activation(buf[:], buf[:], ACT.Ln,
                                                     bias=parh[:, ((j - LE) // PER) % RING, 1:2]).then_inc(ln_done, 1)
                            else:
                                act.wait_ge(ln_done, se + 1)
                                nc.scalar.activation(buf[:], buf[:], ACT.Exp, scale=-1.0).then_inc(sig_done, 1)

                slots(act, body)

            @block.vector
            def _(dve):
                nc.vector.tensor_copy(identb[:], ident[:]).then_inc(identb_ready, 1)

                def part(it, j, n):
                    if j % PER or at(it, j, 1) is None:
                        return
                    h, top = head(it, j, 1), mx[:, ((j - 1) // PER) % 2, :]
                    if n == 0:
                        dve.wait_ge(max_red, TT * h + TT)
                        if some(h):
                            dve.wait_ge(rows_turned, h)
                        nc.vector.tensor_scalar(neg3[:, 0, :], top, -1.0, None, ALU.mult).then_inc(chain, 1)
                    else:
                        dve.wait_ge(chain, 4 * h + n)
                    if n == 1:
                        nc.vector.scalar_tensor_tensor(rem[:], top, -1.0, neg3[:, 0, :], ALU.mult, ALU.subtract)\
                            .then_inc(chain, 1)
                    if n == 2:
                        nc.vector.tensor_copy(neg3[:, 1, :], rem[:]).then_inc(chain, 1)
                    if n == 3:
                        nc.vector.tensor_tensor(rem[:], rem[:], neg3[:, 1, :], ALU.subtract).then_inc(chain, 1)
                    if n == 4:
                        nc.vector.tensor_copy(neg3[:, 2, :], rem[:]).then_inc(parts_ready, 1)

                def output(it, j, n):
                    if (j - LP - 2) % PER != PER - 1 or at(it, j, LP + 2) is None:
                        return
                    h = head(it, j, LP + 2)
                    o = ptr[:].rearrange("p (c q k) -> p c q k", c=4, q=4)
                    if n == 0:
                        dve.wait_ge(o_turned, h + 1)
                        if some(h):
                            dve.wait_ge(weighed, h)
                        nc.vector.reciprocal(rz[:], o[:, :, :, DH]).then_inc(rz_done, 1)
                    if n == 1:
                        dve.wait_ge(rz_done, h + 1)
                        if some(h):
                            dve.wait_ge(f_done, h)
                        nc.vector.tensor_tensor(fw[:], o[:, :, :, 0:DH], rz[:].unsqueeze(3).broadcast_to([P, 4, 4, DH]),
                                                ALU.mult).then_inc(weighed, 1)
                    if n == 2:
                        dve.wait_ge(weighed, h + 1)
                        nc.vector.tensor_tensor(F[:, :, h, :].rearrange("p (s c) d -> p s c d", s=2),
                                                fw[:, :, 0:2, :].rearrange("p c s d -> p s c d"),
                                                fw[:, :, 2:4, :].rearrange("p c s d -> p s c d"), ALU.add)\
                            .then_inc(f_done, 1)

                def body(it, j):
                    sm, ss = at(it, j, 0), at(it, j, LS)
                    part(it, j, 0)
                    for i in range(2):
                        if sm is not None:
                            t = 2 * (j % PER) + i
                            dve.wait_ge(max_mm, 2 * sm + i + 1)
                            nc.vector.tensor_reduce(mx[:, (j // PER) % 2, t:t + 1], pm[:], AX.X, ALU.max)\
                                .then_inc(max_red, 1)
                        part(it, j, 2 * i + 1)
                        output(it, j, 2 * i)
                        if ss is not None:
                            dve.wait_ge(abs_mm, 2 * ss + i + 1)
                            if i == 0 and some(ss, 4):
                                dve.wait_ge(pv_done, ss - 3)
                            nc.vector.tensor_scalar(sg[(j - LS) % 4][:, i, :].bitcast(I32), pa[:].bitcast(I32),
                                                    SIGN_OFF, None, ALU.bitwise_and).then_inc(abs_done, 1)
                        part(it, j, 2 * i + 2)
                        output(it, j, 2 * i + 1)
                        if i == 0 and j % PER == 1 and at(it, j, 2) is not None:
                            h, r = head(it, j, 2), ((j - 2) // PER - 1) % RING
                            dve.wait_ge(rows_turned, h + 1)
                            if some(h):
                                dve.wait_ge(rows_in[r], 16 * (it + ((j - 2) // PER - 1) // RING + 1))
                            nc.vector.tensor_copy(rows[:], ptr[:].bitcast(BF16)[0:SPLIT * TT, 0:P])\
                                .then_inc(rows_sb, 1)
                    if ss is not None:
                        h, buf = head(it, j, LS), sg[(j - LS) % 4]
                        dve.wait_ge(abs_done, 2 * ss + 2)
                        dve.wait_ge(par_ready, h + 1)
                        nc.vector.scalar_tensor_tensor(buf[:, :, CUT:T], buf[:, :, CUT:T],
                                                       parh[:, ((j - LS) // PER) % RING, 0:1], buf[:, :, CUT:T],
                                                       ALU.add, ALU.mult).then_inc(sq_dve, 1)

                slots(dve, body)
        m.clear_sems()


def load_sharpness(nc, tag, par, beta, t):
    with ExitStack() as ctx:
        m = Mem(nc, ctx, tag)
        bt = m.sb("bt", [P, 2, H])
        one = m.sb("one", [P, 2, H])
        loaded, chain = m.sem("loaded"), m.sem("chain")
        with nc.Block() as block:

            @block.sync
            def _(sp):
                sp.dma_start(bt[:, 0, :], beta.unsqueeze(0).broadcast_to([P, H])).then_inc(loaded, 16)
                sp.dma_start(bt[:, 1, :], t.unsqueeze(0).broadcast_to([P, H])).then_inc(loaded, 16)

            @block.vector
            def _(dve):
                dve.wait_ge(loaded, 32)
                link = Chain(dve, chain)
                link(nc.vector.tensor_scalar(bt[:, 0, :], bt[:, 0, :], DH ** 0.5, None, ALU.mult))
                link(nc.vector.tensor_tensor(bt[:, 1, :], bt[:, 0, :], bt[:, 1, :], ALU.mult))
                link(nc.vector.tensor_tensor(one[:], bt[:], bt[:], ALU.mult))
                for b in range(B):
                    link(nc.vector.tensor_scalar(par[:, b * H:(b + 1) * H, 0], bt[:, 0, :], 2.0, None, ALU.mult))
                    link(nc.vector.tensor_tensor(par[:, b * H:(b + 1) * H, 1], one[:, 0, :], one[:, 1, :], ALU.add))
        m.clear_sems()


def program(nc, x, out, w, stop=99):
    x_v = x.rearrange("b (t p) d -> p (b t) d", p=P)
    out_v = out.rearrange("b (t p) d -> p (b t) d", p=P)
    qd = nc.dram_tensor("q_parts", (SPLIT, HEADS, DH, T), BF16, kind="Internal").ap()
    kd = nc.dram_tensor("k_parts", (SPLIT, HEADS, DH, T), BF16, kind="Internal").ap()
    with ExitStack() as ctx:
        m = Mem(nc, ctx, "all")
        X = m.sb("X", [P, NT, D])
        XNT = m.sb("XNT", [P, TOK])
        V = m.sb("V", [P, HEADS, TT, DH + 1])
        ident = m.sb("ident", [P, P])
        rank0 = m.sb("rank0", [P, E0])
        rank1 = m.sb("rank1", [P, E1])
        par = m.sb("par", [P, HEADS, 2])
        stacks = [m.sb(n, [P, 2 * RING, T], BF16) for n in ("Q", "K")]
        loaded, saved, cleared = m.sem("loaded"), m.sem("saved"), m.sem("cleared")
        layer = {n: {k[3:]: v for k, v in w.items() if k.startswith(n)} for n in ("f0_", "a0_", "a1_", "f1_")}
        f0_in, a0_in, f1_in, a1_in = (m.sem(n) for n in ("f0_in", "a0_in", "f1_in", "a1_in"))
        f0, load_f0 = load_ffn0(nc, m, layer["f0_"], f0_in)
        a0, load_a0 = load_attention(nc, m, layer["a0_"], a0_in, False)
        f1, load_f1 = load_ffn1(nc, m, layer["f1_"], f1_in)
        a1, load_a1 = load_attention(nc, m, layer["a1_"], a1_in, True)
        with nc.Block() as block:

            @block.sync
            def _(sp):
                sp.dma_start(X[:], x_v).then_inc(loaded, 16)
                sp.dma_start(ident[:], w["ident"]).then_inc(loaded, 16)
                sp.dma_start(rank0[:], w["rank"][:, E1 - E0:]).then_inc(loaded, 16)
                sp.dma_start(rank1[:], w["rank"]).then_inc(loaded, 16)
                for load in (load_f0, load_a0, load_f1, load_a1):
                    load(sp)
                sp.wait_ge(loaded, 64)

        F = XNT[:].rearrange("p (t h d) -> p t h d", h=HEADS, t=TT)
        tiles = [XNT[:, (k % TT) * HEADS * DH + (k // TT) * D:][:, 0:D] for k in range(NT)]

        steps = [
            lambda: ln_transposed(nc, "n1", X, XNT, ident),
            lambda: ffn0(nc, "f1", X, XNT, rank0, f0, f0_in, lambda pool: clear_stacks(pool, *stacks, cleared)),
            lambda: ln_transposed(nc, "n2", X, XNT, ident),
            lambda: project(nc, "p2", XNT, V, qd, kd, a0, a0_in, False, 1.0),
            lambda: attend_causal(nc, "a2", V, F, qd, kd, ident, stacks, cleared,
                                  (w["mask_nm"], w["mask_mn"])),
            lambda: project_out(nc, "o2", X, tiles, ident, a0, a0_in, False),
            lambda: ln_transposed(nc, "n3", X, XNT, ident),
            lambda: ffn0(nc, "f3", X, XNT, rank0, f0, f0_in),
            lambda: ln_transposed(nc, "n4", X, XNT, ident),
            lambda: ffn1(nc, "f4", X, XNT, ident, rank1, f1, f1_in),
            lambda: ln_transposed(nc, "n5", X, XNT, ident, add_to_x=True),
            lambda: load_sharpness(nc, "s5", par, layer["a1_"]["beta"], layer["a1_"]["t"]),
            lambda: project(nc, "p5", XNT, V, qd, kd, a1, a1_in, True, 2.0),
            lambda: attend_both(nc, "a5", V, F, par, qd, kd, ident, stacks, cleared),
            lambda: project_out(nc, "o5", X, tiles, ident, a1, a1_in, True),
            lambda: ln_transposed(nc, "n6", X, XNT, ident),
            lambda: ffn1(nc, "f6", X, XNT, ident, rank1, f1, f1_in),
        ]
        for step in (steps[:stop] if isinstance(stop, int) else [steps[i] for i in stop]):
            step()
        with nc.Block() as block:

            @block.sync
            def _(sp):
                sp.dma_start(out_v, X[:]).then_inc(saved, 16)
                sp.wait_ge(saved, 16)


def kernel(**inputs):
    import numpy as _np
    import ml_dtypes as _ml
    import concourse.bacc as _bacc
    from concourse import mybir as _mybir
    from concourse.bass_utils import run_bass_kernel_spmd as _run

    i = {k: _np.asarray(v) for k, v in inputs.items()}
    c = _np.ascontiguousarray
    arrays = {"x": c(i["L0_attn_x"])}
    for n in ("Wr", "br", "We1", "We2", "be2"):
        arrays["f0_" + n] = c(i["L0_ffn_" + n])
    arrays["f0_be1T"] = c(i["L0_ffn_be1"].reshape(E0 * FT0, P).T)
    for n in ("Wq", "Wk", "Wv", "Wo"):
        arrays[f"a0_{n}T"] = c(i["L0_attn_" + n].T)
        arrays[f"a1_{n}T"] = c(i["L1_attn_" + n].T)
    for n in ("bq", "bk", "bv", "bo", "beta", "t", "ln_w", "ln_b"):
        arrays["a1_" + n] = c(i["L1_attn_" + n])
    arrays["f1_w_gate"] = c(i["L1_ffn_w_gate"])
    arrays["f1_w_gP"] = c(i["L1_ffn_w_g"].transpose(1, 0, 2).reshape(D, E1 * M1))
    arrays["f1_w_uP"] = c(i["L1_ffn_w_u"].transpose(1, 0, 2).reshape(D, E1 * M1))
    arrays["f1_w_dP"] = c(i["L1_ffn_w_d"].reshape(E1 * M1, D))
    sel = _np.zeros((96, E1 * M1), _np.float32)
    for part in range(SPLIT):
        sel[32 * part + _np.arange(E1 * M1) // M1, _np.arange(E1 * M1)] = 1.0
    arrays["f1_sel"] = sel.astype(_ml.bfloat16)
    arrays["ident"] = _np.eye(P, dtype=_np.float32)
    arrays["rank"] = _np.tile(_np.arange(E1, 0, -1, dtype=_np.float32), (P, 1))
    above = _np.triu(_np.full((P, P), -1e30, _np.float32), 1)
    arrays["mask_nm"] = above.astype(_ml.bfloat16)
    arrays["mask_mn"] = c(above.T).astype(_ml.bfloat16)

    nc = _bacc.Bacc("TRN2", target_bir_lowering=False, num_devices=1)
    named, aps = {}, {}
    for n, a in arrays.items():
        named[f"in_{n}_dram"] = a
        aps[n] = nc.dram_tensor(f"in_{n}_dram", a.shape, _mybir.dt.from_np(a.dtype), kind="ExternalInput").ap()
    out = nc.dram_tensor("out_0_dram", (B, T, D), _mybir.dt.float32, kind="ExternalOutput").ap()
    program(nc, aps.pop("x"), out, aps)
    r = _run(nc, [named], core_ids=[0])
    return r.results[0]["out_0_dram"]
```

```python
from contextlib import ExitStack

import numpy as np

import concourse.bass as bass
from concourse import mybir

F32 = mybir.dt.float32
F16 = mybir.dt.float16
BF16 = mybir.dt.bfloat16
I32 = mybir.dt.int32
ALU = mybir.AluOpType
ACT = mybir.ActivationFunctionType
AX = mybir.AxisListType

P = 128
B, T, D = 4, 1024, 128
H, DH = 16, 8
TOK = B * T
NT = TOK // P
TT = T // P
HEADS = B * H
CH = 512
NCH = TOK // CH
LN_EPS = 1e-5
E0, F0 = 4, 512
FT0 = F0 // P
E1, M1 = 8, 176
KT1 = E1 * M1 // P
SPLIT = 3
PROD = SPLIT * SPLIT * DH
ONES_ROW = 96
RING = 4
SIGN_OFF = 0x7FFFFFFF
WSCALE = 64.0


class Chain:

    def __init__(self, eng, sem, base=0):
        self.eng, self.sem, self.n = eng, sem, base

    def __call__(self, ins):
        ins.then_inc(self.sem, 1)
        self.n = self.n + 1
        self.eng.wait_ge(self.sem, self.n)


class Mem:

    def __init__(self, nc, ctx, tag):
        self.nc, self.ctx, self.tag, self.sems = nc, ctx, tag, []

    def sb(self, name, shape, dt=F32):
        return self.ctx.enter_context(self.nc.sbuf_tensor(f"{self.tag}_{name}", shape, dt))

    def ps(self, name, shape, dt=F32):
        return self.ctx.enter_context(self.nc.psum_tensor(f"{self.tag}_{name}", shape, dt))

    def sem(self, name):
        self.sems.append(self.ctx.enter_context(self.nc.semaphore(f"{self.tag}_{name}")))
        return self.sems[-1]

    def clear_sems(self):
        nums = sorted(s.num for s in self.sems)
        starts = [n for n in nums if n - 1 not in nums]
        ends = [n + 1 for n in nums if n + 1 not in nums]
        with self.nc.Block() as block:

            @block.gpsimd
            def _(pool):
                for a, b in zip(starts, ends):
                    self.nc.gpsimd.sem_clear(range(a, b))


def ln_transposed(nc, tag, X, XNT, ident, add_to_x=False, split=None, router=None):
    G = 4
    GT = NT // G
    with ExitStack() as ctx:
        m = Mem(nc, ctx, tag)
        stats = m.sb("stats", [P, NT, 6])
        mv = m.sb("mv", [P, NT, 2])
        rs = m.sb("rs", [P, NT])
        t1 = m.sb("t1", [P, NT])
        rstd = m.sb("rstd", [P, NT])
        ve = m.sb("ve", [P, NT])
        xn = m.sb("xn", [P, NT, P])
        pt = m.ps("pt", [P, 4, CH])
        stats_done, mv_done, ve_ready, ln_var, rs_ready = (m.sem(x) for x in ("stats", "mvs", "ve", "lnv", "rsr"))
        dve_chain, xn_ready, turned, evacuated = (m.sem(x) for x in ("chain", "xnr", "turned", "evac"))
        x_added, high_done, low_done = (m.sem(x) for x in ("xadd", "high", "low"))
        rstd_ready = m.sem("rstdr")
        if router:
            wr, router_in, router_loads, score = router
            psr = m.ps("psr", score.shape)
        routed, scored = m.sem("routed"), m.sem("scored")

        with nc.Block() as block:

            @block.vector
            def _(dve):

                def statistics(g):
                    for k in range(g * GT, (g + 1) * GT):
                        nc.vector.bn_stats(stats[:, k, :], X[:, k, :]).then_inc(stats_done, 1)
                    for k in range(g * GT, (g + 1) * GT):
                        dve.wait_ge(stats_done, k + 1)
                        nc.vector.bn_aggr(mv[:, k, :], stats[:, k, :]).then_inc(mv_done, 1)
                    tiles = slice(g * GT, (g + 1) * GT)
                    dve.wait_ge(mv_done, (g + 1) * GT)
                    nc.vector.tensor_scalar(ve[:, tiles], mv[:, tiles, 1], LN_EPS, None, ALU.add).then_inc(ve_ready, 1)

                def normalise(g):
                    tiles = slice(g * GT, (g + 1) * GT)
                    dve.wait_ge(ve_ready, g + 1)
                    dve.wait_ge(rs_ready, g + 1)
                    link = Chain(dve, dve_chain, 3 * g)
                    link(nc.vector.tensor_tensor(t1[:, tiles], rs[:, tiles], rs[:, tiles], ALU.mult))
                    link(nc.vector.tensor_tensor(t1[:, tiles], t1[:, tiles], ve[:, tiles], ALU.mult))
                    link(nc.vector.tensor_scalar(t1[:, tiles], t1[:, tiles], -0.5, 1.5, ALU.mult, ALU.add))
                    nc.vector.tensor_tensor(rstd[:, tiles], rs[:, tiles], t1[:, tiles], ALU.mult)\
                        .then_inc(rstd_ready, 1)
                    dve.wait_ge(rstd_ready, g + 1)
                    for k in range(g * GT, (g + 1) * GT):
                        nc.vector.tensor_scalar(xn[:, k, :], X[:, k, :], mv[:, k, 0:1], rstd[:, k:k + 1],
                                                ALU.subtract, ALU.mult).then_inc(xn_ready, 1)

                statistics(0)
                for g in range(1, G):
                    statistics(g)
                    normalise(g - 1)
                normalise(G - 1)

            XH, XL = split or (None, None)

            @block.gpsimd
            def _(pool):

                def low(c):
                    cols = slice(c * CH, (c + 1) * CH)
                    pool.wait_ge(evacuated, c + 1)
                    pool.wait_ge(high_done, c + 1)
                    nc.gpsimd.tensor_tensor(XL[:, cols], XNT[:, cols], XH[:, cols], ALU.subtract).then_inc(low_done, 1)

                def add(k):
                    pool.wait_ge(xn_ready, k + 1)
                    nc.gpsimd.tensor_tensor(X[:, k, :], X[:, k, :], xn[:, k, :], ALU.add).then_inc(x_added, 1)

                if split:
                    for c in range(NCH):
                        low(c)
                if add_to_x:
                    for k in range(NT):
                        add(k)

            @block.scalar
            def _(act):
                nc.scalar.preload_act_table_set("natural_log_exp_and_others")

                def evacuate(c):
                    act.wait_ge(turned, c + 1)
                    if split:
                        nc.scalar.activation(XH[:, c * CH:(c + 1) * CH], pt[:, c % 4, :], ACT.Copy)\
                            .then_inc(high_done, 1)
                    nc.scalar.activation(XNT[:, c * CH:(c + 1) * CH], pt[:, c % 4, :], ACT.Copy).then_inc(evacuated, 1)

                for g in range(G):
                    tiles = slice(g * GT, (g + 1) * GT)
                    act.wait_ge(ve_ready, g + 1)
                    nc.scalar.activation(rs[:, tiles], ve[:, tiles], ACT.Ln).then_inc(ln_var, 1)
                    act.wait_ge(ln_var, g + 1)
                    nc.scalar.activation(rs[:, tiles], rs[:, tiles], ACT.Exp, scale=-0.5).then_inc(rs_ready, 1)
                    if g >= 2:
                        for c in range((g - 2) * NCH // G, (g - 1) * NCH // G):
                            evacuate(c)
                for c in range((G - 2) * NCH // G, NCH):
                    evacuate(c)
                if router:
                    act.wait_ge(routed, 1)
                    nc.scalar.activation(score[:], psr[:], ACT.Copy).then_inc(scored, 1)

            @block.tensor
            def _(pe):

                def route(c):
                    pe.wait_ge(evacuated, c + 1)
                    for k in range(4 * c, 4 * c + 4):
                        last = nc.tensor.matmul(psr[:, k, :], XNT[:, k * P:(k + 1) * P], wr[:], start=True, stop=True)
                    if c == NCH - 1:
                        last.then_inc(routed, 1)

                if router:
                    pe.wait_ge(router_in, router_loads)
                for c in range(NCH):
                    if c >= 4:
                        pe.wait_ge(evacuated, c - 3)
                    pe.wait_ge(xn_ready, 4 * c + 4)
                    for q in range(4):
                        last = nc.tensor.transpose(pt[:, c % 4, q * P:(q + 1) * P], xn[:, 4 * c + q, :], ident[:])
                    last.then_inc(turned, 1)
                    if router and c >= 2:
                        route(c - 2)
                if router:
                    route(NCH - 2)
                    route(NCH - 1)
        m.clear_sems()


def first_argmax(link, nc, onehot, score, top, pref, eq, rank, n):
    link(nc.vector.tensor_reduce(top[:], score[:], AX.X, ALU.max))
    link(nc.vector.tensor_tensor(eq[:], score[:], top[:].unsqueeze(2).broadcast_to([P, NT, n]), ALU.is_equal))
    link(nc.vector.tensor_tensor(pref[:], eq[:], rank[:].unsqueeze(1).broadcast_to([P, NT, n]), ALU.mult))
    link(nc.vector.tensor_reduce(eq[:, :, 0], pref[:], AX.X, ALU.max))
    link(nc.vector.tensor_tensor(onehot[:], pref[:], eq[:, :, 0:1].broadcast_to([P, NT, n]), ALU.is_equal))


def load_ffn0(m, w, sem):
    b1 = m.sb("b1", [P, E0 * FT0])
    b2 = m.sb("b2", [P, E0, D])
    wr = m.sb("wr", [P, E0])
    br = m.sb("br", [P, E0])

    def load(eng):
        eng.dma_start(wr[:], w["Wr"]).then_inc(sem, 16)
        eng.dma_start(br[:], w["br"].unsqueeze(0).broadcast_to([P, E0])).then_inc(sem, 16)
        eng.dma_start(b1[:], w["be1T"]).then_inc(sem, 16)
        eng.dma_start(b2[:], w["be2"].unsqueeze(0).broadcast_to([P, E0, D])).then_inc(sem, 16)

    return (b1, b2, wr, br), load


FFN0_LOADS = 16 * 4


def load_ffn1(m, w, sem):
    wgate = m.sb("wgate", [P, E1])
    sel = m.sb("sel", [96, KT1, P], BF16)

    def load(eng):
        eng.dma_start(wgate[:], w["w_gate"]).then_inc(sem, 16)
        eng.dma_start(sel[:], w["sel"].rearrange("r (k p) -> r k p", p=P)).then_inc(sem, 16)

    return (wgate, sel), load


FFN1_LOADS = 16 * 2


def split_weights(nc, tag, pairs, stacks, cleared):
    with ExitStack() as ctx:
        m = Mem(nc, ctx, tag)
        raw = [m.sb(f"raw{n}", shape) for n, (shape, *_) in enumerate(pairs)]
        loaded = [m.sem(f"loaded{n}") for n in range(len(pairs))]
        high_done, low_done = m.sem("high"), m.sem("low")
        with nc.Block() as block:

            @block.gpsimd
            def _(pool):
                clear_stacks(pool, *stacks, cleared)

            @block.sync
            def _(sp):
                for n, (_, src, *_) in enumerate(pairs):
                    sp.dma_start(raw[n][:], src).then_inc(loaded[n], 16)

            @block.scalar
            def _(act):
                for n, (_, _, high, _) in enumerate(pairs):
                    act.wait_ge(loaded[n], 16)
                    nc.scalar.activation(high[:], raw[n][:], ACT.Copy, scale=WSCALE).then_inc(high_done, 1)

            @block.vector
            def _(dve):
                for n, (_, _, high, low) in enumerate(pairs):
                    dve.wait_ge(high_done, n + 1)
                    nc.vector.scalar_tensor_tensor(low[:], raw[n][:], WSCALE, high[:], ALU.mult, ALU.subtract)\
                        .then_inc(low_done, 1)
        m.clear_sems()


def s_at(c, e):
    return E0 * c + e if isinstance(c, int) else None


def ffn0(nc, tag, X, split, score, rank, w, parts, weights_in):
    with ExitStack() as ctx:
        m = Mem(nc, ctx, tag)
        top = m.sb("top", [P, NT])
        eq = m.sb("eq", [P, NT, E0])
        pref = m.sb("pref", [P, NT, E0])
        mask = m.sb("mask", [P, NT, E0])
        masky = m.sb("masky", [P, NT, E0])
        XH, XL = split
        w1h, w1l, w2h, w2l = parts
        hid = m.sb("hid", [P, FT0, CH])
        hidh = m.sb("hidh", [P, 2, FT0, CH], F16)
        hidl = m.sb("hidl", [P, 2, FT0, CH], F16)
        psh = m.ps("psh", [P, 4, CH])
        psy = m.ps("psy", [P, 2, 4, D])
        chain = m.sem("chain")
        b1, b2, wr, br = w
        h_done, relu_done, low_done, low_pool, y_done, added = (
            m.sem(x) for x in ("h", "relu", "low", "lowpool", "y", "added"))
        FD = FT0 - 1
        with nc.Block() as block:

            @block.gpsimd
            def _(pool):
                def low(s, e):
                    pool.wait_ge(relu_done, FT0 * s + 1)
                    nc.gpsimd.tensor_tensor(hidl[:, e % 2, 0, :], hid[:, 0, :], hidh[:, e % 2, 0, :],
                                            ALU.subtract).then_inc(low_pool, 1)

                for e in range(E0):
                    low(e, e)
                with pool.Fori(1, NCH) as c:
                    for e in range(E0):
                        low(E0 * c + e, e)

            @block.tensor
            def _(pe):
                pe.wait_ge(weights_in, FFN0_LOADS)

                def hidden(c, e):
                    for j in range(FT0):
                        if e or not isinstance(c, int):
                            pe.wait_ge(relu_done, FT0 * (E0 * c + e - 1) + j + 1)
                        high, low = (part[:, e, j * P:(j + 1) * P] for part in (w1h, w1l))
                        xh, xl = (part[:, bass.ds(c * CH, CH)] for part in (XH, XL))
                        nc.tensor.matmul(psh[:, j, :], high, xh, start=True, stop=False)
                        nc.tensor.matmul(psh[:, j, :], high, xl, start=False, stop=False)
                        nc.tensor.matmul(psh[:, j, :], low, xh, start=False, stop=True).then_inc(h_done, 1)

                def output(c, e):
                    s = E0 * c + e
                    pe.wait_ge(low_done, FD * s + FD)
                    pe.wait_ge(low_pool, s + 1)
                    if s_at(c, e) is None or s_at(c, e) >= 2:
                        pe.wait_ge(added, 8 * (s - 1))
                    for q in range(4):
                        for j in range(FT0):
                            high, low = (part[:, e % 2, j, q * P:(q + 1) * P] for part in (hidh, hidl))
                            out, k = psy[:, e % 2, q, :], e * FT0 + j
                            nc.tensor.matmul(out, high, w2h[:, k, :], start=(j == 0), stop=False)
                            nc.tensor.matmul(out, high, w2l[:, k, :], start=False, stop=False)
                            last = nc.tensor.matmul(out, low, w2h[:, k, :], start=False, stop=(j == FT0 - 1))
                    last.then_inc(y_done, 1)

                def chunk(c, first):
                    hidden(c, 0)
                    if not first:
                        output(c - 1, E0 - 1)
                    for e in range(1, E0):
                        hidden(c, e)
                        output(c, e - 1)

                chunk(0, True)
                with pe.Fori(1, NCH) as c:
                    chunk(c, False)
                output(NCH - 1, E0 - 1)

            @block.scalar
            def _(act):
                act.wait_ge(weights_in, FFN0_LOADS)

                def relu(c, e, j):
                    s = E0 * c + e
                    act.wait_ge(h_done, FT0 * s + j + 1)
                    if s_at(c, e) is None or s_at(c, e) >= 2:
                        act.wait_ge(y_done, s - 1)
                    if e or not isinstance(c, int):
                        if j:
                            act.wait_ge(low_done, FD * (s - 1) + j)
                        else:
                            act.wait_ge(low_pool, s)
                    bias = b1[:, e * FT0 + j:e * FT0 + j + 1]
                    nc.scalar.activation(hidh[:, e % 2, j, :], psh[:, j, :], ACT.Relu, bias=bias,
                                         scale=1.0 / WSCALE)
                    nc.scalar.activation(hid[:, j, :], psh[:, j, :], ACT.Relu, bias=bias,
                                         scale=1.0 / WSCALE).then_inc(relu_done, 1)

                for e in range(E0):
                    for j in range(FT0):
                        relu(0, e, j)
                with act.Fori(1, NCH) as c:
                    for e in range(E0):
                        for j in range(FT0):
                            relu(c, e, j)

            @block.vector
            def _(dve):
                dve.wait_ge(weights_in, FFN0_LOADS)
                link = Chain(dve, chain)
                link(nc.vector.tensor_tensor(score[:], score[:], br[:].unsqueeze(1).broadcast_to([P, NT, E0]), ALU.add))
                first_argmax(link, nc, mask, score, top, pref, eq, rank, E0)

                def low(c, e):
                    for j in range(1, FT0):
                        dve.wait_ge(relu_done, FT0 * (E0 * c + e) + j + 1)
                        nc.vector.tensor_tensor(hidl[:, e % 2, j, :], hid[:, j, :], hidh[:, e % 2, j, :], ALU.subtract)\
                            .then_inc(low_done, 1)

                def bias(c, e):
                    for q in range(4):
                        if e:
                            dve.wait_ge(added, 8 * (E0 * c + e - 1) + 4 + q + 1)
                        nc.vector.scalar_tensor_tensor(X[:, 4 * c + q, :], b2[:, e, :], mask[:, 4 * c + q, e:e + 1],
                                                       X[:, 4 * c + q, :], ALU.mult, ALU.add).then_inc(added, 1)

                def add(c, e):
                    dve.wait_ge(y_done, E0 * c + e + 1)
                    for q in range(4):
                        dve.wait_ge(added, 8 * (E0 * c + e) + q + 1)
                        nc.vector.scalar_tensor_tensor(X[:, 4 * c + q, :], psy[:, e % 2, q, :],
                                                       masky[:, 4 * c + q, e:e + 1], X[:, 4 * c + q, :],
                                                       ALU.mult, ALU.add).then_inc(added, 1)

                def chunk(c):
                    for e in range(E0):
                        low(c, e)
                        if e:
                            add(c, e - 1)
                        else:
                            add(c - 1, E0 - 1)
                        bias(c, e)

                low(0, 0)
                link(nc.vector.tensor_scalar(masky[:], mask[:], 0.5 / WSCALE, None, ALU.mult))
                link(nc.vector.tensor_scalar(mask[:], mask[:], 0.5, None, ALU.mult))
                bias(0, 0)
                for e in range(1, E0):
                    low(0, e)
                    add(0, e - 1)
                    bias(0, e)
                with dve.Fori(1, NCH) as c:
                    chunk(c)
                add(NCH - 1, E0 - 1)
        m.clear_sems()


def ffn1(nc, tag, X, spare, split, score, ident, rank, w, parts, weights_in, out=None):
    with ExitStack() as ctx:
        m = Mem(nc, ctx, tag)
        wgate, sel = w
        wgh, wgl, wuh, wul, wdh, wdl = parts
        XH, XL = split
        rest = m.sb("rest", [P, NT, E1])
        top = m.sb("top", [P, NT])
        top2 = m.sb("top2", [P, NT])
        eq = m.sb("eq", [P, NT, E1])
        pref = m.sb("pref", [P, NT, E1])
        one1 = m.sb("one1", [P, NT, E1])
        one2 = m.sb("one2", [P, NT, E1])
        pr = m.sb("pr", [P, 4, NT])
        gate = m.sb("gate", [P, NT, E1])
        gate3 = m.sb("gate3", [P, NT, 96], BF16)
        gateT = m.sb("gateT", [96, TOK], BF16)
        identb = m.sb("identb", [P, P], BF16)
        sg = m.sb("sg", [P, 2, CH])
        su = m.sb("su", [P, 2, CH])
        hid = m.sb("hid", [P, 4, CH])
        hidh, hidl = ((m.sb(n, [P, KT1, CH], F16), buf[:, 0:KT1 * CH // 2].bitcast(F16)
                       .rearrange("p (k n) -> p k n", n=CH)) for n, buf in zip(("hidh", "hidl"), spare))
        psg = m.ps("psg", [P, 2, CH])
        psu = m.ps("psu", [P, 2, CH])
        psm = m.ps("psm", [P, 2, CH])
        psy = m.ps("psy", [P, 4, D])
        ident_ready, chain, e2, saved = (m.sem(x) for x in ("identb", "chain", "e2", "saved"))
        cleared, gate_ready, turned, gate_out = (m.sem(x) for x in ("cleared", "gate", "turned", "gateout"))
        g_done, u_done, m_done, silu_done, su_done, hid_done, high_done, low_done, y_done, added = (
            m.sem(x) for x in ("gd", "ud", "md", "silu", "sud", "hidd", "high", "low", "yd", "added"))
        EARLY = 4

        def chunks(eng, body):
            for p in range(2):
                body(p, p)
            with eng.Fori(1, NCH // 2) as pair:
                for p in range(2):
                    body(2 * pair + p, p)

        def s_min(s):
            return s if isinstance(s, int) else KT1

        def bank(p, k):
            return (KT1 * p + k) % 2

        with nc.Block() as block:

            if out is not None:

                @block.sync
                def _(sp):
                    for c in range(NCH):
                        sp.wait_ge(added, 4 * c + 4)
                        sp.dma_start(out[:, 4 * c:4 * c + 4, :], X[:, 4 * c:4 * c + 4, :]).then_inc(saved, 16)
                    sp.wait_ge(saved, 16 * NCH)

            @block.gpsimd
            def _(pool):
                nc.gpsimd.memset(gate3[:], 0.0).then_inc(cleared, 1)

                def low(c, p, k):
                    s = KT1 * c + k
                    pool.wait_ge(high_done, s + 1)
                    nc.gpsimd.tensor_tensor(hidl[p][:, k, :], hid[:, k % 4, :], hidh[p][:, k, :], ALU.subtract)\
                        .then_inc(low_done, 1)

                def chunk(c, p):
                    for k in range(KT1):
                        low(c, p, k)

                chunks(pool, chunk)

            @block.tensor
            def _(pe):
                pe.wait_ge(weights_in, FFN1_LOADS)
                pe.wait_ge(gate_ready, 1)
                pe.wait_ge(ident_ready, 1)
                for c in range(NCH):
                    if c >= 2:
                        pe.wait_ge(gate_out, c - 1)
                    out = psm[:, c % 2, :].bitcast(BF16)
                    for q in range(4):
                        last = nc.tensor.transpose(out[0:96, q * P:(q + 1) * P], gate3[:, 4 * c + q, :], identb[:])
                    last.then_inc(turned, 1)
                pe.wait_ge(gate_out, NCH)

                def step(c, p, k):
                    b = bank(p, k)
                    s = KT1 * c + k
                    if s_min(s) >= 2:
                        pe.wait_ge(silu_done, s - 1)
                        pe.wait_ge(su_done, s - 1)
                        pe.wait_ge(hid_done, s - 1)
                    xh, xl = (part[:, bass.ds(c * CH, CH)] for part in (XH, XL))
                    for out, highs, lows, done in ((psg, wgh, wgl, g_done), (psu, wuh, wul, u_done)):
                        high, low = (part[:, k * P:(k + 1) * P] for part in (highs, lows))
                        nc.tensor.matmul(out[:, b, :], high, xh, start=True, stop=False)
                        nc.tensor.matmul(out[:, b, :], high, xl, start=False, stop=False)
                        nc.tensor.matmul(out[:, b, :], low, xh, start=False, stop=True).then_inc(done, 1)
                    nc.tensor.matmul(psm[:, b, :], sel[:, k, :], gateT[:, bass.ds(c * CH, CH)],
                                     start=True, stop=True).then_inc(m_done, 1)

                def output(c, p):
                    pe.wait_ge(low_done, KT1 * c + KT1)
                    if not (isinstance(c, int) and c == 0):
                        pe.wait_ge(added, 4 * c)
                    for q in range(4):
                        for k in range(KT1):
                            high, low = (part[p][:, k, q * P:(q + 1) * P] for part in (hidh, hidl))
                            nc.tensor.matmul(psy[:, q, :], high, wdh[:, k, :], start=(k == 0), stop=False)
                            nc.tensor.matmul(psy[:, q, :], high, wdl[:, k, :], start=False, stop=False)
                            last = nc.tensor.matmul(psy[:, q, :], low, wdh[:, k, :], start=False,
                                                    stop=(k == KT1 - 1))
                    last.then_inc(y_done, 1)

                def chunk(c, p):
                    for k in range(KT1):
                        step(c, p, k)
                        if k == EARLY - 1 and not (isinstance(c, int) and c == 0):
                            output(c - 1, 1 - p)

                chunks(pe, chunk)
                output(NCH - 1, 1)

            @block.scalar
            def _(act):
                act.wait_ge(e2, 1)
                nc.scalar.activation(pr[:, 1, :], pr[:, 0, :], ACT.Exp).then_inc(e2, 1)
                for c in range(NCH):
                    act.wait_ge(turned, c + 1)
                    nc.scalar.activation(gateT[:, c * CH:(c + 1) * CH], psm[:, c % 2, :].bitcast(BF16)[0:96, 0:CH],
                                         ACT.Copy).then_inc(gate_out, 1)

                def silu(c, p, k):
                    b = bank(p, k)
                    s = KT1 * c + k
                    act.wait_ge(g_done, s + 1)
                    if s_min(s) >= 2:
                        act.wait_ge(su_done, s - 1)
                    nc.scalar.activation(sg[:, b, :], psg[:, b, :], ACT.Silu, scale=1.0 / WSCALE)\
                        .then_inc(silu_done, 1)

                def high(c, p, k):
                    act.wait_ge(hid_done, KT1 * c + k + 1)
                    if k == 0 and not (isinstance(c, int) and c < 2):
                        act.wait_ge(y_done, c - 1)
                    nc.scalar.activation(hidh[p][:, k, :], hid[:, k % 4, :], ACT.Copy).then_inc(high_done, 1)

                def chunk(c, p):
                    for k in range(KT1):
                        silu(c, p, k)
                        if k:
                            high(c, p, k - 1)
                        elif not (isinstance(c, int) and c == 0):
                            high(c - 1, 1 - p, KT1 - 1)

                chunks(act, chunk)
                high(NCH - 1, 1, KT1 - 1)

            @block.vector
            def _(dve):
                nc.vector.tensor_copy(identb[:], ident[:]).then_inc(ident_ready, 1)
                link = Chain(dve, chain)
                first_argmax(link, nc, one1, score, top, pref, eq, rank, E1)
                link(nc.vector.scalar_tensor_tensor(rest[:], one1[:], -3.0e38, score[:], ALU.mult, ALU.add))
                first_argmax(link, nc, one2, rest, top2, pref, eq, rank, E1)
                nc.vector.tensor_tensor(pr[:, 0, :], top2[:], top[:], ALU.subtract).then_inc(e2, 1)
                dve.wait_ge(e2, 2)
                link(nc.vector.tensor_scalar(pr[:, 0, :], pr[:, 1, :], 2.0 * WSCALE, 2.0 * WSCALE, ALU.mult, ALU.add))
                link(nc.vector.reciprocal(pr[:, 2, :], pr[:, 0, :]))
                link(nc.vector.tensor_tensor(pr[:, 3, :], pr[:, 2, :], pr[:, 1, :], ALU.mult))
                link(nc.vector.tensor_tensor(gate[:], one1[:], pr[:, 2, :].unsqueeze(2).broadcast_to([P, NT, E1]),
                                             ALU.mult))
                link(nc.vector.tensor_tensor(eq[:], one2[:], pr[:, 3, :].unsqueeze(2).broadcast_to([P, NT, E1]),
                                             ALU.mult))
                link(nc.vector.tensor_tensor(gate[:], gate[:], eq[:], ALU.add))
                dve.wait_ge(cleared, 1)
                link(nc.vector.tensor_copy(gate3[:, :, 0:E1], gate[:]))
                link(nc.vector.tensor_tensor(gate[:], gate[:], gate3[:, :, 0:E1], ALU.subtract))
                link(nc.vector.tensor_copy(gate3[:, :, 32:32 + E1], gate[:]))
                link(nc.vector.tensor_tensor(gate[:], gate[:], gate3[:, :, 32:32 + E1], ALU.subtract))
                nc.vector.tensor_copy(gate3[:, :, 64:64 + E1], gate[:]).then_inc(gate_ready, 1)

                def products(c, p, k):
                    b = bank(p, k)
                    s = KT1 * c + k
                    dve.wait_ge(silu_done, s + 1)
                    dve.wait_ge(u_done, s + 1)
                    if s_min(s) >= 2:
                        dve.wait_ge(hid_done, s - 1)
                    nc.vector.tensor_tensor(su[:, b, :], psu[:, b, :], sg[:, b, :], ALU.mult)\
                        .then_inc(su_done, 1)
                    dve.wait_ge(m_done, s + 1)
                    dve.wait_ge(su_done, s + 1)
                    if s_min(s) >= 3:
                        dve.wait_ge(low_done, s - 2)
                    nc.vector.tensor_tensor(hid[:, k % 4, :], psm[:, b, :], su[:, b, :], ALU.mult)\
                        .then_inc(hid_done, 1)

                def add(c):
                    dve.wait_ge(y_done, c + 1)
                    for q in range(4):
                        nc.vector.scalar_tensor_tensor(X[:, 4 * c + q, :], psy[:, q, :], 1.0 / WSCALE,
                                                       X[:, 4 * c + q, :], ALU.mult, ALU.add).then_inc(added, 1)

                def chunk(c, p):
                    for k in range(KT1):
                        products(c, p, k)
                        if k == EARLY - 1 and not (isinstance(c, int) and c == 0):
                            add(c - 1)

                chunks(dve, chunk)
                add(NCH - 1)
        m.clear_sems()


def load_attention(m, w, sem, biased):
    wqT, wkT, wvT, woT = (m.sb(f"w{n}T{int(biased)}", [P, D]) for n in "qkvo")
    bq, bv, bo, lw, lb = (m.sb(n, [P, 2 if n == "bq" else D]) if biased else None
                          for n in ("bq", "bv", "bo", "lw", "lb"))

    def load(eng):
        for dst, name in ((wqT, "WqT"), (wkT, "WkT"), (wvT, "WvT"), (woT, "WoT")):
            eng.dma_start(dst[:], w[name]).then_inc(sem, 16)
        if biased:
            eng.dma_start(bq[:, 0:1], w["bq"].unsqueeze(1)).then_inc(sem, 16)
            eng.dma_start(bq[:, 1:2], w["bk"].unsqueeze(1)).then_inc(sem, 16)
            for dst, name in ((bv, "bv"), (bo, "bo"), (lw, "ln_w"), (lb, "ln_b")):
                eng.dma_start(dst[:], w[name].unsqueeze(0).broadcast_to([P, D])).then_inc(sem, 16)

    return (wqT, wkT, wvT, bq, bv, woT, bo, lw, lb), load


ATTENTION_LOADS = (16 * 4, 16 * 10)


def project(nc, tag, XNT, V, qd, kd, w, weights_in, biased, ones):
    wqT, wkT, wvT, bq, bv = w[:5]
    with ExitStack() as ctx:
        m = Mem(nc, ctx, tag)
        parts = m.sb("parts", [P, 4, SPLIT, CH], BF16)
        rest = m.sb("rest", [P, 4, CH])
        psq = m.ps("psq", [P, 4, CH])
        psv = m.ps("psv", [P, 2, 4, D])
        q_done, hi_done, rest_done, mid_done, lo_done = (m.sem(x) for x in ("qd", "hi", "rest", "mid", "lo"))
        stored = [m.sem(f"stored{r}") for r in range(4)]
        v_done, v_out, ones_set = m.sem("vd"), m.sem("vo"), m.sem("ones")
        loads = ATTENTION_LOADS[biased]
        pieces = range(2 * NCH)
        with nc.Block() as block:

            @block.sync
            def _(sp):
                for i in pieces:
                    c, n = divmod(i, 2)
                    b, half = divmod(c, 2)
                    sp.wait_ge(lo_done, i + 1)
                    sp.dma_start((qd, kd)[n][:, b * H:(b + 1) * H, :, half * CH:(half + 1) * CH]
                                 .rearrange("s h d t -> (h d) s t"), parts[:, i % 4]).then_inc(stored[i % 4], 16)
                for r in range(4):
                    sp.wait_ge(stored[r], 16 * 2 * NCH // 4)

            @block.tensor
            def _(pe):
                pe.wait_ge(weights_in, loads)
                for c in range(NCH):
                    for n, wT in enumerate((wqT, wkT)):
                        i = 2 * c + n
                        if i >= 4:
                            pe.wait_ge(rest_done, i - 3)
                        nc.tensor.matmul(psq[:, i % 4, :], wT[:], XNT[:, c * CH:(c + 1) * CH], start=True, stop=True)\
                            .then_inc(q_done, 1)
                    if c >= 2:
                        pe.wait_ge(v_out, 4 * (c - 1))
                    for q in range(4):
                        last = nc.tensor.matmul(psv[:, c % 2, q, :], XNT[:, (4 * c + q) * P:(4 * c + q + 1) * P],
                                                wvT[:], start=True, stop=True)
                    last.then_inc(v_done, 1)

            @block.scalar
            def _(act):
                act.wait_ge(weights_in, loads)

                def high(i):
                    act.wait_ge(q_done, i + 1)
                    if i >= 4:
                        act.wait_ge(stored[i % 4], 16 * (i // 4))
                    nc.scalar.activation(parts[:, i % 4, 0, :], psq[:, i % 4, :], ACT.Identity,
                                         bias=bq[:, i % 2:i % 2 + 1] if biased else 0.0).then_inc(hi_done, 1)

                def middle(i):
                    act.wait_ge(rest_done, i + 1)
                    nc.scalar.activation(parts[:, i % 4, 1, :], rest[:, i % 4, :], ACT.Copy).then_inc(mid_done, 1)

                high(0)
                for i in pieces[1:]:
                    high(i)
                    middle(i - 1)
                middle(pieces[-1])

            @block.vector
            def _(dve):
                dve.wait_ge(weights_in, loads)
                nc.vector.memset(V[:, :, :, DH:DH + 1], ones).then_inc(ones_set, 1)

                def rest_of(i):
                    dve.wait_ge(hi_done, i + 1)
                    if i >= 4:
                        dve.wait_ge(lo_done, i - 3)
                    nc.vector.scalar_tensor_tensor(rest[:, i % 4, :], psq[:, i % 4, :],
                                                   bq[:, i % 2:i % 2 + 1] if biased else 0.0,
                                                   parts[:, i % 4, 0, :], ALU.add, ALU.subtract).then_inc(rest_done, 1)

                def low(i):
                    dve.wait_ge(mid_done, i + 1)
                    nc.vector.tensor_tensor(parts[:, i % 4, 2, :], rest[:, i % 4, :], parts[:, i % 4, 1, :],
                                            ALU.subtract).then_inc(lo_done, 1)

                def values(c):
                    dve.wait_ge(v_done, c + 1)
                    for q in range(4):
                        b, t = c // 2, (4 * c + q) % TT
                        out = V[:, b * H:(b + 1) * H, t, 0:DH]
                        src = psv[:, c % 2, q, :].rearrange("p (h d) -> p h d", d=DH)
                        if biased:
                            nc.vector.tensor_tensor(out, src, bv[:].rearrange("p (h d) -> p h d", d=DH), ALU.add)\
                                .then_inc(v_out, 1)
                        else:
                            nc.vector.tensor_copy(out, src).then_inc(v_out, 1)

                for c in range(NCH):
                    rest_of(2 * c)
                    if c:
                        low(2 * c - 1)
                    rest_of(2 * c + 1)
                    if c:
                        values(c - 1)
                    low(2 * c)
                low(2 * NCH - 1)
                values(NCH - 1)
        m.clear_sems()


def project_out(nc, tag, X, F, ident, w, weights_in, normed):
    G = 4
    GT = NT // G
    woT, bo, lw, lb = w[5:]
    with ExitStack() as ctx:
        m = Mem(nc, ctx, tag)
        fT = m.sb("fT", [P, 2, CH])
        y = m.sb("y", [P, NT, D])
        stats = m.sb("stats", [P, NT, 6])
        mv = m.sb("mv", [P, NT, 2])
        ve = m.sb("ve", [P, NT])
        rs = m.sb("rs", [P, NT])
        t1 = m.sb("t1", [P, NT])
        rstd = m.sb("rstd", [P, NT])
        ptr = m.ps("ptr", [P, 2, CH])
        psy = m.ps("psy", [P, 2, 4, D])
        turned, copied, y_done, added, chain, ve_ready, ln_var, rs_ready = (
            m.sem(x) for x in ("turned", "copied", "yd", "added", "chain", "ve", "lnv", "rsr"))
        stats_done, mv_done, centred, weighted, lb_added, x_added = (
            m.sem(x) for x in ("st", "ag", "centred", "weighted", "lbadded", "xadded"))
        loads = ATTENTION_LOADS[normed]
        with nc.Block() as block:

            @block.tensor
            def _(pe):
                pe.wait_ge(weights_in, loads)

                def turn(c):
                    if c >= 2:
                        pe.wait_ge(copied, c - 1)
                    for q in range(4):
                        last = nc.tensor.transpose(ptr[:, c % 2, q * P:(q + 1) * P], F[4 * c + q], ident[:])
                    last.then_inc(turned, 1)

                turn(0)
                for c in range(NCH):
                    if c + 1 < NCH:
                        turn(c + 1)
                    pe.wait_ge(copied, c + 1)
                    if c >= 2:
                        pe.wait_ge(added, c - 1)
                    for q in range(4):
                        last = nc.tensor.matmul(psy[:, c % 2, q, :], fT[:, c % 2, q * P:(q + 1) * P], woT[:],
                                                start=True, stop=True)
                    last.then_inc(y_done, 1)

            @block.scalar
            def _(act):

                def copy(c):
                    act.wait_ge(turned, c + 1)
                    if c >= 2:
                        act.wait_ge(y_done, c - 1)
                    nc.scalar.activation(fT[:, c % 2, :], ptr[:, c % 2, :], ACT.Copy).then_inc(copied, 1)

                for c in range(NCH):
                    copy(c)
                for g in range(G if normed else 0):
                    tiles = slice(g * GT, (g + 1) * GT)
                    act.wait_ge(ve_ready, g + 1)
                    nc.scalar.activation(rs[:, tiles], ve[:, tiles], ACT.Ln).then_inc(ln_var, 1)
                    act.wait_ge(ln_var, g + 1)
                    nc.scalar.activation(rs[:, tiles], rs[:, tiles], ACT.Exp, scale=-0.5).then_inc(rs_ready, 1)

            if normed:

                @block.gpsimd
                def _(pool):
                    pool.wait_ge(weights_in, loads)
                    for g in range(G):
                        tiles = slice(g * GT, (g + 1) * GT)
                        nc.gpsimd.tensor_tensor(X[:, tiles, :], X[:, tiles, :],
                                                lb[:].unsqueeze(1).broadcast_to([P, GT, D]), ALU.add)\
                            .then_inc(lb_added, 1)
                        pool.wait_ge(centred, (g + 1) * GT)
                        nc.gpsimd.tensor_tensor(y[:, tiles, :], y[:, tiles, :],
                                                lw[:].unsqueeze(1).broadcast_to([P, GT, D]), ALU.mult)\
                            .then_inc(weighted, 1)

            @block.vector
            def _(dve):
                dve.wait_ge(weights_in, loads)

                def add(c):
                    dve.wait_ge(y_done, c + 1)
                    tiles = slice(4 * c, 4 * c + 4)
                    if normed:
                        nc.vector.tensor_tensor(y[:, tiles, :], psy[:, c % 2],
                                                bo[:].unsqueeze(1).broadcast_to([P, 4, D]), ALU.add).then_inc(added, 1)
                    else:
                        nc.vector.tensor_tensor(X[:, tiles, :], psy[:, c % 2], X[:, tiles, :], ALU.add)\
                            .then_inc(added, 1)

                def statistics(g):
                    for k in range(g * GT, (g + 1) * GT):
                        dve.wait_ge(added, k // 4 + 1)
                        nc.vector.bn_stats(stats[:, k, :], y[:, k, :]).then_inc(stats_done, 1)
                    for k in range(g * GT, (g + 1) * GT):
                        dve.wait_ge(stats_done, k + 1)
                        nc.vector.bn_aggr(mv[:, k, :], stats[:, k, :]).then_inc(mv_done, 1)
                    tiles = slice(g * GT, (g + 1) * GT)
                    dve.wait_ge(mv_done, (g + 1) * GT)
                    nc.vector.tensor_scalar(ve[:, tiles], mv[:, tiles, 1], LN_EPS, None, ALU.add).then_inc(ve_ready, 1)

                def centre(g):
                    tiles = slice(g * GT, (g + 1) * GT)
                    dve.wait_ge(ve_ready, g + 1)
                    dve.wait_ge(rs_ready, g + 1)
                    link = Chain(dve, chain, 4 * g)
                    link(nc.vector.tensor_tensor(t1[:, tiles], rs[:, tiles], rs[:, tiles], ALU.mult))
                    link(nc.vector.tensor_tensor(t1[:, tiles], t1[:, tiles], ve[:, tiles], ALU.mult))
                    link(nc.vector.tensor_scalar(t1[:, tiles], t1[:, tiles], -0.5, 1.5, ALU.mult, ALU.add))
                    link(nc.vector.tensor_tensor(rstd[:, tiles], rs[:, tiles], t1[:, tiles], ALU.mult))
                    for k in range(g * GT, (g + 1) * GT):
                        nc.vector.tensor_scalar(y[:, k, :], y[:, k, :], mv[:, k, 0:1], rstd[:, k:k + 1],
                                                ALU.subtract, ALU.mult).then_inc(centred, 1)

                def add_normed(g):
                    tiles = slice(g * GT, (g + 1) * GT)
                    dve.wait_ge(lb_added, g + 1)
                    dve.wait_ge(weighted, g + 1)
                    nc.vector.tensor_tensor(X[:, tiles, :], X[:, tiles, :], y[:, tiles, :], ALU.add)\
                        .then_inc(x_added, 1)

                if not normed:
                    for c in range(NCH):
                        add(c)
                    return
                for g in range(G):
                    for c in range(g * GT // 4, (g + 1) * GT // 4):
                        add(c)
                    statistics(g)
                    if g:
                        centre(g - 1)
                    if g > 1:
                        add_normed(g - 2)
                centre(G - 1)
                add_normed(G - 2)
                add_normed(G - 1)
        m.clear_sems()


def load_stacks(eng, Q, K, qd, kd, g, sem):
    for i in range(SPLIT):
        rows = slice(i * SPLIT * DH, (i + 1) * SPLIT * DH)
        eng.dma_start(Q[rows, :], qd[:, g]).then_inc(sem, 16)
        eng.dma_start(K[rows, :], kd[i, g].unsqueeze(0).broadcast_to([SPLIT, DH, T])).then_inc(sem, 16)


STACK_DMAS = 2 * SPLIT


def clear_stacks(eng, Qs, Ks, sem):
    eng.memset(Qs[64:P].bitcast(F32), 0.0).then_inc(sem, 1)
    eng.memset(Ks[64:P].bitcast(F32), 0.0).then_inc(sem, 1)
    eng.wait_ge(sem, 2)
    eng.memset(Ks[ONES_ROW:P], 1.0).then_inc(sem, 1)
    eng.wait_ge(sem, CLEARS)


CLEARS = 3


def attend_causal(nc, tag, V, F, qd, kd, ident, stacks, cleared, masks):
    SLOTS = HEADS // 2
    UNROLL = RING
    LT = 2
    SC = DH ** -0.5
    MAXIMA = [(u, t, half) for u in range(2) for t in range(TT) for half in range(2) if half * CH < (t + 1) * P]
    WEIGHTS = [(u, t, half) for t in range(TT) for u in range(2) for half in range(2) if t * P < (half + 1) * CH]
    NP = len(MAXIMA)
    done = [1 + max(y for y, (_, t, _) in enumerate(WEIGHTS) if t == k) for k in range(TT)]
    with ExitStack() as ctx:
        m = Mem(nc, ctx, tag)
        Q, K = ([stack[:, r, :] for r in range(2 * RING)] for stack in stacks)
        mask_nm = m.sb("mask_nm", [P, P], BF16)
        mask_mn = m.sb("mask_mn", [P, P], BF16)
        identb = m.sb("identb", [P, P], BF16)
        Vh = m.sb("Vh", [P, 2, 2, TT, 32])
        mx = m.sb("mx", [P, 2, 2, 2, TT])
        rem = m.sb("rem", [P, 2, TT])
        neg = m.sb("neg", [P, P], BF16)
        neg3 = neg[:, 0:2 * SPLIT * TT].rearrange("p (u s t) -> p u s t", u=2, s=SPLIT)
        rows = m.sb("rows", [2 * SPLIT * TT, P], BF16)
        pt = m.sb("pt", [P, 2, 2, T])
        osb = m.sb("osb", [P, CH])
        rz = m.sb("rz", [P, 4, 4])
        pm = m.ps("pm", [P, 3, CH])
        pb = m.ps("pb", [P, 3, CH])
        po = m.ps("po", [P, CH])
        ptr = m.ps("ptr", [P, CH])
        loaded, identb_ready, vh_cleared, neg_cleared = (
            m.sem(x) for x in ("loaded", "identb", "vhc", "negc"))
        stack_in = [m.sem(f"stack{r}") for r in range(RING)]
        rows_in = [m.sem(f"rowsin{r}") for r in range(RING)]
        max_mm, max_red, parts_ready, rows_turned, rows_sb, chain = (
            m.sem(x) for x in ("maxmm", "maxred", "parts", "rturned", "rsb", "chain"))
        tau_exp = [m.sem(f"tauexp{r}") for r in range(3)]
        tau_mm, vh_ready, pv_done, o_sb, o_turned, f_done, rz_done = (
            m.sem(x) for x in ("taumm", "vh", "pv", "osb", "oturned", "fd", "rz"))
        PAIR_LOADS = 16 * 2 * STACK_DMAS

        def at(it, j, lag):
            s = UNROLL * it + (j - lag)
            return None if isinstance(s, int) and not 0 <= s < SLOTS else s

        def wait_from(eng, sem, value):
            if not (isinstance(value, int) and value <= 0):
                eng.wait_ge(sem, value)

        def slots(eng, body):
            for j in range(UNROLL):
                body(0, j)
            with eng.Fori(1, SLOTS // UNROLL) as it:
                for j in range(UNROLL):
                    body(it, j)
            for j in range(LT + 1):
                body(SLOTS // UNROLL, j)

        with nc.Block() as block:

            @block.gpsimd
            def _(pool):
                nc.gpsimd.memset(Vh[:], 0.0).then_inc(vh_cleared, 1)
                pool.wait_ge(vh_cleared, 1)

                def body(it, j):
                    s = at(it, j, LT)
                    if s is None:
                        return
                    if not (isinstance(s, int) and s < 2):
                        pool.wait_ge(pv_done, TT * (s - 1))
                    for u in range(2):
                        nc.gpsimd.tensor_copy(Vh[:, (j - LT) % 2, u, :, 0:DH + 1], V[:, 2 * s + u, :, :])\
                            .then_inc(vh_ready, 1)

                slots(pool, body)

            @block.sync
            def _(sp):
                sp.dma_start(mask_nm[:], masks[0]).then_inc(loaded, 16)
                sp.dma_start(mask_mn[:], masks[1]).then_inc(loaded, 16)
                sp.wait_ge(cleared, CLEARS)

                def load(s, r, wait):
                    if wait:
                        sp.wait_ge(tau_mm, NP * (s - RING) + NP)
                    for u in range(2):
                        load_stacks(sp, Q[2 * r + u], K[2 * r + u], qd, kd, 2 * s + u, stack_in[r])

                def send_rows(s, r):
                    sp.wait_ge(rows_sb, s + 1)
                    for u in range(2):
                        n = SPLIT * TT
                        sp.dma_start(Q[2 * r + u][ONES_ROW:ONES_ROW + SPLIT, :].rearrange("s (t n) -> s t n", n=P),
                                     rows[u * n:(u + 1) * n, :])\
                            .then_inc(rows_in[r], 16)

                load(0, 0, False)
                load(1, 1, False)
                for j in range(UNROLL):
                    load(j + 2, (j + 2) % RING, j + 2 >= RING)
                    send_rows(j, j)
                with sp.Fori(1, SLOTS // UNROLL - 1) as it:
                    for j in range(UNROLL):
                        load(UNROLL * it + j + 2, (j + 2) % RING, True)
                        send_rows(UNROLL * it + j, j)
                for j in range(UNROLL):
                    s = SLOTS - UNROLL + j
                    if s + 2 < SLOTS:
                        load(s + 2, (j + 2) % RING, True)
                    send_rows(s, j)

            @block.tensor
            def _(pe):
                pe.wait_ge(loaded, 32)
                pe.wait_ge(identb_ready, 1)

                def scores_max(s, j, y):
                    u, t, half = MAXIMA[y]
                    r, lo, hi = 2 * (j % RING) + u, half * CH, min((half + 1) * CH, (t + 1) * P)
                    diagonal = hi == (t + 1) * P
                    wait_from(pe, max_red, NP * s + y - 2)
                    out = pm[:, y % 3, :]
                    last = nc.tensor.matmul(out[:, 0:hi - lo], Q[r][0:96, t * P:(t + 1) * P], K[r][0:96, lo:hi],
                                            start=True, stop=not diagonal)
                    if diagonal:
                        last = nc.tensor.matmul(out[:, hi - lo - P:hi - lo], identb[:], mask_nm[:],
                                                start=False, stop=True)
                    last.then_inc(max_mm, 1)

                def scores_tau(s, j, y):
                    u, t, half = WEIGHTS[y]
                    r, lo, hi = 2 * (j % RING) + u, max(half * CH, t * P), (half + 1) * CH
                    diagonal = lo == t * P
                    wait_from(pe, tau_exp[y % 3], NP // 3 * s + y // 3)
                    out = pb[:, y % 3, :]
                    last = nc.tensor.matmul(out[:, lo % CH:CH], K[r][:, t * P:(t + 1) * P], Q[r][:, lo:hi],
                                            start=True, stop=not diagonal)
                    if diagonal:
                        last = nc.tensor.matmul(out[:, lo % CH:lo % CH + P], identb[:], mask_mn[:],
                                                start=False, stop=True)
                    last.then_inc(tau_mm, 1)

                def weigh(s, j, t):
                    final = done[t] - 1
                    pe.wait_ge(tau_exp[final % 3], NP // 3 * s + final // 3 + 1)
                    if t == 0:
                        pe.wait_ge(vh_ready, 2 * s + 2)
                        if not (isinstance(s, int) and s < 1):
                            pe.wait_ge(o_sb, s)
                    for u in range(2):
                        for half in range(2):
                            lo, hi = max(half * CH, t * P), (half + 1) * CH
                            if lo >= hi:
                                continue
                            q = 2 * u + half
                            last = nc.tensor.matmul(po[32 * q:32 * q + 32, lo - half * CH:CH],
                                                    Vh[:, j % 2, u, t, :], pt[:, u, t % 2, lo:hi],
                                                    start=(t == 0), stop=(lo + P == hi))
                    last.then_inc(pv_done, 1)

                def turn_rows(s):
                    pe.wait_ge(parts_ready, s + 1)
                    if not (isinstance(s, int) and s < LT + 1):
                        pe.wait_ge(f_done, 2 * (s - LT))
                    nc.tensor.transpose(ptr[:].bitcast(BF16)[:, 0:P], neg[:], identb[:]).then_inc(rows_turned, 1)

                def turn_out(s, rows_before):
                    pe.wait_ge(o_sb, s + 1)
                    if rows_before is not None:
                        pe.wait_ge(rows_sb, rows_before + 1)
                    else:
                        pe.wait_ge(rows_sb, SLOTS)
                        pe.wait_ge(f_done, 2 * s)
                    for c in range(4):
                        last = nc.tensor.transpose(ptr[:, c * P:(c + 1) * P], osb[:, c * P:(c + 1) * P], ident[:])
                    last.then_inc(o_turned, 1)

                def body(it, j):
                    sm, sr, st, so = at(it, j, 0), at(it, j, 1), at(it, j, LT), at(it, j, LT + 1)
                    if sm is not None:
                        pe.wait_ge(stack_in[j % RING], PAIR_LOADS * (it + 1))
                    if st is not None:
                        jt = j - LT
                        pe.wait_ge(rows_in[jt % RING], 32 * (it + jt // RING + 1))
                    for y in range(NP):
                        if sm is not None:
                            scores_max(sm, j, y)
                        if y == 9 and sr is not None:
                            turn_rows(sr)
                        if st is not None:
                            scores_tau(st, j - LT, y)
                            if y - 2 in done:
                                weigh(st, j - LT, done.index(y - 2))
                        if y == 15 and so is not None:
                            turn_out(so, sr)
                    if st is not None:
                        for t in range(TT):
                            if done[t] >= NP - 2:
                                weigh(st, j - LT, t)

                slots(pe, body)

            @block.scalar
            def _(act):

                def exp_tau(s, y):
                    u, t, half = WEIGHTS[y]
                    lo, hi = max(half * CH, t * P), (half + 1) * CH
                    act.wait_ge(tau_mm, NP * s + y + 1)
                    wait_from(act, pv_done, TT * s + t - 1)
                    nc.scalar.activation(pt[:, u, t % 2, lo:hi], pb[:, y % 3, lo % CH:CH], ACT.Exp, scale=SC)\
                        .then_inc(tau_exp[y % 3], 1)

                def copy_out(s):
                    act.wait_ge(pv_done, TT * s + TT)
                    if not (isinstance(s, int) and s < 1):
                        act.wait_ge(o_turned, s)
                    nc.scalar.activation(osb[:], po[:], ACT.Copy).then_inc(o_sb, 1)

                def body(it, j):
                    st, so = at(it, j, LT), at(it, j, LT + 1)
                    for y in range(NP):
                        if st is not None:
                            exp_tau(st, y)
                        if y == 0 and so is not None:
                            copy_out(so)

                slots(act, body)

            @block.vector
            def _(dve):
                nc.vector.tensor_copy(identb[:], ident[:]).then_inc(identb_ready, 1)
                nc.vector.memset(neg[:], 0.0).then_inc(neg_cleared, 1)
                dve.wait_ge(neg_cleared, 1)

                def part(s, j, n):
                    far, top = mx[:, (j - 1) % 2, 1], mx[:, (j - 1) % 2, 0]
                    if n == 0:
                        dve.wait_ge(max_red, NP * s + NP)
                        nc.vector.tensor_tensor(top[:, :, TT // 2:], top[:, :, TT // 2:], far[:, :, TT // 2:], ALU.max)\
                            .then_inc(chain, 1)
                    else:
                        dve.wait_ge(chain, 5 * s + n)
                    if n == 1:
                        wait_from(dve, rows_turned, s)
                        nc.vector.tensor_scalar(neg3[:, :, 0, :], top, -1.0, None, ALU.mult).then_inc(chain, 1)
                    if n == 2:
                        nc.vector.scalar_tensor_tensor(rem[:], top, -1.0, neg3[:, :, 0, :], ALU.mult, ALU.subtract)\
                            .then_inc(chain, 1)
                    if n == 3:
                        nc.vector.tensor_copy(neg3[:, :, 1, :], rem[:]).then_inc(chain, 1)
                    if n == 4:
                        nc.vector.tensor_tensor(rem[:], rem[:], neg3[:, :, 1, :], ALU.subtract).then_inc(chain, 1)
                    if n == 5:
                        nc.vector.tensor_copy(neg3[:, :, 2, :], rem[:]).then_inc(parts_ready, 1)

                def output(s, n):
                    o = ptr[:].rearrange("p (c q k) -> p c q k", c=4, q=4)
                    if n == 0:
                        dve.wait_ge(o_turned, s + 1)
                        if not (isinstance(s, int) and s < 1):
                            dve.wait_ge(f_done, 2 * s)
                        nc.vector.reciprocal(rz[:], o[:, :, :, DH]).then_inc(rz_done, 1)
                    else:
                        u = n - 1
                        dve.wait_ge(rz_done, s + 1)
                        nc.vector.tensor_tensor(
                            F[:, :, 2 * s + u, :].rearrange("p (h c) d -> p c h d", h=2),
                            o[:, :, 2 * u:2 * u + 2, 0:DH],
                            rz[:, :, 2 * u:2 * u + 2].unsqueeze(3).broadcast_to([P, 4, 2, DH]), ALU.mult)\
                            .then_inc(f_done, 1)

                def body(it, j):
                    sm, sr, so = at(it, j, 0), at(it, j, 1), at(it, j, LT + 1)
                    for y in range(NP):
                        if y < 6 and sr is not None:
                            part(sr, j, y)
                        if sm is not None:
                            u, t, half = MAXIMA[y]
                            dve.wait_ge(max_mm, NP * sm + y + 1)
                            nc.vector.tensor_reduce(mx[:, j % 2, half, u, t:t + 1],
                                                    pm[:, y % 3, 0:min(CH, (t + 1) * P - half * CH)],
                                                    AX.X, ALU.max).then_inc(max_red, 1)
                        if y == 11 and sr is not None:
                            dve.wait_ge(rows_turned, sr + 1)
                            if not (isinstance(sr, int) and sr < 1):
                                jr = j - 2
                                dve.wait_ge(rows_in[jr % RING], 32 * (it + jr // RING + 1))
                            nc.vector.tensor_copy(rows[:], ptr[:].bitcast(BF16)[0:2 * SPLIT * TT, 0:P])\
                                .then_inc(rows_sb, 1)
                        if 17 <= y < 20 and so is not None:
                            output(so, y - 17)

                slots(dve, body)
        m.clear_sems()


def attend_both(nc, tag, V, F, par, qd, kd, ident, stacks, cleared):
    SLOTS = HEADS * TT // 2
    PER = TT // 2
    UNROLL = PER * RING
    LS, LT, LE, LP = 4, 6, 6, 7
    SC = DH ** -0.5
    EDGE = 8
    CUT = 25 * T // 32
    with ExitStack() as ctx:
        m = Mem(nc, ctx, tag)
        Q, K = ([stack[:, r, :] for r in range(RING)] for stack in stacks)
        identb = m.sb("identb", [P, P], BF16)
        Vh = m.sb("Vh", [P, 2, TT, 32])
        parh = m.sb("parh", [P, RING, 2])
        mx = m.sb("mx", [P, 2, TT])
        rem = m.sb("rem", [P, TT])
        neg3 = m.sb("neg3", [P, SPLIT, TT], BF16)
        rows = m.sb("rows", [SPLIT * TT, P], BF16)
        pt = [m.sb(f"pt{r}", [P, 2, T]) for r in range(4)]
        sg = [m.sb(f"sg{r}", [P, 2, T]) for r in range(4)]
        shifted = m.sb("shifted", [P, 2, CUT])
        osb = m.sb("osb", [P, CH])
        rz = m.sb("rz", [P, 4, 4])
        fw = m.sb("fw", [P, 4, 4, DH])
        pm = m.ps("pm", [P, T])
        pa = m.ps("pa", [P, T])
        pb = m.ps("pb", [P, T])
        po = m.ps("po", [P, CH])
        ptr = m.ps("ptr", [P, CH])
        identb_ready, vh_cleared = (m.sem(x) for x in ("identb", "vhc"))
        stack_in = [m.sem(f"stack{r}") for r in range(RING)]
        rows_in = [m.sem(f"rowsin{r}") for r in range(RING)]
        max_mm, max_red, parts_ready, rows_turned, rows_sb, chain = (
            m.sem(x) for x in ("maxmm", "maxred", "parts", "rturned", "rsb", "chain"))
        abs_mm, abs_done, shift_done, sq_pool, sq_dve, ln_done, sig_done = (
            m.sem(x) for x in ("absmm", "abs", "shift", "sqp", "sqd", "ln", "sig"))
        tau_mm, tau_exp, vh_ready, par_ready, pv_done, o_sb, o_turned, f_done, rz_done, weighed = (
            m.sem(x) for x in ("taumm", "tauexp", "vh", "par", "pv", "osb", "oturned", "fd", "rz", "weighed"))
        HEAD_LOADS = 16 * STACK_DMAS

        def at(it, j, lag):
            s = UNROLL * it + (j - lag)
            return None if isinstance(s, int) and not 0 <= s < SLOTS else s

        def head(it, j, lag):
            return RING * it + (j - lag) // PER

        def slots(eng, body):
            for j in range(UNROLL):
                body(0, j)
            with eng.Fori(1, SLOTS // UNROLL) as it:
                for j in range(UNROLL):
                    body(it, j)
            for j in range(LP + 2):
                body(SLOTS // UNROLL, j)

        def some(x, least=1):
            return not (isinstance(x, int) and x < least)

        with nc.Block() as block:

            @block.gpsimd
            def _(pool):
                nc.gpsimd.memset(Vh[:], 0.0).then_inc(vh_cleared, 1)
                pool.wait_ge(vh_cleared, 1)

                def body(it, j):
                    s = at(it, j, LS)
                    if s is None:
                        return
                    h = head(it, j, LS)
                    if (j - LS) % PER == 0:
                        if some(h, 2):
                            pool.wait_ge(pv_done, PER * (h - 1))
                        nc.gpsimd.tensor_copy(parh[:, ((j - LS) // PER) % RING, :], par[:, h, :])\
                            .then_inc(par_ready, 1)
                        nc.gpsimd.tensor_copy(Vh[:, ((j - LS) // PER) % 2, :, 0:DH + 1], V[:, h, :, :])\
                            .then_inc(vh_ready, 1)
                    buf = sg[(j - LS) % 4]
                    if some(s):
                        pool.wait_ge(sq_pool, s)
                    pool.wait_ge(abs_done, 2 * s + 2)
                    pool.wait_ge(par_ready, h + 1)
                    b2 = parh[:, ((j - LS) // PER) % RING, 0:1]
                    nc.gpsimd.tensor_tensor(shifted[:, :, 0:EDGE], buf[:, :, 0:EDGE],
                                            b2.unsqueeze(2).broadcast_to([P, 2, EDGE]), ALU.add).then_inc(shift_done, 1)
                    nc.gpsimd.tensor_scalar(shifted[:, :, EDGE:CUT], buf[:, :, EDGE:CUT], b2, 1.0, ALU.add, ALU.mult)\
                        .then_inc(shift_done, 1)
                    pool.wait_ge(shift_done, 2 * s + 2)
                    nc.gpsimd.tensor_tensor(buf[:, :, 0:CUT], buf[:, :, 0:CUT], shifted[:], ALU.mult)\
                        .then_inc(sq_pool, 1)

                slots(pool, body)

            @block.sync
            def _(sp):
                sp.wait_ge(cleared, CLEARS)

                def load(h, r, wait):
                    if wait:
                        sp.wait_ge(tau_mm, TT * (h - RING) + TT)
                    load_stacks(sp, Q[r], K[r], qd, kd, h, stack_in[r])

                def send_rows(h, r):
                    sp.wait_ge(rows_sb, h + 1)
                    sp.dma_start(Q[r][ONES_ROW:ONES_ROW + SPLIT, :].rearrange("s (t n) -> s t n", n=P),
                                 rows[:]).then_inc(rows_in[r], 16)

                load(0, 0, False)
                load(1, 1, False)
                for j in range(RING):
                    load(j + 2, (j + 2) % RING, j + 2 >= RING)
                    send_rows(j, j)
                with sp.Fori(1, HEADS // RING - 1) as it:
                    for j in range(RING):
                        load(RING * it + j + 2, (j + 2) % RING, True)
                        send_rows(RING * it + j, j)
                for j in range(RING):
                    h = HEADS - RING + j
                    if h + 2 < HEADS:
                        load(h + 2, (j + 2) % RING, True)
                    send_rows(h, j)

            @block.tensor
            def _(pe):
                pe.wait_ge(identb_ready, 1)

                def scores(out, lhsT, rhs, t, rows_, sem):
                    for lo in range(0, T, CH):
                        last = nc.tensor.matmul(out[:, lo:lo + CH], lhsT[0:rows_, t * P:(t + 1) * P],
                                                rhs[0:rows_, lo:lo + CH], start=True, stop=True)
                    last.then_inc(sem, 1)

                def weigh(it, j, s, i):
                    h, k, r = head(it, j, LP), (j - LP) % PER, (j - LP) % 4
                    t = 2 * k + i
                    if i == 0:
                        pe.wait_ge(tau_exp, 2 * s + 2)
                        pe.wait_ge(sig_done, s + 1)
                    if t == 0:
                        pe.wait_ge(vh_ready, h + 1)
                        if some(h):
                            pe.wait_ge(o_sb, h)
                    for q, (wts, half) in enumerate(((pt[r], 0), (pt[r], 1), (sg[r], 0), (sg[r], 1))):
                        last = nc.tensor.matmul(po[32 * q:32 * q + 32, :], Vh[:, ((j - LP) // PER) % 2, t, :],
                                                wts[:, i, half * CH:(half + 1) * CH],
                                                start=(t == 0), stop=(t == TT - 1))
                    if i:
                        last.then_inc(pv_done, 1)

                def body(it, j):
                    sm, ss, st, sp_ = at(it, j, 0), at(it, j, LS), at(it, j, LT), at(it, j, LP)
                    rm, rs, rt = (((j - lag) // PER) % RING for lag in (0, LS, LT))
                    if sm is not None and j % PER == 0:
                        pe.wait_ge(stack_in[rm], HEAD_LOADS * (it + 1))
                    if st is not None and (j - LT) % PER == 0:
                        pe.wait_ge(rows_in[rt], 16 * (it + (j - LT) // PER // RING + 1))
                    for i in range(2):
                        if sm is not None:
                            if some(2 * sm + i):
                                pe.wait_ge(max_red, 2 * sm + i)
                            scores(pm, Q[rm], K[rm], 2 * (j % PER) + i, 96, max_mm)
                        if st is not None:
                            if some(2 * st + i):
                                pe.wait_ge(tau_exp, 2 * st + i)
                            scores(pb, K[rt], Q[rt], 2 * ((j - LT) % PER) + i, P, tau_mm)
                        if ss is not None:
                            if some(2 * ss + i):
                                pe.wait_ge(abs_done, 2 * ss + i)
                            scores(pa, K[rs], Q[rs], 2 * ((j - LS) % PER) + i, 96, abs_mm)
                        if i and sp_ is not None:
                            weigh(it, j, sp_, 0)
                        if i and sp_ is not None:
                            weigh(it, j, sp_, 1)
                    if j % PER == 0 and at(it, j, 1) is not None:
                        h = head(it, j, 1)
                        pe.wait_ge(parts_ready, h + 1)
                        if some(h, 2):
                            pe.wait_ge(f_done, h - 1)
                        nc.tensor.transpose(ptr[:].bitcast(BF16)[0:SPLIT * TT, 0:P],
                                            neg3[:].rearrange("p s t -> p (s t)"), identb[:])\
                            .then_inc(rows_turned, 1)
                    if (j - LP - 1) % PER == PER - 1 and at(it, j, LP + 1) is not None:
                        h = head(it, j, LP + 1)
                        pe.wait_ge(o_sb, h + 1)
                        if isinstance(h, int) and h + 3 > HEADS:
                            pe.wait_ge(rows_sb, HEADS)
                            pe.wait_ge(f_done, h)
                        else:
                            pe.wait_ge(rows_sb, h + 2)
                        for c in range(4):
                            last = nc.tensor.transpose(ptr[:, c * P:(c + 1) * P], osb[:, c * P:(c + 1) * P],
                                                       ident[:])
                        last.then_inc(o_turned, 1)

                slots(pe, body)

            @block.scalar
            def _(act):
                nc.scalar.preload_act_table_set("natural_log_exp_and_others")

                def body(it, j):
                    st, se, so = at(it, j, LT), at(it, j, LE), at(it, j, LP + 1)
                    for i in range(2):
                        if st is not None:
                            act.wait_ge(tau_mm, 2 * st + i + 1)
                            if i == 0 and some(st, 4):
                                act.wait_ge(pv_done, st - 3)
                            nc.scalar.activation(pt[(j - LT) % 4][:, i, :], pb[:], ACT.Exp, scale=SC)\
                                .then_inc(tau_exp, 1)
                        if i == 0 and so is not None and (j - LP - 1) % PER == PER - 1:
                            h = head(it, j, LP + 1)
                            act.wait_ge(pv_done, PER * h + PER)
                            if some(h):
                                act.wait_ge(o_turned, h)
                            nc.scalar.activation(osb[:], po[:], ACT.Copy).then_inc(o_sb, 1)
                        if se is not None:
                            buf = sg[(j - LE) % 4]
                            if i == 0:
                                h = head(it, j, LE)
                                act.wait_ge(sq_pool, se + 1)
                                act.wait_ge(sq_dve, se + 1)
                                act.wait_ge(par_ready, h + 1)
                                nc.scalar.activation(buf[:], buf[:], ACT.Ln,
                                                     bias=parh[:, ((j - LE) // PER) % RING, 1:2]).then_inc(ln_done, 1)
                            else:
                                act.wait_ge(ln_done, se + 1)
                                nc.scalar.activation(buf[:], buf[:], ACT.Exp, scale=-1.0).then_inc(sig_done, 1)

                slots(act, body)

            @block.vector
            def _(dve):
                nc.vector.tensor_copy(identb[:], ident[:]).then_inc(identb_ready, 1)

                def part(it, j, n):
                    if j % PER or at(it, j, 1) is None:
                        return
                    h, top = head(it, j, 1), mx[:, ((j - 1) // PER) % 2, :]
                    if n == 0:
                        dve.wait_ge(max_red, TT * h + TT)
                        if some(h):
                            dve.wait_ge(rows_turned, h)
                        nc.vector.tensor_scalar(neg3[:, 0, :], top, -1.0, None, ALU.mult).then_inc(chain, 1)
                    else:
                        dve.wait_ge(chain, 4 * h + n)
                    if n == 1:
                        nc.vector.scalar_tensor_tensor(rem[:], top, -1.0, neg3[:, 0, :], ALU.mult, ALU.subtract)\
                            .then_inc(chain, 1)
                    if n == 2:
                        nc.vector.tensor_copy(neg3[:, 1, :], rem[:]).then_inc(chain, 1)
                    if n == 3:
                        nc.vector.tensor_tensor(rem[:], rem[:], neg3[:, 1, :], ALU.subtract).then_inc(chain, 1)
                    if n == 4:
                        nc.vector.tensor_copy(neg3[:, 2, :], rem[:]).then_inc(parts_ready, 1)

                def output(it, j, n):
                    if (j - LP - 2) % PER != PER - 1 or at(it, j, LP + 2) is None:
                        return
                    h = head(it, j, LP + 2)
                    o = ptr[:].rearrange("p (c q k) -> p c q k", c=4, q=4)
                    if n == 0:
                        dve.wait_ge(o_turned, h + 1)
                        if some(h):
                            dve.wait_ge(weighed, h)
                        nc.vector.reciprocal(rz[:], o[:, :, :, DH]).then_inc(rz_done, 1)
                    if n == 1:
                        dve.wait_ge(rz_done, h + 1)
                        if some(h):
                            dve.wait_ge(f_done, h)
                        nc.vector.tensor_tensor(fw[:], o[:, :, :, 0:DH], rz[:].unsqueeze(3).broadcast_to([P, 4, 4, DH]),
                                                ALU.mult).then_inc(weighed, 1)
                    if n == 2:
                        dve.wait_ge(weighed, h + 1)
                        nc.vector.tensor_tensor(F[:, :, h, :].rearrange("p (s c) d -> p s c d", s=2),
                                                fw[:, :, 0:2, :].rearrange("p c s d -> p s c d"),
                                                fw[:, :, 2:4, :].rearrange("p c s d -> p s c d"), ALU.add)\
                            .then_inc(f_done, 1)

                def body(it, j):
                    sm, ss = at(it, j, 0), at(it, j, LS)
                    part(it, j, 0)
                    for i in range(2):
                        if sm is not None:
                            t = 2 * (j % PER) + i
                            dve.wait_ge(max_mm, 2 * sm + i + 1)
                            nc.vector.tensor_reduce(mx[:, (j // PER) % 2, t:t + 1], pm[:], AX.X, ALU.max)\
                                .then_inc(max_red, 1)
                        part(it, j, 2 * i + 1)
                        output(it, j, 2 * i)
                        if ss is not None:
                            dve.wait_ge(abs_mm, 2 * ss + i + 1)
                            if i == 0 and some(ss, 4):
                                dve.wait_ge(pv_done, ss - 3)
                            nc.vector.tensor_scalar(sg[(j - LS) % 4][:, i, :].bitcast(I32), pa[:].bitcast(I32),
                                                    SIGN_OFF, None, ALU.bitwise_and).then_inc(abs_done, 1)
                        part(it, j, 2 * i + 2)
                        output(it, j, 2 * i + 1)
                        if i == 0 and j % PER == 1 and at(it, j, 2) is not None:
                            h, r = head(it, j, 2), ((j - 2) // PER - 1) % RING
                            dve.wait_ge(rows_turned, h + 1)
                            if some(h):
                                dve.wait_ge(rows_in[r], 16 * (it + ((j - 2) // PER - 1) // RING + 1))
                            nc.vector.tensor_copy(rows[:], ptr[:].bitcast(BF16)[0:SPLIT * TT, 0:P])\
                                .then_inc(rows_sb, 1)
                    if ss is not None:
                        h, buf = head(it, j, LS), sg[(j - LS) % 4]
                        dve.wait_ge(abs_done, 2 * ss + 2)
                        dve.wait_ge(par_ready, h + 1)
                        nc.vector.scalar_tensor_tensor(buf[:, :, CUT:T], buf[:, :, CUT:T],
                                                       parh[:, ((j - LS) // PER) % RING, 0:1], buf[:, :, CUT:T],
                                                       ALU.add, ALU.mult).then_inc(sq_dve, 1)

                slots(dve, body)
        m.clear_sems()


def load_sharpness(nc, tag, par, beta, t):
    with ExitStack() as ctx:
        m = Mem(nc, ctx, tag)
        bt = m.sb("bt", [P, 2, H])
        one = m.sb("one", [P, 2, H])
        loaded, chain = m.sem("loaded"), m.sem("chain")
        with nc.Block() as block:

            @block.sync
            def _(sp):
                sp.dma_start(bt[:, 0, :], beta.unsqueeze(0).broadcast_to([P, H])).then_inc(loaded, 16)
                sp.dma_start(bt[:, 1, :], t.unsqueeze(0).broadcast_to([P, H])).then_inc(loaded, 16)

            @block.vector
            def _(dve):
                dve.wait_ge(loaded, 32)
                link = Chain(dve, chain)
                link(nc.vector.tensor_scalar(bt[:, 0, :], bt[:, 0, :], DH ** 0.5, None, ALU.mult))
                link(nc.vector.tensor_tensor(bt[:, 1, :], bt[:, 0, :], bt[:, 1, :], ALU.mult))
                link(nc.vector.tensor_tensor(one[:], bt[:], bt[:], ALU.mult))
                for b in range(B):
                    link(nc.vector.tensor_scalar(par[:, b * H:(b + 1) * H, 0], bt[:, 0, :], 2.0, None, ALU.mult))
                    link(nc.vector.tensor_tensor(par[:, b * H:(b + 1) * H, 1], one[:, 0, :], one[:, 1, :], ALU.add))
        m.clear_sems()


def program(nc, x, out, w, stop=99):
    x_v = x.rearrange("b (t p) d -> p (b t) d", p=P)
    out_v = out.rearrange("b (t p) d -> p (b t) d", p=P)
    qd = nc.dram_tensor("q_parts", (SPLIT, HEADS, DH, T), BF16, kind="Internal").ap()
    kd = nc.dram_tensor("k_parts", (SPLIT, HEADS, DH, T), BF16, kind="Internal").ap()
    with ExitStack() as ctx:
        m = Mem(nc, ctx, "all")
        X = m.sb("X", [P, NT, D])
        XNT = m.sb("XNT", [P, TOK])
        V = m.sb("V", [P, HEADS, TT, DH + 1])
        ident = m.sb("ident", [P, P])
        rank0 = m.sb("rank0", [P, E0])
        rank1 = m.sb("rank1", [P, E1])
        par = m.sb("par", [P, HEADS, 2])
        stacks = [m.sb(n, [P, 2 * RING, T], BF16) for n in ("Q", "K")]
        loaded, cleared = m.sem("loaded"), m.sem("cleared")
        layer = {n: {k[3:]: v for k, v in w.items() if k.startswith(n)} for n in ("f0_", "a0_", "a1_", "f1_")}
        f0_parts = [m.sb(n, [P, E0, F0] if n[:2] == "w1" else [P, E0 * FT0, D], F16)
                    for n in ("w1h", "w1l", "w2h", "w2l")]
        f1_parts = [m.sb(n, [P, KT1, D] if n[:2] == "wd" else [P, E1 * M1], F16)
                    for n in ("wgh", "wgl", "wuh", "wul", "wdh", "wdl")]
        raw = [([P, E0, F0], layer["f0_"]["We1"].rearrange("e h f -> h e f"), *f0_parts[0:2]),
               ([P, E0 * FT0, D], layer["f0_"]["We2"].rearrange("e (j p) d -> p (e j) d", p=P), *f0_parts[2:4]),
               ([P, E1 * M1], layer["f1_"]["w_gP"], *f1_parts[0:2]),
               ([P, E1 * M1], layer["f1_"]["w_uP"], *f1_parts[2:4]),
               ([P, KT1, D], layer["f1_"]["w_dP"].rearrange("(k p) d -> p k d", p=P), *f1_parts[4:6])]
        f0_in, a0_in, f1_in, a1_in = (m.sem(n) for n in ("f0_in", "a0_in", "f1_in", "a1_in"))
        f0, load_f0 = load_ffn0(m, layer["f0_"], f0_in)
        a0, load_a0 = load_attention(m, layer["a0_"], a0_in, False)
        f1, load_f1 = load_ffn1(m, layer["f1_"], f1_in)
        a1, load_a1 = load_attention(m, layer["a1_"], a1_in, True)
        with nc.Block() as block:

            @block.sync
            def _(sp):
                sp.dma_start(X[:], x_v).then_inc(loaded, 16)
                sp.dma_start(ident[:], w["ident"]).then_inc(loaded, 16)
                sp.dma_start(rank0[:], w["rank"][:, E1 - E0:]).then_inc(loaded, 16)
                sp.dma_start(rank1[:], w["rank"]).then_inc(loaded, 16)
                for load in (load_f0, load_a0, load_f1, load_a1):
                    load(sp)
                sp.wait_ge(loaded, 64)

        F = XNT[:].rearrange("p (t h d) -> p t h d", h=HEADS, t=TT)
        tiles = [XNT[:, (k % TT) * HEADS * DH + (k // TT) * D:][:, 0:D] for k in range(NT)]

        def ffn_first(tag):
            with ExitStack() as inner:
                split = [inner.enter_context(nc.sbuf_tensor(f"{tag}_{n}", [P, TOK], F16)) for n in ("XH", "XL")]
                score = inner.enter_context(nc.sbuf_tensor(f"{tag}_score", [P, NT, E0], F32))
                ln_transposed(nc, f"n{tag}", X, XNT, ident, split=split, router=(f0[2], f0_in, FFN0_LOADS, score))
                ffn0(nc, f"f{tag}", X, split, score, rank0, f0, f0_parts, f0_in)

        def ffn_second(tag, out=None):
            with ExitStack() as inner:
                split = [inner.enter_context(nc.sbuf_tensor(f"{tag}_{n}", [P, TOK], F16)) for n in ("XH", "XL")]
                score = inner.enter_context(nc.sbuf_tensor(f"{tag}_score", [P, NT, E1], F32))
                ln_transposed(nc, f"n{tag}", X, XNT, ident, split=split, router=(f1[0], f1_in, FFN1_LOADS, score))
                spare = (XNT, V[:].rearrange("p h t d -> p (h t d)"))
                ffn1(nc, f"f{tag}", X, spare, split, score, ident, rank1, f1, f1_parts, f1_in, out)

        steps = [
            lambda: split_weights(nc, "sw", raw, stacks, cleared),
            lambda: ffn_first("1"),
            lambda: ln_transposed(nc, "n2", X, XNT, ident),
            lambda: project(nc, "p2", XNT, V, qd, kd, a0, a0_in, False, 1.0),
            lambda: attend_causal(nc, "a2", V, F, qd, kd, ident, stacks, cleared,
                                  (w["mask_nm"], w["mask_mn"])),
            lambda: project_out(nc, "o2", X, tiles, ident, a0, a0_in, False),
            lambda: ffn_first("3"),
            lambda: ffn_second("4"),
            lambda: ln_transposed(nc, "n5", X, XNT, ident, add_to_x=True),
            lambda: load_sharpness(nc, "s5", par, layer["a1_"]["beta"], layer["a1_"]["t"]),
            lambda: project(nc, "p5", XNT, V, qd, kd, a1, a1_in, True, 2.0),
            lambda: attend_both(nc, "a5", V, F, par, qd, kd, ident, stacks, cleared),
            lambda: project_out(nc, "o5", X, tiles, ident, a1, a1_in, True),
            lambda: ffn_second("6", out_v),
        ]
        for step in (steps[:stop] if isinstance(stop, int) else [steps[i] for i in stop]):
            step()


def kernel(**inputs):
    import numpy as _np
    import ml_dtypes as _ml
    import concourse.bacc as _bacc
    from concourse import mybir as _mybir
    from concourse.bass_utils import run_bass_kernel_spmd as _run

    i = {k: _np.asarray(v) for k, v in inputs.items()}
    c = _np.ascontiguousarray
    arrays = {"x": c(i["L0_attn_x"])}
    for n in ("Wr", "br", "We1", "We2", "be2"):
        arrays["f0_" + n] = c(i["L0_ffn_" + n])
    arrays["f0_be1T"] = c(i["L0_ffn_be1"].reshape(E0 * FT0, P).T)
    for n in ("Wq", "Wk", "Wv", "Wo"):
        arrays[f"a0_{n}T"] = c(i["L0_attn_" + n].T)
        arrays[f"a1_{n}T"] = c(i["L1_attn_" + n].T)
    for n in ("bq", "bk", "bv", "bo", "beta", "t", "ln_w", "ln_b"):
        arrays["a1_" + n] = c(i["L1_attn_" + n])
    arrays["f1_w_gate"] = c(i["L1_ffn_w_gate"])
    arrays["f1_w_gP"] = c(i["L1_ffn_w_g"].transpose(1, 0, 2).reshape(D, E1 * M1))
    arrays["f1_w_uP"] = c(i["L1_ffn_w_u"].transpose(1, 0, 2).reshape(D, E1 * M1))
    arrays["f1_w_dP"] = c(i["L1_ffn_w_d"].reshape(E1 * M1, D))
    sel = _np.zeros((96, E1 * M1), _np.float32)
    for part in range(SPLIT):
        sel[32 * part + _np.arange(E1 * M1) // M1, _np.arange(E1 * M1)] = 1.0
    arrays["f1_sel"] = sel.astype(_ml.bfloat16)
    arrays["ident"] = _np.eye(P, dtype=_np.float32)
    arrays["rank"] = _np.tile(_np.arange(E1, 0, -1, dtype=_np.float32), (P, 1))
    above = _np.triu(_np.full((P, P), -1e30, _np.float32), 1)
    arrays["mask_nm"] = above.astype(_ml.bfloat16)
    arrays["mask_mn"] = c(above.T).astype(_ml.bfloat16)

    nc = _bacc.Bacc("TRN2", target_bir_lowering=False, num_devices=1)
    named, aps = {}, {}
    for n, a in arrays.items():
        named[f"in_{n}_dram"] = a
        aps[n] = nc.dram_tensor(f"in_{n}_dram", a.shape, _mybir.dt.from_np(a.dtype), kind="ExternalInput").ap()
    out = nc.dram_tensor("out_0_dram", (B, T, D), _mybir.dt.float32, kind="ExternalOutput").ap()
    program(nc, aps.pop("x"), out, aps)
    r = _run(nc, [named], core_ids=[0])
    return r.results[0]["out_0_dram"]
```
